# Optimizing a Trainium2 kernel written in Bass

```python
import numpy as np
import jax
import jax.numpy as jnp

def _softmax(x, axis=-1):
    return jax.nn.softmax(x, axis=axis)

def _gelu(x):
    return jax.nn.gelu(x, approximate=True)

def _silu(x):
    return jax.nn.silu(x)

def _sigmoid(x):
    return jax.nn.sigmoid(x)

def _layernorm(x, axis=-1, eps=1e-05):
    m = jnp.mean(x, axis=axis, keepdims=True)
    v = jnp.var(x, axis=axis, keepdims=True)
    return (x - m) / jnp.sqrt(v + eps)

def _scatter_add(tgt, idx, src, axis=0):
    return tgt.at[idx].add(src)

def _segment_sum(src, seg, n):
    return jax.ops.segment_sum(src, seg, n)
kernel_name = 'mk_adaln_d1_jaxref_r4_bb4f68'

def setup_inputs(seed: int=0):
    np.random.seed(seed)
    _w = jnp.asarray

    def _L0_attn_setup():
        import jax, jax.numpy as jnp
        import numpy as np
        B, N, D = (2, 2048, 256)
        H, Dh = (16, 64)
        P = H * Dh
        EPS = 1e-06
        DECAY_BIAS_SHIFT = 2.0

        def _elu_plus_one(x):
            return jax.nn.elu(x) + 1.0

        def _ssd_scan(q, k, v, a, eps):
            qT = jnp.moveaxis(q, 2, 0)
            kT = jnp.moveaxis(k, 2, 0)
            vT = jnp.moveaxis(v, 2, 0)
            aT = jnp.moveaxis(a, 2, 0)
            Bb, Hh, _, Dk = q.shape
            Dv = v.shape[-1]
            S0 = jnp.zeros((Bb, Hh, Dk, Dv), q.dtype)
            z0 = jnp.zeros((Bb, Hh, Dk), q.dtype)

            def step(carry, inp):
                S, z = carry
                qt, kt, vt, at = inp
                S = at[..., None, None] * S + kt[..., :, None] * vt[..., None, :]
                z = at[..., None] * z + kt
                num = jnp.einsum('bhk,bhkv->bhv', qt, S)
                den = jnp.einsum('bhk,bhk->bh', qt, z) + eps
                return ((S, z), num / den[..., None])
            _, outT = jax.lax.scan(step, (S0, z0), (qT, kT, vT, aT))
            return jnp.moveaxis(outT, 0, 2)
        key = jax.random.key(seed)
        ks = jax.random.split(key, 7)
        s_in = 1.0 / np.sqrt(D)
        s_out = 1.0 / np.sqrt(P)
        return {'x': jax.random.normal(ks[0], (B, N, D), jnp.float32), 'Wq': jax.random.normal(ks[1], (D, P), jnp.float32) * s_in, 'Wk': jax.random.normal(ks[2], (D, P), jnp.float32) * s_in, 'Wv': jax.random.normal(ks[3], (D, P), jnp.float32) * s_in, 'Wo': jax.random.normal(ks[4], (P, D), jnp.float32) * s_out, 'Wa': jax.random.normal(ks[5], (D, H), jnp.float32) * s_in, 'ba': jnp.zeros((H,), jnp.float32)}
    _L0_attn_in = _L0_attn_setup()

    def _L0_ffn_setup():
        import jax, jax.numpy as jnp
        import numpy as np
        B, S, D, E, K = (4, 512, 256, 8, 2)
        EPS, W_THRES, TEMP = (0.0001, 0.1, 1.0)
        key = jax.random.key(seed)
        k1, k2, k3, k4, k5 = jax.random.split(key, 5)
        x = jax.random.normal(k1, (B, S, D), dtype=jnp.float32)
        gate_W = jax.random.normal(k2, (D, E), dtype=jnp.float32) * 0.02
        gate_b = jnp.zeros((E,), dtype=jnp.float32)
        expert_W = jax.random.normal(k3, (E, D, D), dtype=jnp.float32) * 0.02
        expert_b = jnp.zeros((E, D), dtype=jnp.float32)
        return {'x': x, 'gate_W': gate_W, 'gate_b': gate_b, 'expert_W': expert_W, 'expert_b': expert_b}
    _L0_ffn_in = _L0_ffn_setup()
    _L0_c = _w((lambda *s: np.random.randn(*s).astype(np.float32) * 0.05)(8, 256))
    _L0_wmod = _w((lambda *s: np.random.randn(*s).astype(np.float32) * 0.05)(256, 6 * 256) * 256 ** (-0.5))
    _d = {'L0_attn_x': _L0_attn_in['x'], 'L0_attn_Wq': _L0_attn_in['Wq'], 'L0_attn_Wk': _L0_attn_in['Wk'], 'L0_attn_Wv': _L0_attn_in['Wv'], 'L0_attn_Wo': _L0_attn_in['Wo'], 'L0_attn_Wa': _L0_attn_in['Wa'], 'L0_attn_ba': _L0_attn_in['ba'], 'L0_ffn_gate_W': _L0_ffn_in['gate_W'], 'L0_ffn_gate_b': _L0_ffn_in['gate_b'], 'L0_ffn_expert_W': _L0_ffn_in['expert_W'], 'L0_ffn_expert_b': _L0_ffn_in['expert_b'], 'L0_c': _L0_c, 'L0_wmod': _L0_wmod}
    _x0 = _d['L0_attn_x']
    _d['L0_attn_x'] = jax.random.normal(jax.random.fold_in(jax.random.key(seed), 1), (8, 2048, 256), dtype=_x0.dtype)
    del _x0
    return _d

def reference(L0_attn_x, L0_attn_Wq, L0_attn_Wk, L0_attn_Wv, L0_attn_Wo, L0_attn_Wa, L0_attn_ba, L0_ffn_gate_W, L0_ffn_gate_b, L0_ffn_expert_W, L0_ffn_expert_b, L0_c, L0_wmod):

    def _L0_attn_ref(x, Wq, Wk, Wv, Wo, Wa, ba):
        import jax, jax.numpy as jnp
        import numpy as np
        B, N, D = (2, 2048, 256)
        H, Dh = (16, 64)
        P = H * Dh
        EPS = 1e-06
        DECAY_BIAS_SHIFT = 2.0

        def _elu_plus_one(x):
            return jax.nn.elu(x) + 1.0

        def _ssd_scan(q, k, v, a, eps):
            qT = jnp.moveaxis(q, 2, 0)
            kT = jnp.moveaxis(k, 2, 0)
            vT = jnp.moveaxis(v, 2, 0)
            aT = jnp.moveaxis(a, 2, 0)
            Bb, Hh, _, Dk = q.shape
            Dv = v.shape[-1]
            S0 = jnp.zeros((Bb, Hh, Dk, Dv), q.dtype)
            z0 = jnp.zeros((Bb, Hh, Dk), q.dtype)

            def step(carry, inp):
                S, z = carry
                qt, kt, vt, at = inp
                S = at[..., None, None] * S + kt[..., :, None] * vt[..., None, :]
                z = at[..., None] * z + kt
                num = jnp.einsum('bhk,bhkv->bhv', qt, S)
                den = jnp.einsum('bhk,bhk->bh', qt, z) + eps
                return ((S, z), num / den[..., None])
            _, outT = jax.lax.scan(step, (S0, z0), (qT, kT, vT, aT))
            return jnp.moveaxis(outT, 0, 2)
        b, n, _ = x.shape
        q = (x @ Wq).reshape(b, n, H, Dh).transpose(0, 2, 1, 3)
        k = (x @ Wk).reshape(b, n, H, Dh).transpose(0, 2, 1, 3)
        v = (x @ Wv).reshape(b, n, H, Dh).transpose(0, 2, 1, 3)
        q = _elu_plus_one(q)
        k = _elu_plus_one(k)
        a = jax.nn.sigmoid(x @ Wa + ba + DECAY_BIAS_SHIFT)
        a = a.transpose(0, 2, 1)
        out = _ssd_scan(q, k, v, a, EPS)
        out = out.transpose(0, 2, 1, 3).reshape(b, n, P)
        return out @ Wo

    def _L0_ffn_ref(x, gate_W, gate_b, expert_W, expert_b):
        import jax, jax.numpy as jnp
        import numpy as np
        B, S, D, E, K = (4, 512, 256, 8, 2)
        EPS, W_THRES, TEMP = (0.0001, 0.1, 1.0)
        scores = jnp.maximum((x @ gate_W + gate_b) / TEMP, EPS)
        p = jax.nn.softmax(scores, axis=-1)
        _, topk_idx = jax.lax.top_k(p, K)
        topk_mask = jax.nn.one_hot(topk_idx, E, dtype=p.dtype).sum(-2) > 0
        w = jnp.maximum(p, W_THRES)
        w_gather = jnp.take_along_axis(w, topk_idx, axis=-1)
        total = jax.lax.stop_gradient(w_gather.sum(-1, keepdims=True))
        w = w / total
        comb = jnp.where(topk_mask, w, jnp.zeros_like(w))
        y = jnp.einsum('bsd,edf->bsef', x, expert_W) + expert_b
        out = jnp.einsum('bsef,bse->bsf', y, comb) / K
        return out
    x = L0_attn_x
    mod = (_silu(L0_c) @ L0_wmod).reshape(L0_c.shape[0], 6, 1, -1)
    sa, ca, ga, sb, cb, gb = (mod[:, 0], mod[:, 1], mod[:, 2], mod[:, 3], mod[:, 4], mod[:, 5])
    ga = (2 * (ga >= 0) - 1) * jnp.maximum(jnp.abs(ga), 0.25)
    gb = (2 * (gb >= 0) - 1) * jnp.maximum(jnp.abs(gb), 0.25)
    h = _layernorm(x, axis=-1) * (1 + ca) + sa
    x = x + ga * _L0_attn_ref(h, L0_attn_Wq, L0_attn_Wk, L0_attn_Wv, L0_attn_Wo, L0_attn_Wa, L0_attn_ba)
    h = _layernorm(x, axis=-1) * (1 + cb) + sb
    x = x + gb * _L0_ffn_ref(h, L0_ffn_gate_W, L0_ffn_gate_b, L0_ffn_expert_W, L0_ffn_expert_b)
    return x

_drawn_inputs = setup_inputs


def setup_inputs(seed=0):
    import zlib

    import numpy as np

    out = dict(_drawn_inputs(seed))
    spreads = {'L0_attn_ba': (0.0, 2.0), 'L0_ffn_gate_b': (0.0, 0.453), 'L0_ffn_expert_b': (0.0, 0.8)}
    factors = {'L0_attn_Wq': 21.962, 'L0_attn_Wk': 7.636, 'L0_attn_Wa': 3.105}
    for name, (base, spread) in spreads.items():
        noise = np.random.default_rng([zlib.crc32(name.encode()), seed]).standard_normal(out[name].shape)
        drawn = base * np.exp(spread * noise) if base else spread * noise
        out[name] = jnp.asarray(drawn.astype(out[name].dtype))
    for name, factor in factors.items():
        out[name] = (out[name] * factor).astype(out[name].dtype)
    return out
```

```python
import concourse.bass as bass
from concourse import mybir
from contextlib import ExitStack

F32 = mybir.dt.float32
F32R = mybir.dt.float32r
ALU = mybir.AluOpType
ACT = mybir.ActivationFunctionType
AX_X = mybir.AxisListType.X

BATCH, SEQ, D = 8, 2048, 256
HEADS, DH = 16, 64
P_DIM = HEADS * DH
EXPERTS = 8
LN_EPS = 1e-5
DEN_EPS = 1e-6
DECAY_BIAS_SHIFT = 2.0
SCORE_EPS, W_THRES = 1e-4, 0.1
TOP_K = 2
GATE_FLOOR = 0.25
BIG = 3.0e38

CH = 128
NCH = 4
GT = CH * NCH
NG = BATCH * SEQ // GT
GPB = SEQ // GT
KT = D // 128
PAIRS = HEADS // 2
PT = P_DIM // 128
VW = DH + 1
LO = 32
ROWS = LO + HEADS


def after(eng, sem, count):
    if isinstance(count, int) and count <= 0:
        return
    eng.wait_ge(sem, count)


def exists(T):
    return not isinstance(T, int) or 0 <= T < NG


def unit(T, u, ahead):
    Tn, p = (T, u + ahead) if u + ahead < PAIRS else (T + 1, u + ahead - PAIRS)
    return Tn, p, Tn * PAIRS + p


def batch_row(T):
    b = T // GPB if isinstance(T, int) else T >> (GPB.bit_length() - 1)
    return b if isinstance(b, int) else b.with_bounds(min_val=0, max_val=BATCH - 1)


def attention_steps(eng, step):
    for T in (-1, 0, 1):
        for u in range(PAIRS):
            step(T, T % 2, u)
    with eng.Fori(1, NG // 2 - 1) as i:
        for s in range(2):
            for u in range(PAIRS):
                step(i * 2 + s, s, u)
    for T in (NG - 2, NG - 1):
        for u in range(PAIRS):
            step(T, T % 2, u)
    step(NG, 0, 0)


def expert_groups(eng, group):
    group(-1, GPB - 1)
    for T in range(GPB):
        group(T, T)
    with eng.Fori(1, BATCH - 1) as b:
        for s in range(GPB):
            group(b * GPB + s, s)
    for T in range(NG - GPB, NG):
        group(T, T % GPB)


def adaln_block(nc, x, Wq, Wk, Wv, Wo, Wa, ba, gate_W, gate_b, expert_W, expert_b, c, wmod, out):
    tokens = x.rearrange("b (g c p) d -> (b g) p c d", p=CH, c=NCH)
    out_tokens = out.rearrange("b (g c p) d -> (b g) p c d", p=CH, c=NCH)
    x1_dram = nc.dram_tensor("x1_dram", [NG, CH, NCH, D], F32, kind="Internal").ap()
    gates_dram = nc.dram_tensor("gates_dram", [2, BATCH, D], F32, kind="Internal").ap()

    with ExitStack() as keep:
        mod = keep.enter_context(nc.sbuf_tensor("mod", [128, 4, KT, BATCH], F32))
        ident = keep.enter_context(nc.sbuf_tensor("ident", [128, 128], F32))
        bank = [keep.enter_context(nc.psum_tensor(f"bank{i}", [128, 512], F32)) for i in range(8)]
        attention_phase(nc, tokens, Wq, Wk, Wv, Wo, Wa, ba, c, wmod, x1_dram, gates_dram, mod, ident, bank)
        expert_phase(nc, x1_dram, gates_dram, gate_W, gate_b, expert_W, expert_b, out_tokens, mod, ident, bank)


def attention_phase(nc, tokens, Wq, Wk, Wv, Wo, Wa, ba, c, wmod, x1_dram, gates_dram, mod, ident, bank):
    with ExitStack() as ctx:
        def sb(name, shape, dt=F32):
            return ctx.enter_context(nc.sbuf_tensor(name, shape, dt))

        def sem(name):
            return ctx.enter_context(nc.semaphore(name))

        w_names = ["wq", "wk", "wv"]
        w_hi = {n: sb(n + "_hi", [128, KT, P_DIM], F32R) for n in w_names}
        w_lo = {n: sb(n + "_lo", [128, KT, P_DIM], F32R) for n in w_names}
        wo_hi, wo_lo = (sb("wo_" + h, [128, PT, D], F32R) for h in ("hi", "lo"))
        wa = sb("wa", [128, KT, HEADS])
        ba2 = sb("ba2", [128, HEADS])
        ga = sb("ga", [128, BATCH, D])
        eye4 = sb("eye4", [128, NCH, CH])
        head_sel = sb("head_sel", [ROWS, HEADS, DH], F32R)
        head_sel32 = sb("head_sel32", [ROWS, HEADS])
        zero_row = sb("zero_row", [HEADS, CH])
        bound = sb("bound", [128, NG // 2])
        neg_bound = sb("neg_bound", [128, NG // 2])
        half_neg = sb("half_neg", [128, NCH])
        silu_t = sb("silu_t", [128, KT, BATCH])
        x_sb = sb("x_sb", [128, 2, NCH, D])
        xn = sb("xn", [128, NCH, D])
        stats = sb("stats", [128, NCH, 6])
        mean_var = sb("mean_var", [128, NCH, 2])
        var_eps = sb("var_eps", [128, NCH])
        rstd = sb("rstd", [128, NCH])
        h32 = sb("h32", [128, KT, GT])
        h_hi = [sb(f"h_hi{i}", [128, KT, GT], F32R) for i in range(2)]
        h_lo = [sb(f"h_lo{i}", [128, KT, GT], F32R) for i in range(2)]
        v_sb = sb("v_sb", [128, NCH, HEADS, VW])
        a_tok = sb("a_tok", [128, NCH, HEADS])
        a_row = sb("a_row", [HEADS, GT])
        lam_row = sb("lam_row", [HEADS, GT])
        az = [sb(f"az{i}", [ROWS, NCH, CH], F32R) for i in range(2)]
        lam = [sb(f"lam{i}", [ROWS, NCH, CH], F32R) for i in range(2)]
        oT_hi = sb("oT_hi", [128, PT, GT], F32R)
        oT_lo = sb("oT_lo", [128, PT, GT], F32R)
        q_sb = sb("q_sb", [128, GT])
        k_sb = sb("k_sb", [128, GT])
        qs_sb = sb("qs_sb", [128, 2, GT])
        lam_end = sb("lam_end", [128, 2, NCH])
        decay = sb("decay", [128, 2, GT])
        p_sb = sb("p_sb", [128, 2, 2, GT])
        kd_sb = sb("kd_sb", [128, NCH, 128])
        s_mid = sb("s_mid", [128, NCH - 1, 2 * VW])
        carry = sb("carry", [128, 2, PAIRS, 2 * VW])
        den = sb("den", [128, 2, NCH])
        rden = sb("rden", [128, 2, NCH])
        o_sb = sb("o_sb", [128, NCH, 128])
        c_sb, c_e = h32[0:BATCH, 0, 0:D], h32[0:BATCH, 0, D:2 * D]
        gates = h32[0:BATCH, 1, :].rearrange("b (s d) -> b s d", s=2)
        gates_sign = o_sb[0:BATCH, :, :].rearrange("b c n -> b (c n)").rearrange("b (s d) -> b s d", s=2)

        Q, K, SA, SB, KTR, NUM0, NUM1, DENSE = bank
        S = [SA, SB]
        U = [KTR, NUM0]
        NUM = [NUM0, NUM1]

        wmod_loaded = sem("wmod_loaded"); small_loaded = sem("small_loaded"); w_loaded = [sem(f"w_loaded{i}") for i in range(2)]
        hi_split = sem("hi_split"); lo_split = sem("lo_split")
        consts_ready = sem("consts_ready"); fills = sem("fills")
        silu_e = sem("silu_e"); silu_step = sem("silu_step"); silu_ps = sem("silu_ps"); siluT_ready = sem("siluT_ready")
        mod_ps = sem("mod_ps"); mod_ready = sem("mod_ready"); gates_step = sem("gates_step")
        gates_stored = sem("gates_stored"); ga_loaded = sem("ga_loaded"); ba_ready = sem("ba_ready")
        x_loaded = [sem(f"x_loaded{i}") for i in range(2)]; x1_stored = sem("x1_stored")
        ln_step = sem("ln_step"); var_ready = sem("var_ready"); rstd_ready = sem("rstd_ready"); xn_ready = sem("xn_ready")
        hT_ps = sem("hT_ps"); h32_ready = sem("h32_ready"); h_hi_ready = sem("h_hi_ready"); h_lo_ready = sem("h_lo_ready")
        z_ps = sem("z_ps"); zb_ready = sem("zb_ready"); z_exp = sem("z_exp"); a_step = sem("a_step"); a_ready = sem("a_ready")
        arow_ps = sem("arow_ps"); arow_ready = sem("arow_ready"); row_step = sem("row_step"); rows_ready = sem("rows_ready")
        v_ps = sem("v_ps"); v_ready = sem("v_ready")
        wo_ps = sem("wo_ps"); wo_scaled = sem("wo_scaled"); x1_ready = sem("x1_ready")
        stats_seen = sem("stats_seen")
        q_ps = sem("q_ps"); q_exp = sem("q_exp"); q_neg = sem("q_neg"); q_ready = sem("q_ready")
        k_ps = sem("k_ps"); k_exp = sem("k_exp"); k_neg = sem("k_neg"); k_ready = sem("k_ready")
        abc_ps = sem("abc_ps"); decay_ready = sem("decay_ready")
        lam_ps = sem("lam_ps"); qs_ready = sem("qs_ready"); lam_end_ready = sem("lam_end_ready")
        s_ps = sem("s_ps"); p_ready = sem("p_ready")
        ktr_ps = sem("ktr_ps"); kd_ready = sem("kd_ready")
        u_ps = sem("u_ps"); state_step = sem("state_step"); entry_clamped = sem("entry_clamped")
        num_ps = sem("num_ps"); den_step = sem("den_step"); o_ready = sem("o_ready")
        oT_ps = sem("oT_ps"); oT_hi_ready = sem("oT_hi_ready"); oT_lo_ready = sem("oT_lo_ready")

        stage = [p_sb[:, :, :, :].rearrange("p a h n -> p (a h n)"), x_sb[:, :, :, :].rearrange("p a c d -> p (a c d)")]
        wmod_half = [s[:, 0:KT * 3 * D].rearrange("p (k n) -> p k n", k=KT) for s in stage]
        big_w = [(Wq.rearrange("(k p) n -> p k n", p=128), w_hi["wq"], w_lo["wq"]),
                 (Wk.rearrange("(k p) n -> p k n", p=128), w_hi["wk"], w_lo["wk"]),
                 (Wv.rearrange("(k p) n -> p k n", p=128), w_hi["wv"], w_lo["wv"]),
                 (Wo.rearrange("(k p) n -> p k n", p=128), wo_hi, wo_lo)]
        SMALL = 3
        MOD_A = 4
        SECTION = [0, 1, 3, 4]

        def flat(t):
            return t[:, :, :].rearrange("p k n -> p (k n)")

        block = ctx.enter_context(nc.Block())

        @block.sync
        def _(sp):
            wm = wmod.rearrange("(k p) n -> p k n", p=128)
            for half in range(2):
                sp.dma_start(wmod_half[half], wm[:, :, half * 3 * D:(half + 1) * 3 * D]).then_inc(wmod_loaded, 16)
            sp.dma_start(c_sb, c).then_inc(small_loaded, 16)
            sp.dma_start(ba2[:, :], ba.partition_broadcast(128)).then_inc(small_loaded, 16)
            sp.dma_start(wa[:, :, :], Wa.rearrange("(k p) n -> p k n", p=128)).then_inc(small_loaded, 16)
            for n, (src, _, _) in enumerate(big_w):
                if n < 2:
                    sp.wait_ge(mod_ps, 1)
                else:
                    sp.wait_ge(lo_split, n - 1)
                dst = stage[n % 2].rearrange("p (k n) -> p k n", k=src.shape[1])
                sp.dma_start(dst, src).then_inc(w_loaded[n % 2], 16)
            sp.wait_ge(gates_step, 4)
            sp.dma_start(gates_dram.rearrange("s b d -> b s d"), gates).then_inc(gates_stored, 16)
            sp.wait_ge(gates_stored, 16)
            sp.dma_start(ga[:, :, :], gates_dram[0].partition_broadcast(128)).then_inc(ga_loaded, 16)
            sp.wait_ge(lo_split, len(big_w))

            def step(T, s, u):
                if u != 0:
                    return
                if exists(T - 1):
                    after(sp, x1_ready, T * 2)
                    sp.dma_start(x1_dram[bass.ds(T - 1, 1)].rearrange("g p c d -> (g p) c d"),
                                 x_sb[:, 1 - s, :, :]).then_inc(x1_stored, 16)
                if exists(T + 1):
                    after(sp, x1_stored, T * 16)
                    sp.dma_start(x_sb[:, 1 - s, :, :],
                                 tokens[bass.ds(T + 1, 1)].rearrange("g p c d -> (g p) c d")).then_inc(x_loaded[1 - s], 16)

            attention_steps(sp, step)
            sp.wait_ge(x1_stored, 16 * NG)

        @block.gpsimd
        def _(pool):
            pool.memset(ident[:, :], 0.0).then_inc(fills, 1)
            pool.memset(eye4[:, :, :], 0.0).then_inc(fills, 1)
            pool.memset(head_sel32[:, :], 0.0).then_inc(fills, 1)
            pool.memset(bound[:, :], 0.0).then_inc(fills, 1)
            pool.memset(neg_bound[:, :], 0.0).then_inc(fills, 1)
            pool.memset(half_neg[:, :], -0.5).then_inc(consts_ready, 1)
            pool.memset(zero_row[:, :], 0.0).then_inc(consts_ready, 1)
            pool.memset(carry[:, :, :, :], 0.0).then_inc(consts_ready, 1)
            pool.memset(s_mid[:, :, :], 0.0).then_inc(consts_ready, 1)
            pool.memset(v_sb[:, :, :, DH:VW], 1.0).then_inc(consts_ready, 1)
            pool.wait_ge(fills, 5)
            pool.memset(bound[:, :].rearrange("p (r e) -> p r e", e=2)[:, :, 1:2], BIG).then_inc(consts_ready, 1)
            pool.memset(neg_bound[:, :].rearrange("p (r e) -> p r e", e=2)[:, :, 1:2], -BIG).then_inc(consts_ready, 1)
            pool.affine_select(out=ident[:, :], in_=ident[:, :], compare_op=ALU.not_equal, fill=1.0, base=0,
                               pattern=[[-1, 128]], channel_multiplier=1).then_inc(consts_ready, 1)
            pool.affine_select(out=eye4[:, :, :], in_=eye4[:, :, :], compare_op=ALU.not_equal, fill=1.0, base=0,
                               pattern=[[0, NCH], [-1, CH]], channel_multiplier=1).then_inc(consts_ready, 1)
            pool.affine_select(out=head_sel32[:, :], in_=head_sel32[:, :], compare_op=ALU.not_equal, fill=1.0,
                               base=0, pattern=[[-1, HEADS]], channel_multiplier=1).then_inc(fills, 1)
            pool.wait_ge(fills, 6)
            pool.affine_select(out=head_sel32[:, :], in_=head_sel32[:, :], compare_op=ALU.not_equal, fill=1.0,
                               base=-LO, pattern=[[-1, HEADS]], channel_multiplier=1).then_inc(consts_ready, 1)

            def step(T, s, u):
                if u == 0 and exists(T - 1):
                    for j in range(2):
                        after(pool, wo_scaled, (T - 1) * 2 + j + 1)
                        rows = x_sb[:, 1 - s, 2 * j:2 * j + 2, :]
                        pool.tensor_tensor(rows, rows, xn[:, 2 * j:2 * j + 2, :], ALU.add).then_inc(x1_ready, 1)
                if u == 2 and exists(T + 1):
                    after(pool, var_ready, T + 2)
                    pool.tensor_tensor(rstd[:, :], var_eps[:, :], half_neg[:, :], ALU.pow).then_inc(rstd_ready, 1)
            attention_steps(pool, step)

        @block.scalar
        def _(act):
            act.wait_ge(small_loaded, 16 * SMALL)
            act.activation(c_e, c_sb, ACT.Exp, scale=-1.0).then_inc(silu_e, 1)
            for n, (_, hi, _) in enumerate(big_w):
                act.wait_ge(w_loaded[n % 2], 16 * (n // 2 + 1))
                act.activation(flat(hi), stage[n % 2], ACT.Copy).then_inc(hi_split, 1)

            def v_out(T, half, ch):
                act.wait_ge(v_ps, T * 8 + half * NCH + ch + 1)
                hs = half * (HEADS // 2)
                act.activation(v_sb[:, ch, hs:hs + HEADS // 2, 0:DH],
                               DENSE[:, :].rearrange("p (h d) -> p h d", d=DH), ACT.Copy).then_inc(v_ready, 1)

            def h_out(T, s, kt):
                act.wait_ge(hT_ps, T * 2 + kt + 1)
                if kt == 0:
                    act.wait_ge(mod_ready, 2)
                    if isinstance(T, int) and T == 0:
                        act.wait_ge(gates_stored, 16)
                b = batch_row(T)
                act.activation(h32[:, kt, :], DENSE[:, :], ACT.Identity, bias=mod[:, 0, kt, bass.ds(b, 1)],
                               scale=mod[:, 1, kt, bass.ds(b, 1)]).then_inc(h32_ready, 1)
                act.wait_ge(h32_ready, T * 2 + kt + 1)
                act.activation(h_hi[s][:, kt, :], h32[:, kt, :], ACT.Copy).then_inc(h_hi_ready, 1)

            def dense_out(T, s, u, part):
                if u in (1, 2) and exists(T):
                    v_out(T, 1, 2 * (u - 1) + part)
                if u == 4 and exists(T + 1):
                    h_out(T + 1, 1 - s, part)
                if u in (6, 7) and exists(T + 1):
                    v_out(T + 1, 0, 2 * (u - 6) + part)

            def step(T, s, u):
                Ta, _, a = unit(T, u, 2)
                dense_out(T, s, u, 0)
                if exists(Ta):
                    act.wait_ge(q_ps, a + 1)
                    after(act, qs_ready, a)
                    act.activation(q_sb[:, :], Q[:, :], ACT.Relu, scale=-1.0).then_inc(q_neg, 1)
                    act.wait_ge(q_neg, a + 1)
                    act.activation(q_sb[:, :], q_sb[:, :], ACT.Exp, scale=-1.0).then_inc(q_exp, 1)
                if u == 5 and exists(T + 1):
                    act.wait_ge(zb_ready, T + 2)
                    act.activation(a_tok[:, :, :], a_tok[:, :, :], ACT.Exp, scale=-1.0).then_inc(z_exp, 1)
                if exists(Ta):
                    act.wait_ge(k_ps, a + 1)
                    act.activation(k_sb[:, :], K[:, :], ACT.Relu, scale=-1.0).then_inc(k_neg, 1)
                    act.wait_ge(k_neg, a + 1)
                    act.activation(k_sb[:, :], k_sb[:, :], ACT.Exp, scale=-1.0).then_inc(k_exp, 1)
                dense_out(T, s, u, 1)
                if exists(T):
                    n = T * PAIRS + u
                    act.wait_ge(oT_ps, n + 1)
                    act.activation(oT_hi[:, u, :], NUM1[:, :], ACT.Copy).then_inc(oT_hi_ready, 1)

            attention_steps(act, step)

        @block.tensor
        def _(pe):
            pe.wait_ge(consts_ready, 10)
            pe.wait_ge(silu_step, 3)
            for kt in range(KT):
                mm = pe.transpose(DENSE[:, kt * BATCH:(kt + 1) * BATCH], c_e[:, kt * 128:(kt + 1) * 128],
                                  ident[0:BATCH, 0:BATCH])
            mm.then_inc(silu_ps, 1)
            pe.wait_ge(siluT_ready, 1)
            pe.wait_ge(wmod_loaded, 32)
            for m, sec in enumerate(SECTION):
                for kt in range(KT):
                    col = (m * KT + kt) * BATCH
                    w = wmod_half[sec // 3][:, :, (sec % 3) * D + kt * 128:(sec % 3) * D + (kt + 1) * 128]
                    for k2 in range(KT):
                        pe.matmul(SA[:, col:col + BATCH], w[:, k2, :], silu_t[:, k2, :],
                                  start=(k2 == 0), stop=(k2 == KT - 1))
            for g in range(2):
                for k2 in range(KT):
                    mm = pe.matmul(SB[0:BATCH, g * D:(g + 1) * D], silu_t[:, k2, :],
                                   wmod_half[g][:, k2, 2 * D:3 * D], start=(k2 == 0), stop=(k2 == KT - 1))
            mm.then_inc(mod_ps, 1)
            pe.wait_ge(mod_ready, 3)
            pe.wait_ge(gates_step, 3)

            def three_pass(dst, pairs):
                last = len(pairs) - 1
                for n, (s_hi, s_lo, m_hi, m_lo) in enumerate(pairs):
                    pe.matmul(dst, s_hi, m_hi, start=(n == 0), stop=False)
                    pe.matmul(dst, s_hi, m_lo, start=False, stop=False)
                    mm = pe.matmul(dst, s_lo, m_hi, start=False, stop=(n == last))
                return mm

            def project(Tn, sn, p, w, dst, done):
                h, l = h_hi[sn], h_lo[sn]
                cols = slice(p * 128, (p + 1) * 128)
                three_pass(dst[:, :], [(w_hi[w][:, kt, cols], w_lo[w][:, kt, cols], h[:, kt, :], l[:, kt, :])
                                       for kt in range(KT)]).then_inc(done, 1)

            def h_job(T, kt):
                if kt == 0:
                    after(pe, v_ready, (T - 1) * 8 + 8)
                    pe.wait_ge(xn_ready, T + 1)
                else:
                    pe.wait_ge(h32_ready, T * 2 + 1)
                for ch in range(NCH):
                    mm = pe.transpose(DENSE[:, ch * CH:(ch + 1) * CH], xn[:, ch, kt * 128:(kt + 1) * 128], ident[:, :])
                mm.then_inc(hT_ps, 1)

            def z_job(T):
                pe.wait_ge(h32_ready, T * 2 + 2)
                for ch in range(NCH):
                    for kt in range(KT):
                        mm = pe.matmul(DENSE[:, ch * HEADS:(ch + 1) * HEADS], h32[:, kt, ch * CH:(ch + 1) * CH],
                                       wa[:, kt, :], start=(kt == 0), stop=(kt == KT - 1))
                mm.then_inc(z_ps, 1)

            def arow_job(T):
                pe.wait_ge(a_ready, T + 1)
                for ch in range(NCH):
                    mm = pe.transpose(DENSE[0:HEADS, ch * CH:(ch + 1) * CH], a_tok[:, ch, :], ident[:, :])
                mm.then_inc(arow_ps, 1)

            def v_job(T, s, half, ch):
                n = T * 8 + half * NCH + ch
                if half == 0 and ch == 0:
                    pe.wait_ge(arow_ready, T + 1)
                    after(pe, num_ps, ((T - 1) * PAIRS + PAIRS // 2) * 2)
                elif half == 1 and ch == 0:
                    after(pe, wo_scaled, T * 2)
                    after(pe, v_ready, n)
                else:
                    pe.wait_ge(v_ready, n)
                pe.wait_ge(h_lo_ready, T * 2 + 2)
                tok = slice(ch * CH, (ch + 1) * CH)
                cols = slice(half * 512, (half + 1) * 512)
                three_pass(DENSE[:, :], [(h_hi[s][:, kt, tok], h_lo[s][:, kt, tok], w_hi["wv"][:, kt, cols],
                                          w_lo["wv"][:, kt, cols]) for kt in range(KT)]).then_inc(v_ps, 1)

            def wo_job(T, j):
                if j == 0:
                    after(pe, v_ready, T * 8 + (12 if exists(T + 1) else 8))
                    pe.wait_ge(oT_lo_ready, T * PAIRS + PAIRS)
                else:
                    pe.wait_ge(wo_scaled, T * 2 + 1)
                for i in range(2):
                    tok = slice((2 * j + i) * CH, (2 * j + i + 1) * CH)
                    mm = three_pass(DENSE[:, i * D:(i + 1) * D],
                                    [(oT_hi[:, pt, tok], oT_lo[:, pt, tok], wo_hi[:, pt, :], wo_lo[:, pt, :])
                                     for pt in range(PT)])
                mm.then_inc(wo_ps, 1)

            def dense_job(T, s, u, part):
                if u == 0 and exists(T - 1):
                    wo_job(T - 1, part)
                if u in (1, 2) and exists(T):
                    v_job(T, s, 1, 2 * (u - 1) + part)
                if u == 4 and exists(T + 1):
                    h_job(T + 1, part)
                if u == 5 and exists(T + 1):
                    (z_job, arow_job)[part](T + 1)
                if u in (6, 7) and exists(T + 1):
                    v_job(T + 1, 1 - s, 0, 2 * (u - 6) + part)

            def step(T, s, u):
                n = T * PAIRS + u
                Tb, pb, b = unit(T, u, 1)
                Ta, pa, a = unit(T, u, 2)
                sa = s if u + 2 < PAIRS else 1 - s
                if exists(Tb):
                    pe.wait_ge(q_ready, b + 1)
                    pe.wait_ge(k_ready, b + 1)
                    pe.wait_ge(decay_ready, 2 * b + 2)
                    for ch in range(NCH):
                        tok = slice(ch * CH, (ch + 1) * CH)
                        for hd in range(2):
                            rows = slice(hd * DH, (hd + 1) * DH)
                            mm = pe.matmul(S[hd][:, tok], k_sb[rows, tok], q_sb[rows, tok], start=True, stop=True)
                            if ch == NCH - 1:
                                mm.then_inc(s_ps, 1)
                    after(pe, state_step, b * 8)
                    for ch in range(NCH):
                        mm = pe.transpose(KTR[:, ch * CH:(ch + 1) * CH], k_sb[:, ch * CH:(ch + 1) * CH], ident[:, :])
                    mm.then_inc(ktr_ps, 1)
                dense_job(T, s, u, 0)
                if exists(Ta):
                    pe.wait_ge(h_lo_ready, Ta * 2 + 2)
                    after(pe, qs_ready, a)
                    project(Ta, sa, pa, "wq", Q, q_ps)
                if exists(T):
                    pe.wait_ge(qs_ready, n + 1)
                    pe.wait_ge(p_ready, 2 * n + 2)
                    pe.wait_ge(state_step, n * 8 + 8)
                    after(pe, oT_lo_ready, n)
                    for ch in range(NCH):
                        tok = slice(ch * CH, (ch + 1) * CH)
                        state = carry[:, s, u, :] if ch == 0 else s_mid[:, ch - 1, :]
                        at = (ch % 2) * 2 * VW
                        num = NUM[ch // 2]
                        pe.matmul(num[:, at:at + 2 * VW], qs_sb[:, u % 2, tok], state, start=True, stop=False)
                        for hd in range(2):
                            mm = pe.matmul(num[:, at + hd * VW:at + (hd + 1) * VW], p_sb[:, u % 2, hd, tok],
                                           v_sb[:, ch, 2 * u + hd, :], start=False, stop=(hd == 1))
                        if ch % 2:
                            mm.then_inc(num_ps, 1)
                if exists(Ta):
                    after(pe, k_ready, a)
                    project(Ta, sa, pa, "wk", K, k_ps)
                dense_job(T, s, u, 1)

                def states(half):
                    for ch in (2 * half, 2 * half + 1):
                        at = (ch % 2) * 2 * VW
                        mm = pe.matmul(U[half][:, at:at + 2 * VW], kd_sb[:, ch, :],
                                       v_sb[:, ch, 2 * pb:2 * pb + 2, :], start=True, stop=True)
                    mm.then_inc(u_ps, 1)

                if exists(Tb):
                    pe.wait_ge(kd_ready, b + 1)
                    pe.wait_ge(v_ready, Tb * 8 + (NCH if pb < PAIRS // 2 else 2 * NCH))
                    states(0)
                if exists(Ta):
                    pe.wait_ge(rows_ready, Ta + 1)
                    after(pe, p_ready, 2 * a)
                    for hd in range(2):
                        hcol = head_sel[:, 2 * pa + hd, 0:1]
                        pe.matmul(S[hd][:, :], hcol.to_broadcast([ROWS, 128]),
                                  az[sa][:, :, :].rearrange("r c i -> r (c i)"),
                                  start=True, stop=True).then_inc(abc_ps, 1)
                if exists(Tb):
                    after(pe, o_ready, 2 * b - 1)
                    states(1)
                if exists(T):
                    pe.wait_ge(o_ready, 2 * n + 2)
                    for ch in range(NCH):
                        mm = pe.transpose(NUM1[:, ch * CH:(ch + 1) * CH], o_sb[:, ch, :], ident[:, :])
                    mm.then_inc(oT_ps, 1)
                if exists(Ta):
                    pe.wait_ge(q_ready, a + 1)
                    pe.matmul(Q[:, :], head_sel[:, 2 * pa:2 * pa + 2, :].rearrange("r h d -> r (h d)"),
                              lam[sa][:, :, :].rearrange("r c i -> r (c i)"), start=True, stop=True).then_inc(lam_ps, 1)

            attention_steps(pe, step)

        @block.vector
        def _(dve):
            dve.wait_ge(silu_e, 1)
            dve.tensor_scalar(c_e, c_e, 1.0, None, ALU.add).then_inc(silu_step, 1)
            dve.wait_ge(silu_step, 1)
            dve.reciprocal(c_e, c_e).then_inc(silu_step, 1)
            dve.wait_ge(silu_step, 2)
            dve.tensor_tensor(c_e, c_e, c_sb, ALU.mult).then_inc(silu_step, 1)
            dve.tensor_scalar(ba2[:, :], ba2[:, :], DECAY_BIAS_SHIFT, None, ALU.add).then_inc(ba_ready, 1)
            dve.wait_ge(silu_ps, 1)
            dve.tensor_copy(silu_t[:, :, :], DENSE[:, 0:KT * BATCH].rearrange("p (k b) -> p k b", b=BATCH))\
               .then_inc(siluT_ready, 1)
            dve.wait_ge(consts_ready, 10)
            dve.tensor_copy(head_sel[:, :, :], head_sel32[:, :].unsqueeze(2).to_broadcast([ROWS, HEADS, DH]))
            for t in (*az, *lam):
                dve.memset(t[:, :, :].bitcast(F32), 0.0)
            dve.wait_ge(mod_ps, 1)
            mods = SA[:, 0:MOD_A * KT * BATCH].rearrange("p (m k b) -> p m k b", k=KT, b=BATCH)
            for m in range(MOD_A):
                dve.tensor_scalar(mod[:, m, :, :], mods[:, m, :, :], float(m % 2), None, ALU.add)\
                   .then_inc(mod_ready, 1)
            g_ps = SB[0:BATCH, :].rearrange("b (s d) -> b s d", s=2)
            dve.tensor_scalar(gates_sign, g_ps, 0.0, 2.0, ALU.is_ge, ALU.mult).then_inc(gates_step, 1)
            dve.tensor_scalar(gates, g_ps, -1.0, None, ALU.mult).then_inc(gates_step, 1)
            dve.wait_ge(gates_step, 2)
            dve.scalar_tensor_tensor(gates, g_ps, GATE_FLOOR, gates, ALU.max, ALU.max).then_inc(gates_step, 1)
            dve.wait_ge(gates_step, 3)
            dve.scalar_tensor_tensor(gates, gates_sign, -1.0, gates, ALU.add, ALU.mult).then_inc(gates_step, 1)
            for n, (_, hi, lo) in enumerate(big_w):
                dve.wait_ge(hi_split, n + 1)
                dve.tensor_tensor(flat(lo), stage[n % 2], flat(hi).bitcast(F32), ALU.subtract).then_inc(lo_split, 1)

            def wo_out(T, s, j):
                b = batch_row(T)
                if j == 0 and isinstance(T, int) and T == 0:
                    dve.wait_ge(ga_loaded, 16)
                dve.wait_ge(wo_ps, T * 2 + j + 1)
                after(dve, x1_ready, T * 2)
                gb = ga[:, bass.ds(b, 1), :].to_broadcast([128, 2, D])
                dve.tensor_tensor(xn[:, 2 * j:2 * j + 2, :], DENSE[:, :].rearrange("p (c d) -> p c d", d=D), gb,
                                  ALU.mult).then_inc(wo_scaled, 1)

            def ln_stats(T, s):
                dve.wait_ge(x_loaded[s], T * 8 + 16 - 8 * s)
                for ch in range(NCH):
                    dve.bn_stats(stats[:, ch, :], x_sb[:, s, ch, :]).then_inc(ln_step, 1)
                dve.wait_ge(ln_step, T * 8 + NCH)
                dve.sem_inc(stats_seen)
                for ch in range(NCH):
                    dve.bn_aggr(mean_var[:, ch, :], stats[:, ch, :]).then_inc(ln_step, 1)
                dve.wait_ge(ln_step, T * 8 + 8)
                dve.tensor_scalar(var_eps[:, :].unsqueeze(2), mean_var[:, :, 1:2], LN_EPS, None, ALU.add)\
                   .then_inc(var_ready, 1)

            def ln_apply(T, s):
                dve.wait_ge(rstd_ready, T + 1)
                after(dve, x1_ready, T * 2 - 2)
                for ch in range(NCH):
                    ins = dve.tensor_scalar(xn[:, ch, :], x_sb[:, s, ch, :], mean_var[:, ch, 0:1], rstd[:, ch:ch + 1],
                                            ALU.subtract, ALU.mult)
                ins.then_inc(xn_ready, 1)

            def h_low(T, s, kt):
                dve.wait_ge(h_hi_ready, T * 2 + kt + 1)
                dve.tensor_tensor(h_lo[s][:, kt, :], h32[:, kt, :], h_hi[s][:, kt, :].bitcast(F32), ALU.subtract)\
                   .then_inc(h_lo_ready, 1)

            def z_out(T):
                dve.wait_ge(z_ps, T + 1)
                dve.wait_ge(ba_ready, 1)
                dve.tensor_tensor(a_tok[:, :, :], DENSE[:, 0:NCH * HEADS].rearrange("p (c h) -> p c h", h=HEADS),
                                  ba2[:, :].unsqueeze(1).to_broadcast([128, NCH, HEADS]), ALU.add).then_inc(zb_ready, 1)

            def sigmoid(T):
                dve.wait_ge(z_exp, T + 1)
                dve.tensor_scalar(a_tok[:, :, :], a_tok[:, :, :], 1.0, None, ALU.add).then_inc(a_step, 1)
                dve.wait_ge(a_step, T + 1)
                dve.reciprocal(a_tok[:, :, :], a_tok[:, :, :]).then_inc(a_ready, 1)

            def arow_out(T):
                dve.wait_ge(arow_ps, T + 1)
                dve.tensor_copy(a_row[:, :], DENSE[0:HEADS, :]).then_inc(arow_ready, 1)

            def decay_rows(T, s):
                dve.wait_ge(arow_ready, T + 1)
                for ch in range(NCH):
                    tok = slice(ch * CH, (ch + 1) * CH)
                    ins = dve.tensor_tensor_scan(lam_row[:, tok], a_row[:, tok], zero_row[:, :], 1.0, ALU.mult, ALU.add)
                ins.then_inc(row_step, 1)
                for dst, src in ((az[s], a_row), (lam[s], lam_row)):
                    if src is lam_row:
                        dve.wait_ge(row_step, T * 4 + 2)
                    hi = dst[0:HEADS, :, :].rearrange("r c i -> r (c i)")
                    dve.tensor_copy(hi, src[:, :]).then_inc(row_step, 1)
                    dve.wait_ge(row_step, T * 4 + (2 if src is a_row else 4))
                    lo = dve.tensor_tensor(dst[LO:ROWS, :, :].rearrange("r c i -> r (c i)"), src[:, :], hi.bitcast(F32),
                                           ALU.subtract)
                    lo.then_inc(row_step if src is a_row else rows_ready, 1)
                    if src is a_row:
                        dve.wait_ge(row_step, T * 4 + 3)
                        dve.memset(dst[:, :, 0:1].bitcast(F32), 0.0)

            def dense_out(T, s, u, part):
                if u == 0 and exists(T - 1):
                    wo_out(T - 1, 1 - s, part)
                if u == 4 and exists(T + 1):
                    h_low(T + 1, 1 - s, part)
                if u == 5 and exists(T + 1):
                    (z_out, arow_out)[part](T + 1)

            def step(T, s, u):
                n = T * PAIRS + u
                Tb, pb, b = unit(T, u, 1)
                Ta, pa, a = unit(T, u, 2)
                nb = (u + 1) % 2
                na = u % 2
                sb_ = s if u + 1 < PAIRS else 1 - s
                if exists(Tb):
                    for hd in range(2):
                        dve.wait_ge(s_ps, 2 * b + hd + 1)
                        dve.wait_ge(decay_ready, 2 * b + hd + 1)
                        dve.tensor_tensor(p_sb[:, nb, hd, :], S[hd][:, :], decay[:, hd, :], ALU.mult)\
                           .then_inc(p_ready, 1)
                    dve.wait_ge(ktr_ps, b + 1)
                    to_end = decay[:, :, :].rearrange("p h (c i) -> p c h i", i=CH)[:, :, :, CH - 1:CH]
                    dve.tensor_tensor(kd_sb[:, :, :].rearrange("p c (h d) -> p c h d", d=DH),
                                      KTR[:, :].rearrange("p (c h d) -> p c h d", h=2, d=DH),
                                      to_end.to_broadcast([128, NCH, 2, DH]), ALU.mult).then_inc(kd_ready, 1)
                dense_out(T, s, u, 0)
                if exists(Ta):
                    dve.wait_ge(q_exp, a + 1)
                    dve.scalar_tensor_tensor(q_sb[:, :], Q[:, :], 1.0, q_sb[:, :], ALU.add, ALU.max).then_inc(q_ready, 1)
                if u == 5 and exists(T + 1):
                    sigmoid(T + 1)
                if exists(T):
                    for half in range(2):
                        dve.wait_ge(num_ps, 2 * n + half + 1)
                        num = NUM[half][:, 0:4 * VW].rearrange("p (e v) -> p e v", v=VW)
                        dve.tensor_scalar(den[:, half, :].unsqueeze(2), num[:, :, DH:VW], DEN_EPS, None, ALU.add)\
                           .then_inc(den_step, 1)
                    dve.wait_ge(den_step, 3 * n + 2)
                    dve.reciprocal(rden[:, :, :], den[:, :, :]).then_inc(den_step, 1)
                    dve.wait_ge(den_step, 3 * n + 3)
                    for half in range(2):
                        num = NUM[half][:, 0:4 * VW].rearrange("p (e v) -> p e v", v=VW)
                        dve.tensor_tensor(o_sb[:, 2 * half:2 * half + 2, :].rearrange("p c (h d) -> p (c h) d", d=DH),
                                          num[:, :, 0:DH], rden[:, half, :].unsqueeze(2).to_broadcast([128, 4, DH]),
                                          ALU.mult).then_inc(o_ready, 1)
                if exists(Ta):
                    dve.wait_ge(k_exp, a + 1)
                    dve.scalar_tensor_tensor(k_sb[:, :], K[:, :], 1.0, k_sb[:, :], ALU.add, ALU.max).then_inc(k_ready, 1)
                dense_out(T, s, u, 1)
                if exists(Ta):
                    for hd in range(2):
                        dve.wait_ge(abc_ps, 2 * a + hd + 1)
                        dve.tensor_tensor_scan(decay[:, hd, :], S[hd][:, :], eye4[:, :, :].rearrange("p c i -> p (c i)"),
                                               0.0, ALU.mult, ALU.add).then_inc(decay_ready, 1)
                if exists(Tb):
                    entry = carry[:, sb_, pb, :]
                    if sb_ == 0 and not (isinstance(Tb, int) and Tb == 0):
                        i = Tb >> 1
                        dve.wait_ge(state_step, (b - PAIRS + 1) * 8)
                        dve.tensor_scalar(entry, entry, bound[:, bass.ds(i, 1)], neg_bound[:, bass.ds(i, 1)],
                                          ALU.min, ALU.max).then_inc(entry_clamped, 1)
                        dve.wait_ge(entry_clamped, Tb * (PAIRS // 2) - PAIRS + pb + 1)
                    dve.wait_ge(lam_end_ready, b + 1)
                    for ch in range(NCH):
                        src = entry if ch == 0 else s_mid[:, ch - 1, :]
                        dst = s_mid[:, ch, :] if ch < NCH - 1 else carry[:, 1 - sb_, pb, :]
                        if ch % 2 == 0:
                            dve.wait_ge(u_ps, 2 * b + ch // 2 + 1)
                        for hd in range(2):
                            rows = slice(hd * DH, (hd + 1) * DH)
                            cols = slice(hd * VW, (hd + 1) * VW)
                            at = (ch % 2) * 2 * VW + hd * VW
                            if ch:
                                dve.wait_ge(state_step, b * 8 + ch * 2 + hd - 1)
                            dve.scalar_tensor_tensor(dst[rows, cols], src[rows, cols],
                                                     lam_end[rows, nb, ch:ch + 1], U[ch // 2][rows, at:at + VW],
                                                     ALU.mult, ALU.add).then_inc(state_step, 1)
                if exists(Ta):
                    dve.wait_ge(lam_ps, a + 1)
                    dve.tensor_copy(lam_end[:, na, :].unsqueeze(2),
                                    Q[:, :].rearrange("p (c i) -> p c i", i=CH)[:, :, CH - 1:CH]).then_inc(lam_end_ready, 1)
                    dve.wait_ge(q_ready, a + 1)
                    dve.tensor_tensor(qs_sb[:, na, :], Q[:, :], q_sb[:, :], ALU.mult).then_inc(qs_ready, 1)
                if exists(T):
                    dve.wait_ge(oT_hi_ready, n + 1)
                    dve.tensor_tensor(oT_lo[:, u, :], NUM1[:, :], oT_hi[:, u, :].bitcast(F32), ALU.subtract)\
                       .then_inc(oT_lo_ready, 1)
                if u == 2 and exists(T + 1):
                    ln_stats(T + 1, 1 - s)
                if u == 3 and exists(T + 1):
                    ln_apply(T + 1, 1 - s)
                if u == 5 and exists(T + 1):
                    decay_rows(T + 1, 1 - s)

            attention_steps(dve, step)


def expert_phase(nc, x1_dram, gates_dram, gate_W, gate_b, expert_W, expert_b, out_tokens, mod, ident, bank):
    EW = EXPERTS * D
    YB = EW // 512
    with ExitStack() as ctx:
        def sb(name, shape, dt=F32):
            return ctx.enter_context(nc.sbuf_tensor(name, shape, dt))

        def sem(name):
            return ctx.enter_context(nc.semaphore(name))

        ew_hi, ew_lo = (sb("ew_" + h, [128, KT, EXPERTS, D], F32R) for h in ("hi", "lo"))
        ew_raw = sb("ew_raw", [128, KT, EXPERTS, D])
        eb = sb("eb", [EXPERTS, D])
        gw = sb("gw", [128, KT, EXPERTS])
        gbias = sb("gbias", [128, EXPERTS])
        gb = sb("gb", [128, BATCH, D])
        rank = sb("rank", [128, EXPERTS])
        half_neg2 = sb("half_neg2", [128, NCH])

        x1 = [sb(f"x1_{i}", [128, NCH, D]) for i in range(GPB)]
        xn = sb("xn2", [128, NCH, D])
        stats = sb("stats2", [128, NCH, 6])
        mean_var = sb("mean_var2", [128, NCH, 2])
        var_eps = sb("var_eps2", [128, NCH])
        rstd = sb("rstd2", [128, NCH])
        h32 = sb("h32_2", [128, KT, GT])
        h_hi = [sb(f"h2_hi{i}", [128, KT, GT], F32R) for i in range(2)]
        h_lo = [sb(f"h2_lo{i}", [128, KT, GT], F32R) for i in range(2)]
        sc, p, first, second, tmp = (sb(n, [128, NCH, EXPERTS]) for n in ("sc", "prob", "first", "second", "tmp"))
        red = sb("red", [128, 8, NCH])
        comb = [sb(f"comb{i}", [128, NCH, EXPERTS]) for i in range(2)]
        combT = sb("combT", [EXPERTS, GT])
        acc = [sb(f"acc{i}", [128, NCH, D]) for i in range(2)]

        Y = bank[0:4]
        HT, GATE, BIAS = bank[4], bank[5], bank[6:8]

        loaded = sem("e_loaded"); gb_loaded = sem("gb_loaded"); hi_split = sem("e_hi_split"); lo_split = sem("e_lo_split")
        fills = sem("e_fills")
        x1_loaded = [sem(f"x1_loaded{i}") for i in range(GPB)]
        out_stored = [sem(f"out_stored{i}") for i in range(GPB)]
        ln_step = sem("ln2_step"); var_ready = sem("var2_ready"); rstd_ready = sem("rstd2_ready"); xn_ready = sem("xn2_ready")
        hT_ps = sem("h2T_ps"); h32_ready = sem("h2_32_ready"); h_hi_ready = sem("h2_hi_ready"); h_lo_ready = sem("h2_lo_ready")
        stats_seen = sem("stats2_seen")
        gate_ps = sem("gate_ps"); route_step = sem("route_step"); route_exp_in = sem("route_exp_in"); route_exp = sem("route_exp"); total_ready = sem("total_ready")
        comb_ready = sem("comb_ready"); combT_ps = sem("combT_ps"); combT_ready = sem("combT_ready")
        bias_ps = sem("bias_ps"); acc_ready = sem("acc_ready")
        y_ps = sem("y_ps"); y_added = sem("y_added"); scaled = sem("scaled"); result_ready = sem("result_ready")

        ROUTE = 20
        ADDS = NCH * EXPERTS

        def wide(t):
            return t[:, :, :, :].rearrange("p k e d -> p (k e d)")

        block = ctx.enter_context(nc.Block())

        @block.sync
        def _(sp):
            for kt in range(KT):
                sp.dma_start(ew_raw[:, kt, :, :], expert_W[:, kt * 128:(kt + 1) * 128, :].rearrange("e p f -> p e f"))\
                  .then_inc(loaded, 16)
            sp.dma_start(eb[:, :], expert_b).then_inc(loaded, 16)
            sp.dma_start(gw[:, :, :], gate_W.rearrange("(k p) e -> p k e", p=128)).then_inc(loaded, 16)
            sp.dma_start(gbias[:, :], gate_b.partition_broadcast(128)).then_inc(loaded, 16)
            sp.dma_start(gb[:, :, :], gates_dram[1].partition_broadcast(128)).then_inc(gb_loaded, 16)

            def load(T, s):
                after(sp, out_stored[s], (T - s) * (16 // GPB))
                sp.dma_start(x1[s][:, :, :], x1_dram[bass.ds(T, 1)].rearrange("g p c d -> (g p) c d"))\
                  .then_inc(x1_loaded[s], 16)

            def group(T, s):
                if isinstance(T, int) and T == -1:
                    load(0, 0)
                    load(1, 1)
                if exists(T) and exists(T + 2):
                    load(T + 2, (s + 2) % GPB)
                if exists(T):
                    sp.wait_ge(result_ready, T + 1)
                    sp.dma_start(out_tokens[bass.ds(T, 1)].rearrange("g p c d -> (g p) c d"), x1[s][:, :, :])\
                      .then_inc(out_stored[s], 16)

            expert_groups(sp, group)
            for s in range(GPB):
                sp.wait_ge(out_stored[s], 16 * NG // GPB)

        @block.gpsimd
        def _(pool):
            pool.memset(half_neg2[:, :], -0.5).then_inc(fills, 1)
            for e in range(EXPERTS):
                pool.memset(rank[:, e:e + 1], float(EXPERTS - e)).then_inc(fills, 1)
            pool.wait_ge(fills, 1 + EXPERTS)

            def group(T, s):
                if exists(T + 1):
                    pool.wait_ge(var_ready, T + 2)
                    pool.tensor_tensor(rstd[:, :], var_eps[:, :], half_neg2[:, :], ALU.pow).then_inc(rstd_ready, 1)
                if exists(T):
                    b = batch_row(T)
                    if isinstance(T, int) and T == 0:
                        pool.wait_ge(gb_loaded, 16)
                    pool.wait_ge(y_added, T * ADDS + ADDS)
                    a = acc[s % 2][:, :, :]
                    pool.tensor_tensor(a, a, gb[:, bass.ds(b, 1), :].to_broadcast([128, NCH, D]), ALU.mult)\
                        .then_inc(scaled, 1)
                    pool.wait_ge(scaled, T + 1)
                    pool.tensor_tensor(x1[s][:, :, :], x1[s][:, :, :], a, ALU.add).then_inc(result_ready, 1)

            expert_groups(pool, group)

        @block.scalar
        def _(act):
            act.wait_ge(loaded, 16 * 5)
            act.activation(wide(ew_hi), wide(ew_raw), ACT.Copy).then_inc(hi_split, 1)

            def group(T, s):
                if not exists(T + 1):
                    return
                Tn, sn = T + 1, (s + 1) % 2
                b = batch_row(Tn)
                for kt in range(KT):
                    act.wait_ge(hT_ps, Tn * 2 + kt + 1)
                    if kt == 0:
                        after(act, gate_ps, Tn)
                    act.activation(h32[:, kt, :], HT[:, :], ACT.Identity, bias=mod[:, 2, kt, bass.ds(b, 1)],
                                   scale=mod[:, 3, kt, bass.ds(b, 1)]).then_inc(h32_ready, 1)
                    act.wait_ge(h32_ready, Tn * 2 + kt + 1)
                    act.activation(h_hi[sn][:, kt, :], h32[:, kt, :], ACT.Copy).then_inc(h_hi_ready, 1)
                act.wait_ge(route_exp_in, Tn + 1)
                act.activation(p[:, :, :], sc[:, :, :], ACT.Exp).then_inc(route_exp, 1)
                for j in range(2):
                    act.wait_ge(bias_ps, Tn * 2 + j + 1)
                    after(act, result_ready, Tn - 1)
                    act.activation(acc[sn][:, 2 * j:2 * j + 2, :], BIAS[j][:, :].rearrange("p (c d) -> p c d", d=D),
                                   ACT.Copy).then_inc(acc_ready, 1)

            expert_groups(act, group)

        @block.tensor
        def _(pe):
            pe.wait_ge(lo_split, 1)

            def y_chunk(T, s, ch):
                tok = slice(ch * CH, (ch + 1) * CH)
                h, l = h_hi[s % 2], h_lo[s % 2]
                for q in range(YB):
                    n = ch * YB + q
                    after(pe, y_added, T * ADDS + 2 * n - 2 * (YB - 1))
                    ex = slice(2 * q, 2 * q + 2)
                    for kt in range(KT):
                        pe.matmul(Y[q][:, :], h[:, kt, tok], ew_hi[:, kt, ex, :], start=(kt == 0), stop=False)
                        pe.matmul(Y[q][:, :], h[:, kt, tok], ew_lo[:, kt, ex, :], start=False, stop=False)
                        mm = pe.matmul(Y[q][:, :], l[:, kt, tok], ew_hi[:, kt, ex, :], start=False, stop=(kt == KT - 1))
                    mm.then_inc(y_ps, 1)

            def transpose_h(Tn):
                pe.wait_ge(xn_ready, Tn + 1)
                for kt in range(KT):
                    after(pe, h32_ready, Tn * 2 + kt)
                    for ch in range(NCH):
                        mm = pe.transpose(HT[:, ch * CH:(ch + 1) * CH], xn[:, ch, kt * 128:(kt + 1) * 128], ident[:, :])
                    mm.then_inc(hT_ps, 1)

            def gate(Tn):
                pe.wait_ge(h32_ready, Tn * 2 + 2)
                after(pe, combT_ready, Tn)
                for ch in range(NCH):
                    for kt in range(KT):
                        mm = pe.matmul(GATE[:, ch * EXPERTS:(ch + 1) * EXPERTS], h32[:, kt, ch * CH:(ch + 1) * CH],
                                       gw[:, kt, :], start=(kt == 0), stop=(kt == KT - 1))
                mm.then_inc(gate_ps, 1)

            def biases(Tn, sn):
                pe.wait_ge(comb_ready, Tn + 1)
                for ch in range(NCH):
                    mm = pe.transpose(GATE[0:EXPERTS, ch * CH:(ch + 1) * CH], comb[sn % 2][:, ch, :], ident[:, :])
                mm.then_inc(combT_ps, 1)
                pe.wait_ge(combT_ready, Tn + 1)
                for j in range(2):
                    after(pe, acc_ready, Tn * 2 + j - 1)
                    for i in range(2):
                        ch = 2 * j + i
                        mm = pe.matmul(BIAS[j][:, i * D:(i + 1) * D], combT[:, ch * CH:(ch + 1) * CH], eb[:, :],
                                       start=True, stop=True)
                    mm.then_inc(bias_ps, 1)

            def group(T, s):
                if exists(T):
                    pe.wait_ge(h_lo_ready, T * 2 + 2)
                    y_chunk(T, s, 0)
                if exists(T + 1):
                    transpose_h(T + 1)
                if exists(T):
                    y_chunk(T, s, 1)
                if exists(T + 1):
                    gate(T + 1)
                if exists(T):
                    y_chunk(T, s, 2)
                    y_chunk(T, s, 3)
                if exists(T + 1):
                    biases(T + 1, s + 1)

            expert_groups(pe, group)

        @block.vector
        def _(dve):
            dve.wait_ge(hi_split, 1)
            dve.tensor_tensor(wide(ew_lo), wide(ew_raw), wide(ew_hi).bitcast(F32), ALU.subtract).then_inc(lo_split, 1)
            dve.wait_ge(fills, 1 + EXPERTS)

            def add_chunk(T, s, ch):
                for e in range(EXPERTS):
                    n = ch * EXPERTS + e
                    if e % 2 == 0:
                        dve.wait_ge(y_ps, T * (NCH * YB) + ch * YB + e // 2 + 1)
                    if n == 0:
                        dve.wait_ge(acc_ready, T * 2 + 2)
                    if e:
                        dve.wait_ge(y_added, T * ADDS + n)
                    a = acc[s % 2][:, ch, :]
                    dve.scalar_tensor_tensor(a, Y[e // 2][:, (e % 2) * D:(e % 2 + 1) * D], comb[s % 2][:, ch, e:e + 1], a,
                                             ALU.mult, ALU.add).then_inc(y_added, 1)

            def ln(Tn, xs):
                dve.wait_ge(x1_loaded[xs], (Tn - xs) * (16 // GPB) + 16)
                for ch in range(NCH):
                    dve.bn_stats(stats[:, ch, :], x1[xs][:, ch, :]).then_inc(ln_step, 1)
                dve.wait_ge(ln_step, Tn * 8 + NCH)
                dve.sem_inc(stats_seen)
                for ch in range(NCH):
                    dve.bn_aggr(mean_var[:, ch, :], stats[:, ch, :]).then_inc(ln_step, 1)
                dve.wait_ge(ln_step, Tn * 8 + 8)
                dve.tensor_scalar(var_eps[:, :].unsqueeze(2), mean_var[:, :, 1:2], LN_EPS, None, ALU.add)\
                   .then_inc(var_ready, 1)
                dve.wait_ge(rstd_ready, Tn + 1)
                for ch in range(NCH):
                    ins = dve.tensor_scalar(xn[:, ch, :], x1[xs][:, ch, :], mean_var[:, ch, 0:1], rstd[:, ch:ch + 1],
                                            ALU.subtract, ALU.mult)
                ins.then_inc(xn_ready, 1)

            def h_low(Tn, sn):
                for kt in range(KT):
                    dve.wait_ge(h_hi_ready, Tn * 2 + kt + 1)
                    dve.tensor_tensor(h_lo[sn][:, kt, :], h32[:, kt, :], h_hi[sn][:, kt, :].bitcast(F32), ALU.subtract)\
                       .then_inc(h_lo_ready, 1)

            def route(Tn, sn):
                count = [0]

                def counted(ins):
                    count[0] += 1
                    ins.then_inc(route_step, 1)
                    dve.wait_ge(route_step, Tn * ROUTE + count[0])

                def per_expert(t):
                    return t.unsqueeze(2).to_broadcast([128, NCH, EXPERTS])

                rank_all = rank[:, :].unsqueeze(1).to_broadcast([128, NCH, EXPERTS])
                s_, p_, f1, f2, t_ = (t[:, :, :] for t in (sc, p, first, second, tmp))
                dve.wait_ge(gate_ps, Tn + 1)
                counted(dve.tensor_tensor(s_, GATE[:, 0:NCH * EXPERTS].rearrange("p (c e) -> p c e", e=EXPERTS),
                                          gbias[:, :].unsqueeze(1).to_broadcast([128, NCH, EXPERTS]), ALU.add))
                counted(dve.tensor_scalar(s_, s_, SCORE_EPS, None, ALU.max))
                counted(dve.tensor_reduce(red[:, 0, :], s_, AX_X, ALU.max))
                dve.tensor_tensor(s_, s_, per_expert(red[:, 0, :]), ALU.subtract).then_inc(route_exp_in, 1)
                dve.wait_ge(route_exp, Tn + 1)
                counted(dve.tensor_reduce(red[:, 1, :], p_, AX_X, ALU.add))
                counted(dve.reciprocal(red[:, 2, :], red[:, 1, :]))
                counted(dve.tensor_tensor(p_, p_, per_expert(red[:, 2, :]), ALU.mult))
                counted(dve.tensor_reduce(red[:, 3, :], p_, AX_X, ALU.max))
                counted(dve.tensor_tensor(f1, p_, per_expert(red[:, 3, :]), ALU.is_equal))
                counted(dve.tensor_tensor(f1, f1, rank_all, ALU.mult))
                counted(dve.tensor_reduce(red[:, 4, :], f1, AX_X, ALU.max))
                counted(dve.tensor_tensor(f1, f1, per_expert(red[:, 4, :]), ALU.is_equal))
                counted(dve.scalar_tensor_tensor(t_, f1, -2.0, p_, ALU.mult, ALU.add))
                counted(dve.tensor_reduce(red[:, 5, :], t_, AX_X, ALU.max))
                counted(dve.tensor_tensor(f2, t_, per_expert(red[:, 5, :]), ALU.is_equal))
                counted(dve.tensor_tensor(f2, f2, rank_all, ALU.mult))
                counted(dve.tensor_reduce(red[:, 6, :], f2, AX_X, ALU.max))
                counted(dve.tensor_tensor(f2, f2, per_expert(red[:, 6, :]), ALU.is_equal))
                counted(dve.tensor_tensor(f1, f1, f2, ALU.add))
                counted(dve.scalar_tensor_tensor(t_, p_, W_THRES, f1, ALU.max, ALU.mult))
                counted(dve.tensor_reduce(red[:, 7, :], t_, AX_X, ALU.add))
                assert count[0] == ROUTE
                dve.reciprocal(red[:, 0, :], red[:, 7, :]).then_inc(total_ready, 1)
                dve.wait_ge(total_ready, Tn + 1)
                dve.scalar_tensor_tensor(comb[sn][:, :, :], t_, 1.0 / TOP_K, per_expert(red[:, 0, :]), ALU.mult, ALU.mult)\
                   .then_inc(comb_ready, 1)

            def combT_out(Tn):
                dve.wait_ge(combT_ps, Tn + 1)
                dve.tensor_copy(combT[:, :], GATE[0:EXPERTS, :]).then_inc(combT_ready, 1)

            def group(T, s):
                if exists(T + 1):
                    ln(T + 1, (s + 1) % GPB)
                if exists(T):
                    add_chunk(T, s, 0)
                if exists(T + 1):
                    h_low(T + 1, (s + 1) % 2)
                if exists(T):
                    add_chunk(T, s, 1)
                if exists(T + 1):
                    route(T + 1, (s + 1) % 2)
                if exists(T):
                    add_chunk(T, s, 2)
                    add_chunk(T, s, 3)
                if exists(T + 1):
                    combT_out(T + 1)

            expert_groups(dve, group)


_INS = ["L0_attn_x", "L0_attn_Wq", "L0_attn_Wk", "L0_attn_Wv", "L0_attn_Wo", "L0_attn_Wa", "L0_attn_ba",
        "L0_ffn_gate_W", "L0_ffn_gate_b", "L0_ffn_expert_W", "L0_ffn_expert_b", "L0_c", "L0_wmod"]
_OUTS = [((BATCH, SEQ, D), "float32")]


def kernel(**inputs):
    import numpy as _np
    import concourse.bacc as _bacc
    from concourse import mybir as _mybir
    from concourse.bass_utils import run_bass_kernel_spmd as _run

    nc = _bacc.Bacc("TRN2", target_bir_lowering=False, num_devices=1)
    arrays, args = {}, []
    for name in _INS:
        a = _np.ascontiguousarray(inputs[name])
        arrays[f"in_{name}_dram"] = a
        args.append(nc.dram_tensor(f"in_{name}_dram", a.shape, _mybir.dt.from_np(a.dtype), kind="ExternalInput").ap())
    for i, (shape, dtype) in enumerate(_OUTS):
        dt = _mybir.dt.from_np(_np.dtype(dtype))
        args.append(nc.dram_tensor(f"out_{i}_dram", shape, dt, kind="ExternalOutput").ap())
    adaln_block(nc, *args)
    r = _run(nc, [arrays], core_ids=[0])
    got = tuple(r.results[0][f"out_{i}_dram"] for i in range(len(_OUTS)))
    return got[0]
```

```python
import concourse.bass as bass
from concourse import mybir
from contextlib import ExitStack

F32 = mybir.dt.float32
F32R = mybir.dt.float32r
ALU = mybir.AluOpType
ACT = mybir.ActivationFunctionType
AX_X = mybir.AxisListType.X

BATCH, SEQ, D = 8, 2048, 256
HEADS, DH = 16, 64
P_DIM = HEADS * DH
EXPERTS = 8
LN_EPS = 1e-5
DEN_EPS = 1e-6
DECAY_BIAS_SHIFT = 2.0
SCORE_EPS, W_THRES = 1e-4, 0.1
TOP_K = 2
GATE_FLOOR = 0.25
BIG = 3.0e38

CH = 128
NCH = 4
GT = CH * NCH
NG = BATCH * SEQ // GT
GPB = SEQ // GT
KT = D // 128
PAIRS = HEADS // 2
PT = P_DIM // 128
VW = DH + 1
LO = 32
ROWS = LO + HEADS


def after(eng, sem, count):
    if isinstance(count, int) and count <= 0:
        return
    eng.wait_ge(sem, count)


def exists(T):
    return not isinstance(T, int) or 0 <= T < NG


def unit(T, u, ahead):
    Tn, p = (T, u + ahead) if u + ahead < PAIRS else (T + 1, u + ahead - PAIRS)
    return Tn, p, Tn * PAIRS + p


DENSE_JOBS = {(0, 0): ("wo", -1, 0), (0, 1): ("wo", -1, 1), (1, 0): ("v", 0, 4), (1, 1): ("v", 0, 5),
              (2, 0): ("v", 0, 6), (2, 1): ("v", 0, 7), (3, 1): ("h", 1, 0), (4, 0): ("h", 1, 1), (4, 1): ("z", 1, 0),
              (5, 0): ("a", 1, 0), (5, 1): ("v", 1, 0), (6, 0): ("v", 1, 1), (6, 1): ("v", 1, 2), (7, 0): ("v", 1, 3)}


def dense_at(T, s, u, part):
    job, ahead, k = DENSE_JOBS.get((u, part), (None, 0, 0))
    return (job, T + ahead, s if ahead == 0 else 1 - s, k) if exists(T + ahead) else (None, T, s, k)


def batch_row(T):
    b = T // GPB if isinstance(T, int) else T >> (GPB.bit_length() - 1)
    return b if isinstance(b, int) else b.with_bounds(min_val=0, max_val=BATCH - 1)


def attention_steps(eng, step):
    for T in (-1, 0, 1):
        for u in range(PAIRS):
            step(T, T % 2, u)
    with eng.Fori(1, NG // 2 - 1) as i:
        for s in range(2):
            for u in range(PAIRS):
                step(i * 2 + s, s, u)
    for T in (NG - 2, NG - 1):
        for u in range(PAIRS):
            step(T, T % 2, u)
    step(NG, 0, 0)


def expert_groups(eng, group):
    group(-2, GPB - 2)
    group(-1, GPB - 1)
    for T in range(GPB):
        group(T, T)
    with eng.Fori(1, BATCH - 1) as b:
        for s in range(GPB):
            group(b * GPB + s, s)
    for T in range(NG - GPB, NG):
        group(T, T % GPB)


def adaln_block(nc, x, Wq, Wk, Wv, Wo, Wa, ba, gate_W, gate_b, expert_W, expert_b, c, wmod, out):
    tokens = x.rearrange("b (g c p) d -> (b g) p c d", p=CH, c=NCH)
    out_tokens = out.rearrange("b (g c p) d -> (b g) p c d", p=CH, c=NCH)
    x1_dram = nc.dram_tensor("x1_dram", [NG, CH, NCH, D], F32, kind="Internal").ap()
    gates_dram = nc.dram_tensor("gates_dram", [2, BATCH, D], F32, kind="Internal").ap()

    with ExitStack() as keep:
        mod = keep.enter_context(nc.sbuf_tensor("mod", [128, 4, KT, BATCH], F32))
        ident = keep.enter_context(nc.sbuf_tensor("ident", [128, 128], F32))
        bank = [keep.enter_context(nc.psum_tensor(f"bank{i}", [128, 512], F32)) for i in range(8)]
        attention_phase(nc, tokens, Wq, Wk, Wv, Wo, Wa, ba, c, wmod, x1_dram, gates_dram, mod, ident, bank)
        expert_phase(nc, x1_dram, gates_dram, gate_W, gate_b, expert_W, expert_b, out_tokens, mod, ident, bank)


def attention_phase(nc, tokens, Wq, Wk, Wv, Wo, Wa, ba, c, wmod, x1_dram, gates_dram, mod, ident, bank):
    with ExitStack() as ctx:
        def sb(name, shape, dt=F32):
            return ctx.enter_context(nc.sbuf_tensor(name, shape, dt))

        def sem(name):
            return ctx.enter_context(nc.semaphore(name))

        w_names = ["wq", "wk", "wv"]
        w_hi = {n: sb(n + "_hi", [128, KT, P_DIM], F32R) for n in w_names}
        w_lo = {n: sb(n + "_lo", [128, KT, P_DIM], F32R) for n in w_names}
        wo_hi, wo_lo = (sb("wo_" + h, [128, PT, D], F32R) for h in ("hi", "lo"))
        wa = sb("wa", [128, KT, HEADS])
        ba2 = sb("ba2", [128, HEADS])
        ga = sb("ga", [128, BATCH, D])
        eye4 = sb("eye4", [128, NCH, CH])
        head_sel = sb("head_sel", [ROWS, HEADS, DH], F32R)
        head_sel32 = sb("head_sel32", [ROWS, HEADS])
        zero_row = sb("zero_row", [HEADS, CH])
        bound = sb("bound", [128, NG // 2])
        neg_bound = sb("neg_bound", [128, NG // 2])
        half_neg = sb("half_neg", [128, NCH])
        silu_t = sb("silu_t", [128, KT, BATCH])
        x_sb = sb("x_sb", [128, 2, NCH, D])
        xn = sb("xn", [128, NCH, D])
        stats = sb("stats", [128, NCH, 6])
        mean_var = sb("mean_var", [128, NCH, 2])
        var_eps = sb("var_eps", [128, NCH])
        rstd = sb("rstd", [128, NCH])
        h32 = sb("h32", [128, KT, GT])
        h_hi = [sb(f"h_hi{i}", [128, KT, GT], F32R) for i in range(2)]
        h_lo = [sb(f"h_lo{i}", [128, KT, GT], F32R) for i in range(2)]
        v_sb = sb("v_sb", [128, NCH, HEADS, VW])
        a_tok = sb("a_tok", [128, NCH, HEADS])
        a_row = sb("a_row", [HEADS, GT])
        lam_row = sb("lam_row", [HEADS, GT])
        az = [sb(f"az{i}", [ROWS, NCH, CH], F32R) for i in range(2)]
        lam = [sb(f"lam{i}", [ROWS, NCH, CH], F32R) for i in range(2)]
        oT_hi = sb("oT_hi", [128, PT, GT], F32R)
        oT_lo = sb("oT_lo", [128, PT, GT], F32R)
        q_sb = sb("q_sb", [128, GT])
        k_sb = sb("k_sb", [128, GT])
        qs_sb = sb("qs_sb", [128, 2, GT])
        lam_end = sb("lam_end", [128, 2, NCH])
        decay = sb("decay", [128, 2, GT])
        p_sb = sb("p_sb", [128, 2, 2, GT])
        kd_sb = sb("kd_sb", [128, NCH, 128])
        s_mid = sb("s_mid", [128, 2, NCH - 1, 2 * VW])
        carry = sb("carry", [128, 2, PAIRS, 2 * VW])
        den = sb("den", [128, 2, NCH])
        rden = sb("rden", [128, 2, NCH])
        o_sb = sb("o_sb", [128, NCH, 128])
        c_sb, c_e = h32[0:BATCH, 0, 0:D], h32[0:BATCH, 0, D:2 * D]
        gates = h32[0:BATCH, 1, :].rearrange("b (s d) -> b s d", s=2)
        gates_sign = o_sb[0:BATCH, :, :].rearrange("b c n -> b (c n)").rearrange("b (s d) -> b s d", s=2)

        Q, K, SA, SB, KTR, NUM0, NUM1, DENSE = bank
        S = [SA, SB]
        U = [KTR[:, ch * 2 * VW:(ch + 1) * 2 * VW] for ch in range(NCH - 1)] + [NUM0[:, 0:2 * VW]]
        NUM = [NUM0, NUM1]

        wmod_loaded = sem("wmod_loaded"); small_loaded = sem("small_loaded"); w_loaded = [sem(f"w_loaded{i}") for i in range(2)]
        hi_split = sem("hi_split"); lo_split = sem("lo_split")
        consts_ready = sem("consts_ready"); fills = sem("fills")
        silu_e = sem("silu_e"); silu_step = sem("silu_step"); silu_ps = sem("silu_ps"); siluT_ready = sem("siluT_ready")
        mod_ps = sem("mod_ps"); mod_ready = sem("mod_ready"); gates_step = sem("gates_step")
        gates_stored = sem("gates_stored"); ga_loaded = sem("ga_loaded"); ba_ready = sem("ba_ready")
        x_loaded = [sem(f"x_loaded{i}") for i in range(2)]; x1_stored = sem("x1_stored")
        ln_step = sem("ln_step"); var_ready = sem("var_ready"); rstd_ready = sem("rstd_ready"); xn_ready = sem("xn_ready")
        hT_ps = sem("hT_ps"); h32_ready = sem("h32_ready"); h_hi_ready = sem("h_hi_ready"); h_lo_ready = sem("h_lo_ready")
        z_ps = sem("z_ps"); zb_ready = sem("zb_ready"); z_exp = sem("z_exp"); a_step = sem("a_step"); a_ready = sem("a_ready")
        arow_ps = sem("arow_ps"); arow_ready = sem("arow_ready"); row_step = sem("row_step"); rows_ready = sem("rows_ready")
        v_ps = sem("v_ps"); v_ready = sem("v_ready")
        wo_ps = sem("wo_ps"); wo_scaled = sem("wo_scaled"); x1_ready = sem("x1_ready")
        stats_seen = sem("stats_seen")
        q_ps = sem("q_ps"); q_exp = sem("q_exp"); q_neg = sem("q_neg"); q_ready = sem("q_ready")
        k_ps = sem("k_ps"); k_exp = sem("k_exp"); k_neg = sem("k_neg"); k_ready = sem("k_ready")
        abc_ps = sem("abc_ps"); decay_ready = sem("decay_ready")
        lam_ps = sem("lam_ps"); qs_ready = sem("qs_ready"); lam_end_ready = sem("lam_end_ready")
        s_ps = sem("s_ps"); p_ready = sem("p_ready")
        ktr_ps = sem("ktr_ps"); kd_ready = sem("kd_ready")
        u_ps = sem("u_ps"); state_step = sem("state_step"); entry_clamped = sem("entry_clamped")
        num_ps = sem("num_ps"); den_step = sem("den_step"); o_ready = sem("o_ready")
        oT_ps = sem("oT_ps"); oT_hi_ready = sem("oT_hi_ready"); oT_lo_ready = sem("oT_lo_ready")

        stage = [p_sb[:, :, :, :].rearrange("p a h n -> p (a h n)"), x_sb[:, :, :, :].rearrange("p a c d -> p (a c d)")]
        wmod_half = [s[:, 0:KT * 3 * D].rearrange("p (k n) -> p k n", k=KT) for s in stage]
        big_w = [(Wq.rearrange("(k p) n -> p k n", p=128), w_hi["wq"], w_lo["wq"]),
                 (Wk.rearrange("(k p) n -> p k n", p=128), w_hi["wk"], w_lo["wk"]),
                 (Wv.rearrange("(k p) n -> p k n", p=128), w_hi["wv"], w_lo["wv"]),
                 (Wo.rearrange("(k p) n -> p k n", p=128), wo_hi, wo_lo)]
        SMALL = 3
        MOD_A = 4
        SECTION = [0, 1, 3, 4]

        def flat(t):
            return t[:, :, :].rearrange("p k n -> p (k n)")

        block = ctx.enter_context(nc.Block())

        @block.sync
        def _(sp):
            wm = wmod.rearrange("(k p) n -> p k n", p=128)
            for half in range(2):
                sp.dma_start(wmod_half[half], wm[:, :, half * 3 * D:(half + 1) * 3 * D]).then_inc(wmod_loaded, 16)
            sp.dma_start(c_sb, c).then_inc(small_loaded, 16)
            sp.dma_start(ba2[:, :], ba.partition_broadcast(128)).then_inc(small_loaded, 16)
            sp.dma_start(wa[:, :, :], Wa.rearrange("(k p) n -> p k n", p=128)).then_inc(small_loaded, 16)
            for n, (src, _, _) in enumerate(big_w):
                if n < 2:
                    sp.wait_ge(mod_ps, 1)
                else:
                    sp.wait_ge(lo_split, n - 1)
                dst = stage[n % 2].rearrange("p (k n) -> p k n", k=src.shape[1])
                sp.dma_start(dst, src).then_inc(w_loaded[n % 2], 16)
            sp.wait_ge(gates_step, 4)
            sp.dma_start(gates_dram.rearrange("s b d -> b s d"), gates).then_inc(gates_stored, 16)
            sp.wait_ge(gates_stored, 16)
            sp.dma_start(ga[:, :, :], gates_dram[0].partition_broadcast(128)).then_inc(ga_loaded, 16)
            sp.wait_ge(lo_split, len(big_w))

            def step(T, s, u):
                if u != 0:
                    return
                if exists(T - 1):
                    after(sp, x1_ready, T * 2)
                    sp.dma_start(x1_dram[bass.ds(T - 1, 1)].rearrange("g p c d -> (g p) c d"),
                                 x_sb[:, 1 - s, :, :]).then_inc(x1_stored, 16)
                if exists(T + 1):
                    after(sp, x1_stored, T * 16)
                    sp.dma_start(x_sb[:, 1 - s, :, :],
                                 tokens[bass.ds(T + 1, 1)].rearrange("g p c d -> (g p) c d")).then_inc(x_loaded[1 - s], 16)

            attention_steps(sp, step)
            sp.wait_ge(x1_stored, 16 * NG)

        @block.gpsimd
        def _(pool):
            pool.memset(ident[:, :], 0.0).then_inc(fills, 1)
            pool.memset(eye4[:, :, :], 0.0).then_inc(fills, 1)
            pool.memset(head_sel32[:, :], 0.0).then_inc(fills, 1)
            pool.memset(bound[:, :], 0.0).then_inc(fills, 1)
            pool.memset(neg_bound[:, :], 0.0).then_inc(fills, 1)
            pool.memset(half_neg[:, :], -0.5).then_inc(consts_ready, 1)
            pool.memset(zero_row[:, :], 0.0).then_inc(consts_ready, 1)
            pool.memset(carry[:, :, :, :], 0.0).then_inc(consts_ready, 1)
            pool.memset(s_mid[:, :, :, :], 0.0).then_inc(consts_ready, 1)
            pool.memset(v_sb[:, :, :, DH:VW], 1.0).then_inc(consts_ready, 1)
            pool.wait_ge(fills, 5)
            pool.memset(bound[:, :].rearrange("p (r e) -> p r e", e=2)[:, :, 1:2], BIG).then_inc(consts_ready, 1)
            pool.memset(neg_bound[:, :].rearrange("p (r e) -> p r e", e=2)[:, :, 1:2], -BIG).then_inc(consts_ready, 1)
            pool.affine_select(out=ident[:, :], in_=ident[:, :], compare_op=ALU.not_equal, fill=1.0, base=0,
                               pattern=[[-1, 128]], channel_multiplier=1).then_inc(consts_ready, 1)
            pool.affine_select(out=eye4[:, :, :], in_=eye4[:, :, :], compare_op=ALU.not_equal, fill=1.0, base=0,
                               pattern=[[0, NCH], [-1, CH]], channel_multiplier=1).then_inc(consts_ready, 1)
            pool.affine_select(out=head_sel32[:, :], in_=head_sel32[:, :], compare_op=ALU.not_equal, fill=1.0,
                               base=0, pattern=[[-1, HEADS]], channel_multiplier=1).then_inc(fills, 1)
            pool.wait_ge(fills, 6)
            pool.affine_select(out=head_sel32[:, :], in_=head_sel32[:, :], compare_op=ALU.not_equal, fill=1.0,
                               base=-LO, pattern=[[-1, HEADS]], channel_multiplier=1).then_inc(consts_ready, 1)

            def step(T, s, u):
                if u == 0 and exists(T - 1):
                    for j in range(2):
                        after(pool, wo_scaled, (T - 1) * 2 + j + 1)
                        rows = x_sb[:, 1 - s, 2 * j:2 * j + 2, :]
                        pool.tensor_tensor(rows, rows, xn[:, 2 * j:2 * j + 2, :], ALU.add).then_inc(x1_ready, 1)
                if u == 2 and exists(T + 1):
                    after(pool, var_ready, T + 2)
                    pool.tensor_tensor(rstd[:, :], var_eps[:, :], half_neg[:, :], ALU.pow).then_inc(rstd_ready, 1)
            attention_steps(pool, step)

        @block.scalar
        def _(act):
            act.wait_ge(small_loaded, 16 * SMALL)
            act.activation(c_e, c_sb, ACT.Exp, scale=-1.0).then_inc(silu_e, 1)
            for n, (_, hi, _) in enumerate(big_w):
                act.wait_ge(w_loaded[n % 2], 16 * (n // 2 + 1))
                act.activation(flat(hi), stage[n % 2], ACT.Copy).then_inc(hi_split, 1)

            def v_out(T, half, ch):
                act.wait_ge(v_ps, T * 8 + half * NCH + ch + 1)
                hs = half * (HEADS // 2)
                act.activation(v_sb[:, ch, hs:hs + HEADS // 2, 0:DH],
                               DENSE[:, :].rearrange("p (h d) -> p h d", d=DH), ACT.Copy).then_inc(v_ready, 1)

            def h_out(T, s, kt):
                act.wait_ge(hT_ps, T * 2 + kt + 1)
                if kt == 0:
                    act.wait_ge(mod_ready, 2)
                    if isinstance(T, int) and T == 0:
                        act.wait_ge(gates_stored, 16)
                b = batch_row(T)
                act.activation(h32[:, kt, :], DENSE[:, :], ACT.Identity, bias=mod[:, 0, kt, bass.ds(b, 1)],
                               scale=mod[:, 1, kt, bass.ds(b, 1)]).then_inc(h32_ready, 1)
                act.wait_ge(h32_ready, T * 2 + kt + 1)
                act.activation(h_hi[s][:, kt, :], h32[:, kt, :], ACT.Copy).then_inc(h_hi_ready, 1)

            def dense_out(T, s, u, part):
                job, of, so, k = dense_at(T, s, u, part)
                if job == "v":
                    v_out(of, k // NCH, k % NCH)
                if job == "h":
                    h_out(of, so, k)

            def step(T, s, u):
                Ta, _, a = unit(T, u, 2)
                if exists(Ta):
                    act.wait_ge(q_ps, a + 1)
                    after(act, qs_ready, a)
                    act.activation(q_sb[:, :], Q[:, :], ACT.Relu, scale=-1.0).then_inc(q_neg, 1)
                    act.wait_ge(q_neg, a + 1)
                    act.activation(q_sb[:, :], q_sb[:, :], ACT.Exp, scale=-1.0).then_inc(q_exp, 1)
                dense_out(T, s, u, 0)
                if exists(Ta):
                    act.wait_ge(k_ps, a + 1)
                    act.activation(k_sb[:, :], K[:, :], ACT.Relu, scale=-1.0).then_inc(k_neg, 1)
                    act.wait_ge(k_neg, a + 1)
                    act.activation(k_sb[:, :], k_sb[:, :], ACT.Exp, scale=-1.0).then_inc(k_exp, 1)
                dense_out(T, s, u, 1)
                if exists(T):
                    n = T * PAIRS + u
                    act.wait_ge(oT_ps, n + 1)
                    act.activation(oT_hi[:, u, :], NUM1[:, :], ACT.Copy).then_inc(oT_hi_ready, 1)
                if u == 4 and exists(T + 1):
                    act.wait_ge(zb_ready, T + 2)
                    act.activation(a_tok[:, :, :], a_tok[:, :, :], ACT.Exp, scale=-1.0).then_inc(z_exp, 1)

            attention_steps(act, step)

        @block.tensor
        def _(pe):
            pe.wait_ge(consts_ready, 10)
            pe.wait_ge(silu_step, 3)
            for kt in range(KT):
                mm = pe.transpose(DENSE[:, kt * BATCH:(kt + 1) * BATCH], c_e[:, kt * 128:(kt + 1) * 128],
                                  ident[0:BATCH, 0:BATCH])
            mm.then_inc(silu_ps, 1)
            pe.wait_ge(siluT_ready, 1)
            pe.wait_ge(wmod_loaded, 32)
            for m, sec in enumerate(SECTION):
                for kt in range(KT):
                    col = (m * KT + kt) * BATCH
                    w = wmod_half[sec // 3][:, :, (sec % 3) * D + kt * 128:(sec % 3) * D + (kt + 1) * 128]
                    for k2 in range(KT):
                        pe.matmul(SA[:, col:col + BATCH], w[:, k2, :], silu_t[:, k2, :],
                                  start=(k2 == 0), stop=(k2 == KT - 1))
            for g in range(2):
                for k2 in range(KT):
                    mm = pe.matmul(SB[0:BATCH, g * D:(g + 1) * D], silu_t[:, k2, :],
                                   wmod_half[g][:, k2, 2 * D:3 * D], start=(k2 == 0), stop=(k2 == KT - 1))
            mm.then_inc(mod_ps, 1)
            pe.wait_ge(mod_ready, 3)
            pe.wait_ge(gates_step, 3)

            def three_pass(dst, pairs):
                last = len(pairs) - 1
                for n, (s_hi, s_lo, m_hi, m_lo) in enumerate(pairs):
                    pe.matmul(dst, s_hi, m_hi, start=(n == 0), stop=False)
                    pe.matmul(dst, s_hi, m_lo, start=False, stop=False)
                    mm = pe.matmul(dst, s_lo, m_hi, start=False, stop=(n == last))
                return mm

            def project(Tn, sn, p, w, dst, done):
                h, l = h_hi[sn], h_lo[sn]
                cols = slice(p * 128, (p + 1) * 128)
                three_pass(dst[:, :], [(w_hi[w][:, kt, cols], w_lo[w][:, kt, cols], h[:, kt, :], l[:, kt, :])
                                       for kt in range(KT)]).then_inc(done, 1)

            def h_job(T, kt):
                if kt == 0:
                    after(pe, v_ready, (T - 1) * 8 + 8)
                    pe.wait_ge(xn_ready, T + 1)
                else:
                    pe.wait_ge(h32_ready, T * 2 + 1)
                for ch in range(NCH):
                    mm = pe.transpose(DENSE[:, ch * CH:(ch + 1) * CH], xn[:, ch, kt * 128:(kt + 1) * 128], ident[:, :])
                mm.then_inc(hT_ps, 1)

            def z_job(T):
                pe.wait_ge(h32_ready, T * 2 + 2)
                for ch in range(NCH):
                    for kt in range(KT):
                        mm = pe.matmul(DENSE[:, ch * HEADS:(ch + 1) * HEADS], h32[:, kt, ch * CH:(ch + 1) * CH],
                                       wa[:, kt, :], start=(kt == 0), stop=(kt == KT - 1))
                mm.then_inc(z_ps, 1)

            def arow_job(T):
                pe.wait_ge(a_ready, T + 1)
                for ch in range(NCH):
                    mm = pe.transpose(DENSE[0:HEADS, ch * CH:(ch + 1) * CH], a_tok[:, ch, :], ident[:, :])
                mm.then_inc(arow_ps, 1)

            def v_job(T, s, half, ch):
                n = T * 8 + half * NCH + ch
                if half == 0 and ch == 0:
                    pe.wait_ge(arow_ready, T + 1)
                    after(pe, num_ps, ((T - 1) * PAIRS + PAIRS // 2) * 2)
                elif half == 1 and ch == 0:
                    after(pe, wo_scaled, T * 2)
                    after(pe, v_ready, n)
                else:
                    pe.wait_ge(v_ready, n)
                pe.wait_ge(h_lo_ready, T * 2 + 2)
                tok = slice(ch * CH, (ch + 1) * CH)
                cols = slice(half * 512, (half + 1) * 512)
                three_pass(DENSE[:, :], [(h_hi[s][:, kt, tok], h_lo[s][:, kt, tok], w_hi["wv"][:, kt, cols],
                                          w_lo["wv"][:, kt, cols]) for kt in range(KT)]).then_inc(v_ps, 1)

            def wo_job(T, j):
                if j == 0:
                    after(pe, v_ready, T * 8 + (12 if exists(T + 1) else 8))
                    pe.wait_ge(oT_lo_ready, T * PAIRS + PAIRS)
                else:
                    pe.wait_ge(wo_scaled, T * 2 + 1)
                for i in range(2):
                    tok = slice((2 * j + i) * CH, (2 * j + i + 1) * CH)
                    mm = three_pass(DENSE[:, i * D:(i + 1) * D],
                                    [(oT_hi[:, pt, tok], oT_lo[:, pt, tok], wo_hi[:, pt, :], wo_lo[:, pt, :])
                                     for pt in range(PT)])
                mm.then_inc(wo_ps, 1)

            def dense_job(T, s, u, part):
                job, of, so, k = dense_at(T, s, u, part)
                if job == "wo":
                    wo_job(of, k)
                if job == "v":
                    v_job(of, so, k // NCH, k % NCH)
                if job == "h":
                    h_job(of, k)
                if job == "z":
                    z_job(of)
                if job == "a":
                    arow_job(of)

            def step(T, s, u):
                n = T * PAIRS + u
                Tb, pb, b = unit(T, u, 1)
                Ta, pa, a = unit(T, u, 2)
                sa = s if u + 2 < PAIRS else 1 - s
                if exists(Tb):
                    pe.wait_ge(q_ready, b + 1)
                    pe.wait_ge(k_ready, b + 1)
                    pe.wait_ge(decay_ready, 2 * b + 2)
                    for ch in range(NCH):
                        tok = slice(ch * CH, (ch + 1) * CH)
                        for hd in range(2):
                            rows = slice(hd * DH, (hd + 1) * DH)
                            mm = pe.matmul(S[hd][:, tok], k_sb[rows, tok], q_sb[rows, tok], start=True, stop=True)
                            if ch == NCH - 1:
                                mm.then_inc(s_ps, 1)
                    after(pe, state_step, b * 8 - 2)
                    for ch in range(NCH):
                        mm = pe.transpose(KTR[:, ch * CH:(ch + 1) * CH], k_sb[:, ch * CH:(ch + 1) * CH], ident[:, :])
                    mm.then_inc(ktr_ps, 1)
                if exists(Ta):
                    pe.wait_ge(h_lo_ready, Ta * 2 + 2)
                    after(pe, qs_ready, a)
                    project(Ta, sa, pa, "wq", Q, q_ps)
                dense_job(T, s, u, 0)
                if exists(Ta):
                    pe.wait_ge(rows_ready, Ta + 1)
                    after(pe, p_ready, 2 * a)
                    for hd in range(2):
                        hcol = head_sel[:, 2 * pa + hd, 0:1]
                        pe.matmul(S[hd][:, :], hcol.to_broadcast([ROWS, 128]),
                                  az[sa][:, :, :].rearrange("r c i -> r (c i)"),
                                  start=True, stop=True).then_inc(abc_ps, 1)
                    after(pe, k_ready, a)
                    project(Ta, sa, pa, "wk", K, k_ps)

                def states(chunks):
                    for ch in chunks:
                        mm = pe.matmul(U[ch], kd_sb[:, ch, :], v_sb[:, ch, 2 * pb:2 * pb + 2, :], start=True, stop=True)
                    mm.then_inc(u_ps, 1)

                if exists(Tb):
                    pe.wait_ge(kd_ready, b + 1)
                    pe.wait_ge(v_ready, Tb * 8 + (NCH if pb < PAIRS // 2 else 2 * NCH))
                    states(range(NCH - 1))
                if exists(T):
                    pe.wait_ge(qs_ready, n + 1)
                    pe.wait_ge(p_ready, 2 * n + 2)
                    pe.wait_ge(state_step, n * 8 + 8)
                    after(pe, oT_lo_ready, n)
                    for ch in range(NCH):
                        tok = slice(ch * CH, (ch + 1) * CH)
                        state = carry[:, s, u, :] if ch == 0 else s_mid[:, u % 2, ch - 1, :]
                        at = (ch % 2) * 2 * VW
                        num = NUM[ch // 2]
                        pe.matmul(num[:, at:at + 2 * VW], qs_sb[:, u % 2, tok], state, start=True, stop=False)
                        for hd in range(2):
                            mm = pe.matmul(num[:, at + hd * VW:at + (hd + 1) * VW], p_sb[:, u % 2, hd, tok],
                                           v_sb[:, ch, 2 * u + hd, :], start=False, stop=(hd == 1))
                        if ch % 2:
                            mm.then_inc(num_ps, 1)
                if exists(Ta):
                    pe.wait_ge(q_ready, a + 1)
                    pe.matmul(Q[:, :], head_sel[:, 2 * pa:2 * pa + 2, :].rearrange("r h d -> r (h d)"),
                              lam[sa][:, :, :].rearrange("r c i -> r (c i)"), start=True, stop=True).then_inc(lam_ps, 1)
                dense_job(T, s, u, 1)
                if exists(Tb):
                    after(pe, o_ready, 2 * b - 1)
                    states(range(NCH - 1, NCH))
                if exists(T):
                    pe.wait_ge(o_ready, 2 * n + 2)
                    for ch in range(NCH):
                        mm = pe.transpose(NUM1[:, ch * CH:(ch + 1) * CH], o_sb[:, ch, :], ident[:, :])
                    mm.then_inc(oT_ps, 1)

            attention_steps(pe, step)

        @block.vector
        def _(dve):
            dve.wait_ge(silu_e, 1)
            dve.tensor_scalar(c_e, c_e, 1.0, None, ALU.add).then_inc(silu_step, 1)
            dve.wait_ge(silu_step, 1)
            dve.reciprocal(c_e, c_e).then_inc(silu_step, 1)
            dve.wait_ge(silu_step, 2)
            dve.tensor_tensor(c_e, c_e, c_sb, ALU.mult).then_inc(silu_step, 1)
            dve.tensor_scalar(ba2[:, :], ba2[:, :], DECAY_BIAS_SHIFT, None, ALU.add).then_inc(ba_ready, 1)
            dve.wait_ge(silu_ps, 1)
            dve.tensor_copy(silu_t[:, :, :], DENSE[:, 0:KT * BATCH].rearrange("p (k b) -> p k b", b=BATCH))\
               .then_inc(siluT_ready, 1)
            dve.wait_ge(consts_ready, 10)
            dve.tensor_copy(head_sel[:, :, :], head_sel32[:, :].unsqueeze(2).to_broadcast([ROWS, HEADS, DH]))
            for t in (*az, *lam):
                dve.memset(t[:, :, :].bitcast(F32), 0.0)
            dve.wait_ge(mod_ps, 1)
            mods = SA[:, 0:MOD_A * KT * BATCH].rearrange("p (m k b) -> p m k b", k=KT, b=BATCH)
            for m in range(MOD_A):
                dve.tensor_scalar(mod[:, m, :, :], mods[:, m, :, :], float(m % 2), None, ALU.add)\
                   .then_inc(mod_ready, 1)
            g_ps = SB[0:BATCH, :].rearrange("b (s d) -> b s d", s=2)
            dve.tensor_scalar(gates_sign, g_ps, 0.0, 2.0, ALU.is_ge, ALU.mult).then_inc(gates_step, 1)
            dve.tensor_scalar(gates, g_ps, -1.0, None, ALU.mult).then_inc(gates_step, 1)
            dve.wait_ge(gates_step, 2)
            dve.scalar_tensor_tensor(gates, g_ps, GATE_FLOOR, gates, ALU.max, ALU.max).then_inc(gates_step, 1)
            dve.wait_ge(gates_step, 3)
            dve.scalar_tensor_tensor(gates, gates_sign, -1.0, gates, ALU.add, ALU.mult).then_inc(gates_step, 1)
            for n, (_, hi, lo) in enumerate(big_w):
                dve.wait_ge(hi_split, n + 1)
                dve.tensor_tensor(flat(lo), stage[n % 2], flat(hi).bitcast(F32), ALU.subtract).then_inc(lo_split, 1)

            def wo_out(T, s, j):
                b = batch_row(T)
                if j == 0 and isinstance(T, int) and T == 0:
                    dve.wait_ge(ga_loaded, 16)
                dve.wait_ge(wo_ps, T * 2 + j + 1)
                after(dve, x1_ready, T * 2)
                gb = ga[:, bass.ds(b, 1), :].to_broadcast([128, 2, D])
                dve.tensor_tensor(xn[:, 2 * j:2 * j + 2, :], DENSE[:, :].rearrange("p (c d) -> p c d", d=D), gb,
                                  ALU.mult).then_inc(wo_scaled, 1)

            def ln_stats(T, s):
                dve.wait_ge(x_loaded[s], T * 8 + 16 - 8 * s)
                for ch in range(NCH):
                    dve.bn_stats(stats[:, ch, :], x_sb[:, s, ch, :]).then_inc(ln_step, 1)
                dve.wait_ge(ln_step, T * 8 + NCH)
                dve.sem_inc(stats_seen)
                for ch in range(NCH):
                    dve.bn_aggr(mean_var[:, ch, :], stats[:, ch, :]).then_inc(ln_step, 1)
                dve.wait_ge(ln_step, T * 8 + 8)
                dve.tensor_scalar(var_eps[:, :].unsqueeze(2), mean_var[:, :, 1:2], LN_EPS, None, ALU.add)\
                   .then_inc(var_ready, 1)

            def ln_apply(T, s):
                dve.wait_ge(rstd_ready, T + 1)
                after(dve, x1_ready, T * 2 - 2)
                for ch in range(NCH):
                    ins = dve.tensor_scalar(xn[:, ch, :], x_sb[:, s, ch, :], mean_var[:, ch, 0:1], rstd[:, ch:ch + 1],
                                            ALU.subtract, ALU.mult)
                ins.then_inc(xn_ready, 1)

            def h_low(T, s, kt):
                dve.wait_ge(h_hi_ready, T * 2 + kt + 1)
                dve.tensor_tensor(h_lo[s][:, kt, :], h32[:, kt, :], h_hi[s][:, kt, :].bitcast(F32), ALU.subtract)\
                   .then_inc(h_lo_ready, 1)

            def z_out(T):
                dve.wait_ge(z_ps, T + 1)
                dve.wait_ge(ba_ready, 1)
                dve.tensor_tensor(a_tok[:, :, :], DENSE[:, 0:NCH * HEADS].rearrange("p (c h) -> p c h", h=HEADS),
                                  ba2[:, :].unsqueeze(1).to_broadcast([128, NCH, HEADS]), ALU.add).then_inc(zb_ready, 1)

            def sigmoid(T):
                dve.wait_ge(z_exp, T + 1)
                dve.tensor_scalar(a_tok[:, :, :], a_tok[:, :, :], 1.0, None, ALU.add).then_inc(a_step, 1)
                dve.wait_ge(a_step, T + 1)
                dve.reciprocal(a_tok[:, :, :], a_tok[:, :, :]).then_inc(a_ready, 1)

            def arow_out(T):
                dve.wait_ge(arow_ps, T + 1)
                dve.tensor_copy(a_row[:, :], DENSE[0:HEADS, :]).then_inc(arow_ready, 1)

            def decay_rows(T, s):
                dve.wait_ge(arow_ready, T + 1)
                for ch in range(NCH):
                    tok = slice(ch * CH, (ch + 1) * CH)
                    ins = dve.tensor_tensor_scan(lam_row[:, tok], a_row[:, tok], zero_row[:, :], 1.0, ALU.mult, ALU.add)
                ins.then_inc(row_step, 1)
                for dst, src in ((az[s], a_row), (lam[s], lam_row)):
                    if src is lam_row:
                        dve.wait_ge(row_step, T * 4 + 2)
                    hi = dst[0:HEADS, :, :].rearrange("r c i -> r (c i)")
                    dve.tensor_copy(hi, src[:, :]).then_inc(row_step, 1)
                    dve.wait_ge(row_step, T * 4 + (2 if src is a_row else 4))
                    lo = dve.tensor_tensor(dst[LO:ROWS, :, :].rearrange("r c i -> r (c i)"), src[:, :], hi.bitcast(F32),
                                           ALU.subtract)
                    lo.then_inc(row_step if src is a_row else rows_ready, 1)
                    if src is a_row:
                        dve.wait_ge(row_step, T * 4 + 3)
                        dve.memset(dst[:, :, 0:1].bitcast(F32), 0.0)

            def dense_out(T, s, u, part):
                job, of, so, k = dense_at(T, s, u, part)
                if job == "wo":
                    wo_out(of, so, k)
                if job == "z":
                    z_out(of)
                if job == "a":
                    arow_out(of)

            def chain(Tb, sb_, pb, b, chunks):
                entry = carry[:, sb_, pb, :]
                nb = pb % 2
                if 0 in chunks:
                    if sb_ == 0 and not (isinstance(Tb, int) and Tb == 0):
                        i = Tb >> 1
                        dve.wait_ge(state_step, (b - PAIRS + 1) * 8)
                        dve.tensor_scalar(entry, entry, bound[:, bass.ds(i, 1)], neg_bound[:, bass.ds(i, 1)],
                                          ALU.min, ALU.max).then_inc(entry_clamped, 1)
                        dve.wait_ge(entry_clamped, Tb * (PAIRS // 2) - PAIRS + pb + 1)
                    dve.wait_ge(lam_end_ready, b + 1)
                    dve.wait_ge(u_ps, 2 * b + 1)
                else:
                    dve.wait_ge(u_ps, 2 * b + 2)
                for ch in chunks:
                    src = entry if ch == 0 else s_mid[:, nb, ch - 1, :]
                    dst = s_mid[:, nb, ch, :] if ch < NCH - 1 else carry[:, 1 - sb_, pb, :]
                    for hd in range(2):
                        rows = slice(hd * DH, (hd + 1) * DH)
                        cols = slice(hd * VW, (hd + 1) * VW)
                        if ch:
                            dve.wait_ge(state_step, b * 8 + ch * 2 + hd - 1)
                        dve.scalar_tensor_tensor(dst[rows, cols], src[rows, cols], lam_end[rows, nb, ch:ch + 1],
                                                 U[ch][rows, cols], ALU.mult, ALU.add).then_inc(state_step, 1)

            def step(T, s, u):
                n = T * PAIRS + u
                Tb, pb, b = unit(T, u, 1)
                Ta, pa, a = unit(T, u, 2)
                nb = (u + 1) % 2
                na = u % 2
                sb_ = s if u + 1 < PAIRS else 1 - s
                if exists(Tb):
                    for hd in range(2):
                        dve.wait_ge(s_ps, 2 * b + hd + 1)
                        dve.wait_ge(decay_ready, 2 * b + hd + 1)
                        dve.tensor_tensor(p_sb[:, nb, hd, :], S[hd][:, :], decay[:, hd, :], ALU.mult)\
                           .then_inc(p_ready, 1)
                    dve.wait_ge(ktr_ps, b + 1)
                    to_end = decay[:, :, :].rearrange("p h (c i) -> p c h i", i=CH)[:, :, :, CH - 1:CH]
                    dve.tensor_tensor(kd_sb[:, :, :].rearrange("p c (h d) -> p c h d", d=DH),
                                      KTR[:, :].rearrange("p (c h d) -> p c h d", h=2, d=DH),
                                      to_end.to_broadcast([128, NCH, 2, DH]), ALU.mult).then_inc(kd_ready, 1)
                if u == 3 and exists(T + 1):
                    ln_apply(T + 1, 1 - s)
                if exists(Ta):
                    dve.wait_ge(q_exp, a + 1)
                    dve.scalar_tensor_tensor(q_sb[:, :], Q[:, :], 1.0, q_sb[:, :], ALU.add, ALU.max).then_inc(q_ready, 1)
                dense_out(T, s, u, 0)
                if exists(Ta):
                    after(dve, kd_ready, a)
                    for hd in range(2):
                        dve.wait_ge(abc_ps, 2 * a + hd + 1)
                        dve.tensor_tensor_scan(decay[:, hd, :], S[hd][:, :], eye4[:, :, :].rearrange("p c i -> p (c i)"),
                                               0.0, ALU.mult, ALU.add).then_inc(decay_ready, 1)
                    dve.wait_ge(k_exp, a + 1)
                    dve.scalar_tensor_tensor(k_sb[:, :], K[:, :], 1.0, k_sb[:, :], ALU.add, ALU.max).then_inc(k_ready, 1)
                if exists(Tb):
                    chain(Tb, sb_, pb, b, range(NCH - 1))
                if exists(T):
                    for half in range(2):
                        dve.wait_ge(num_ps, 2 * n + half + 1)
                        num = NUM[half][:, 0:4 * VW].rearrange("p (e v) -> p e v", v=VW)
                        dve.tensor_scalar(den[:, half, :].unsqueeze(2), num[:, :, DH:VW], DEN_EPS, None, ALU.add)\
                           .then_inc(den_step, 1)
                    dve.wait_ge(den_step, 3 * n + 2)
                    dve.reciprocal(rden[:, :, :], den[:, :, :]).then_inc(den_step, 1)
                    dve.wait_ge(den_step, 3 * n + 3)
                    for half in range(2):
                        num = NUM[half][:, 0:4 * VW].rearrange("p (e v) -> p e v", v=VW)
                        dve.tensor_tensor(o_sb[:, 2 * half:2 * half + 2, :].rearrange("p c (h d) -> p (c h) d", d=DH),
                                          num[:, :, 0:DH], rden[:, half, :].unsqueeze(2).to_broadcast([128, 4, DH]),
                                          ALU.mult).then_inc(o_ready, 1)
                if exists(Ta):
                    dve.wait_ge(lam_ps, a + 1)
                    dve.tensor_copy(lam_end[:, na, :].unsqueeze(2),
                                    Q[:, :].rearrange("p (c i) -> p c i", i=CH)[:, :, CH - 1:CH]).then_inc(lam_end_ready, 1)
                    dve.wait_ge(q_ready, a + 1)
                    dve.tensor_tensor(qs_sb[:, na, :], Q[:, :], q_sb[:, :], ALU.mult).then_inc(qs_ready, 1)
                dense_out(T, s, u, 1)
                if exists(Tb):
                    chain(Tb, sb_, pb, b, range(NCH - 1, NCH))
                if exists(T):
                    dve.wait_ge(oT_hi_ready, n + 1)
                    dve.tensor_tensor(oT_lo[:, u, :], NUM1[:, :], oT_hi[:, u, :].bitcast(F32), ALU.subtract)\
                       .then_inc(oT_lo_ready, 1)
                if u == 2 and exists(T + 1):
                    ln_stats(T + 1, 1 - s)
                if u in (3, 4) and exists(T + 1):
                    h_low(T + 1, 1 - s, u - 3)
                if u == 4 and exists(T + 1):
                    sigmoid(T + 1)
                if u == 5 and exists(T + 1):
                    decay_rows(T + 1, 1 - s)

            attention_steps(dve, step)


def expert_phase(nc, x1_dram, gates_dram, gate_W, gate_b, expert_W, expert_b, out_tokens, mod, ident, bank):
    EW = EXPERTS * D
    EB = 512 // D
    BLOCKS = 2 * EXPERTS // EB
    BLOCK_ADDS = 2 * EB
    with ExitStack() as ctx:
        def sb(name, shape, dt=F32):
            return ctx.enter_context(nc.sbuf_tensor(name, shape, dt))

        def sem(name):
            return ctx.enter_context(nc.semaphore(name))

        ew_hi, ew_lo = (sb("ew_" + h, [128, KT, EXPERTS, D], F32R) for h in ("hi", "lo"))
        ew_raw = sb("ew_raw", [128, KT, EXPERTS, D])
        eb = sb("eb", [EXPERTS, D])
        gw = sb("gw", [128, KT, EXPERTS])
        gbias = sb("gbias", [128, EXPERTS])
        gb = sb("gb", [128, BATCH, D])
        rank = sb("rank", [128, EXPERTS])
        half_neg2 = sb("half_neg2", [128, NCH])

        x1 = [sb(f"x1_{i}", [128, NCH, D]) for i in range(GPB)]
        xn = sb("xn2", [128, NCH, D])
        stats = sb("stats2", [128, NCH, 6])
        mean_var = sb("mean_var2", [128, NCH, 2])
        var_eps = sb("var_eps2", [128, NCH])
        rstd = sb("rstd2", [128, NCH])
        h32 = sb("h32_2", [128, KT, GT])
        h_hi = [sb(f"h2_hi{i}", [128, KT, GT], F32R) for i in range(2)]
        h_lo = [sb(f"h2_lo{i}", [128, KT, GT], F32R) for i in range(2)]
        sc, p, first, second, tmp = (sb(n, [128, NCH, EXPERTS]) for n in ("sc", "prob", "first", "second", "tmp"))
        red = sb("red", [128, 8, NCH])
        comb = [sb(f"comb{i}", [128, NCH, EXPERTS]) for i in range(2)]
        combT = sb("combT", [EXPERTS, GT])
        acc = [sb(f"acc{i}", [128, NCH, D]) for i in range(2)]

        Y = bank[0:4]
        HT, GATE, BIAS = bank[4], bank[5], bank[6:8]

        loaded = sem("e_loaded"); ew_loaded = [sem(f"ew_loaded{i}") for i in range(EXPERTS // EB)]; gb_loaded = sem("gb_loaded"); hi_split = sem("e_hi_split"); lo_split = sem("e_lo_split")
        fills = sem("e_fills")
        x1_loaded = [sem(f"x1_loaded{i}") for i in range(GPB)]
        out_stored = [sem(f"out_stored{i}") for i in range(GPB)]
        ln_step = sem("ln2_step"); var_ready = sem("var2_ready"); rstd_ready = sem("rstd2_ready"); xn_ready = sem("xn2_ready")
        hT_ps = sem("h2T_ps"); h32_ready = sem("h2_32_ready"); h_hi_ready = sem("h2_hi_ready"); h_lo_ready = sem("h2_lo_ready")
        stats_seen = sem("stats2_seen"); sums_seen = sem("sums_seen")
        gate_ps = sem("gate_ps"); route_step = sem("route_step"); route_exp_in = sem("route_exp_in"); route_exp = sem("route_exp"); total_ready = sem("total_ready")
        comb_ready = sem("comb_ready"); combT_ps = sem("combT_ps"); combT_ready = sem("combT_ready")
        bias_ps = sem("bias_ps"); acc_ready = sem("acc_ready")
        y_ps = sem("y_ps"); y_added = sem("y_added"); scaled = sem("scaled"); result_ready = sem("result_ready")

        ROUTE = 20
        ROUTE_BLOCK = 3
        ADDS = BLOCKS * BLOCK_ADDS

        def piece(t, q):
            return t[:, :, EB * q:EB * (q + 1), :].rearrange("p k e d -> p k (e d)")

        block = ctx.enter_context(nc.Block())

        @block.sync
        def _(sp):
            def load(T, s):
                after(sp, out_stored[s], (T - s) * (16 // GPB))
                sp.dma_start(x1[s][:, :, :], x1_dram[bass.ds(T, 1)].rearrange("g p c d -> (g p) c d"))\
                  .then_inc(x1_loaded[s], 16)

            load(0, 0)
            sp.dma_start(eb[:, :], expert_b).then_inc(loaded, 16)
            sp.dma_start(gw[:, :, :], gate_W.rearrange("(k p) e -> p k e", p=128)).then_inc(loaded, 16)
            sp.dma_start(gbias[:, :], gate_b.partition_broadcast(128)).then_inc(loaded, 16)
            for e in range(EXPERTS):
                sp.dma_start(ew_raw[:, :, e, :], expert_W[e].rearrange("(k p) f -> p k f", p=128))\
                  .then_inc(ew_loaded[e // EB], 16)
            load(1, 1)
            sp.dma_start(gb[:, :, :], gates_dram[1].partition_broadcast(128)).then_inc(gb_loaded, 16)

            def store(T, s):
                sp.wait_ge(result_ready, T * 2 + 2)
                sp.dma_start(out_tokens[bass.ds(T, 1)].rearrange("g p c d -> (g p) c d"), x1[s][:, :, :])\
                  .then_inc(out_stored[s], 16)

            def group(T, s):
                if exists(T - 1):
                    store(T - 1, (s - 1) % GPB)
                if exists(T + 3) and not (isinstance(T, int) and T + 3 < 2):
                    load(T + 3, (s + 3) % GPB)

            expert_groups(sp, group)
            store(NG - 1, (NG - 1) % GPB)
            for s in range(GPB):
                sp.wait_ge(out_stored[s], 16 * NG // GPB)

        @block.gpsimd
        def _(pool):
            pool.memset(half_neg2[:, :], -0.5).then_inc(fills, 1)
            for e in range(EXPERTS):
                pool.memset(rank[:, e:e + 1], float(EXPERTS - e)).then_inc(fills, 1)
            pool.wait_ge(fills, 1 + EXPERTS)

            def result(T, s, pair):
                b = batch_row(T)
                if isinstance(T, int) and T == 0:
                    pool.wait_ge(gb_loaded, 16)
                pool.wait_ge(y_added, T * ADDS + (pair + 1) * (ADDS // 2))
                pool.sem_inc(sums_seen)
                a = acc[s % 2][:, 2 * pair:2 * pair + 2, :]
                rows = x1[s][:, 2 * pair:2 * pair + 2, :]
                pool.tensor_tensor(a, a, gb[:, bass.ds(b, 1), :].to_broadcast([128, 2, D]), ALU.mult).then_inc(scaled, 1)
                pool.wait_ge(scaled, T * 2 + pair + 1)
                pool.tensor_tensor(rows, rows, a, ALU.add).then_inc(result_ready, 1)

            def group(T, s):
                if exists(T + 2):
                    pool.wait_ge(var_ready, T + 3)
                    pool.tensor_tensor(rstd[:, :], var_eps[:, :], half_neg2[:, :], ALU.pow).then_inc(rstd_ready, 1)
                if exists(T):
                    result(T, s, 0)
                    result(T, s, 1)

            expert_groups(pool, group)

        @block.scalar
        def _(act):
            def group(T, s):
                if exists(T):
                    for j in range(2):
                        act.wait_ge(bias_ps, T * 2 + j + 1)
                        after(act, result_ready, (T - 2) * 2 + j + 1)
                        act.activation(acc[s % 2][:, 2 * j:2 * j + 2, :], BIAS[j][:, :].rearrange("p (c d) -> p c d", d=D),
                                       ACT.Copy).then_inc(acc_ready, 1)
                if not exists(T + 1):
                    return
                Tn, sn = T + 1, (s + 1) % 2
                b = batch_row(Tn)
                after(act, h_lo_ready, Tn * 2)
                after(act, gate_ps, Tn)
                for kt in range(KT):
                    act.wait_ge(hT_ps, Tn * 2 + kt + 1)
                    act.activation(h32[:, kt, :], HT[:, :], ACT.Identity, bias=mod[:, 2, kt, bass.ds(b, 1)],
                                   scale=mod[:, 3, kt, bass.ds(b, 1)]).then_inc(h32_ready, 1)
                    act.wait_ge(h32_ready, Tn * 2 + kt + 1)
                    act.activation(h_hi[sn][:, kt, :], h32[:, kt, :], ACT.Copy).then_inc(h_hi_ready, 1)
                act.wait_ge(route_exp_in, Tn + 1)
                act.activation(p[:, :, :], sc[:, :, :], ACT.Exp).then_inc(route_exp, 1)
                if isinstance(T, int) and T == -1:
                    for q in range(EXPERTS // EB):
                        act.wait_ge(ew_loaded[q], 16 * EB)
                        act.activation(piece(ew_hi, q), piece(ew_raw, q), ACT.Copy).then_inc(hi_split, 1)
                act.wait_ge(combT_ps, Tn + 1)
                after(act, bias_ps, Tn * 2)
                act.activation(combT[:, :], GATE[0:EXPERTS, :], ACT.Copy).then_inc(combT_ready, 1)

            expert_groups(act, group)

        @block.tensor
        def _(pe):
            pe.wait_ge(loaded, 16 * 3)

            def y_block(T, s, j):
                pair, q = j // (BLOCKS // 2), j % (BLOCKS // 2)
                h, l = h_hi[s % 2], h_lo[s % 2]
                ex = slice(EB * q, EB * (q + 1))
                if isinstance(T, int) and T == 0 and pair == 0:
                    pe.wait_ge(lo_split, q + 1)
                for i in range(2):
                    y = Y[2 * (j % 2) + i]
                    tok = slice((2 * pair + i) * CH, (2 * pair + i + 1) * CH)
                    after(pe, y_added, T * ADDS + (j - 1) * BLOCK_ADDS - 1 + i)
                    for kt in range(KT):
                        pe.matmul(y[:, :], h[:, kt, tok], ew_hi[:, kt, ex, :], start=(kt == 0), stop=False)
                        pe.matmul(y[:, :], h[:, kt, tok], ew_lo[:, kt, ex, :], start=False, stop=False)
                        mm = pe.matmul(y[:, :], l[:, kt, tok], ew_hi[:, kt, ex, :], start=False, stop=(kt == KT - 1))
                    mm.then_inc(y_ps, 1)

            def transpose_h(Tn, kt):
                pe.wait_ge(xn_ready, Tn + 1)
                after(pe, h32_ready, Tn * 2 + kt)
                for ch in range(NCH):
                    mm = pe.transpose(HT[:, ch * CH:(ch + 1) * CH], xn[:, ch, kt * 128:(kt + 1) * 128], ident[:, :])
                mm.then_inc(hT_ps, 1)

            def gate(Tn):
                pe.wait_ge(h32_ready, Tn * 2 + 2)
                after(pe, combT_ready, Tn)
                for ch in range(NCH):
                    for kt in range(KT):
                        mm = pe.matmul(GATE[:, ch * EXPERTS:(ch + 1) * EXPERTS], h32[:, kt, ch * CH:(ch + 1) * CH],
                                       gw[:, kt, :], start=(kt == 0), stop=(kt == KT - 1))
                mm.then_inc(gate_ps, 1)

            def transpose_comb(Tn, sn):
                pe.wait_ge(comb_ready, Tn + 1)
                for ch in range(NCH):
                    mm = pe.transpose(GATE[0:EXPERTS, ch * CH:(ch + 1) * CH], comb[sn % 2][:, ch, :], ident[:, :])
                mm.then_inc(combT_ps, 1)

            def biases(T):
                pe.wait_ge(combT_ready, T + 1)
                after(pe, acc_ready, T * 2)
                for j in range(2):
                    for i in range(2):
                        ch = 2 * j + i
                        mm = pe.matmul(BIAS[j][:, i * D:(i + 1) * D], combT[:, ch * CH:(ch + 1) * CH], eb[:, :],
                                       start=True, stop=True)
                    mm.then_inc(bias_ps, 1)

            def group(T, s):
                for j in range(BLOCKS):
                    if exists(T):
                        if j == 0:
                            pe.wait_ge(h_lo_ready, T * 2 + 2)
                        y_block(T, s, j)
                        if j == 0:
                            biases(T)
                    if j < KT and exists(T + 1):
                        transpose_h(T + 1, j)
                    if j == KT and exists(T + 1):
                        gate(T + 1)
                if exists(T + 1):
                    transpose_comb(T + 1, s + 1)

            expert_groups(pe, group)

        @block.vector
        def _(dve):
            dve.wait_ge(fills, 1 + EXPERTS)
            dve.wait_ge(loaded, 16 * 3)

            def add(T, s, m):
                j, k = m // BLOCK_ADDS, m % BLOCK_ADDS
                pair, q = j // (BLOCKS // 2), j % (BLOCKS // 2)
                i, e = k % 2, EB * q + k // 2
                if k < 2:
                    dve.wait_ge(y_ps, T * BLOCKS * 2 + 2 * j + i + 1)
                if e == 0:
                    dve.wait_ge(acc_ready, T * 2 + pair + 1)
                else:
                    dve.wait_ge(y_added, T * ADDS + m - 1)
                a = acc[s % 2][:, 2 * pair + i, :]
                y = Y[2 * (j % 2) + i]
                dve.scalar_tensor_tensor(a, y[:, (k // 2) * D:(k // 2 + 1) * D], comb[s % 2][:, 2 * pair + i, e:e + 1], a,
                                         ALU.mult, ALU.add).then_inc(y_added, 1)

            def ln_stats(Tn, xs):
                dve.wait_ge(x1_loaded[xs], (Tn - xs) * (16 // GPB) + 16)
                for ch in range(NCH):
                    dve.bn_stats(stats[:, ch, :], x1[xs][:, ch, :]).then_inc(ln_step, 1)
                after(dve, xn_ready, Tn)
                dve.wait_ge(ln_step, Tn * 8 + NCH)
                dve.sem_inc(stats_seen)
                for ch in range(NCH):
                    dve.bn_aggr(mean_var[:, ch, :], stats[:, ch, :]).then_inc(ln_step, 1)
                dve.wait_ge(ln_step, Tn * 8 + 8)
                dve.tensor_scalar(var_eps[:, :].unsqueeze(2), mean_var[:, :, 1:2], LN_EPS, None, ALU.add)\
                   .then_inc(var_ready, 1)

            def ln_apply(Tn, xs):
                dve.wait_ge(rstd_ready, Tn + 1)
                after(dve, hT_ps, Tn * 2)
                for ch in range(NCH):
                    ins = dve.tensor_scalar(xn[:, ch, :], x1[xs][:, ch, :], mean_var[:, ch, 0:1], rstd[:, ch:ch + 1],
                                            ALU.subtract, ALU.mult)
                ins.then_inc(xn_ready, 1)

            def h_low(Tn, sn):
                for kt in range(KT):
                    dve.wait_ge(h_hi_ready, Tn * 2 + kt + 1)
                    dve.tensor_tensor(h_lo[sn][:, kt, :], h32[:, kt, :], h_hi[sn][:, kt, :].bitcast(F32), ALU.subtract)\
                       .then_inc(h_lo_ready, 1)

            def route(Tn, sn, between):
                count = [0]

                def counted(ins):
                    count[0] += 1
                    ins.then_inc(route_step, 1)
                    between(count[0])
                    dve.wait_ge(route_step, Tn * ROUTE + count[0])

                def per_expert(t):
                    return t.unsqueeze(2).to_broadcast([128, NCH, EXPERTS])

                rank_all = rank[:, :].unsqueeze(1).to_broadcast([128, NCH, EXPERTS])
                s_, p_, f1, f2, t_ = (t[:, :, :] for t in (sc, p, first, second, tmp))
                dve.wait_ge(gate_ps, Tn + 1)
                counted(dve.tensor_tensor(s_, GATE[:, 0:NCH * EXPERTS].rearrange("p (c e) -> p c e", e=EXPERTS),
                                          gbias[:, :].unsqueeze(1).to_broadcast([128, NCH, EXPERTS]), ALU.add))
                counted(dve.tensor_scalar(s_, s_, SCORE_EPS, None, ALU.max))
                counted(dve.tensor_reduce(red[:, 0, :], s_, AX_X, ALU.max))
                dve.tensor_tensor(s_, s_, per_expert(red[:, 0, :]), ALU.subtract).then_inc(route_exp_in, 1)
                dve.wait_ge(route_exp, Tn + 1)
                counted(dve.tensor_reduce(red[:, 1, :], p_, AX_X, ALU.add))
                counted(dve.reciprocal(red[:, 2, :], red[:, 1, :]))
                counted(dve.tensor_tensor(p_, p_, per_expert(red[:, 2, :]), ALU.mult))
                counted(dve.tensor_reduce(red[:, 3, :], p_, AX_X, ALU.max))
                counted(dve.tensor_tensor(f1, p_, per_expert(red[:, 3, :]), ALU.is_equal))
                counted(dve.tensor_tensor(f1, f1, rank_all, ALU.mult))
                counted(dve.tensor_reduce(red[:, 4, :], f1, AX_X, ALU.max))
                counted(dve.tensor_tensor(f1, f1, per_expert(red[:, 4, :]), ALU.is_equal))
                counted(dve.scalar_tensor_tensor(t_, f1, -2.0, p_, ALU.mult, ALU.add))
                counted(dve.tensor_reduce(red[:, 5, :], t_, AX_X, ALU.max))
                counted(dve.tensor_tensor(f2, t_, per_expert(red[:, 5, :]), ALU.is_equal))
                counted(dve.tensor_tensor(f2, f2, rank_all, ALU.mult))
                counted(dve.tensor_reduce(red[:, 6, :], f2, AX_X, ALU.max))
                counted(dve.tensor_tensor(f2, f2, per_expert(red[:, 6, :]), ALU.is_equal))
                counted(dve.tensor_tensor(f1, f1, f2, ALU.add))
                counted(dve.scalar_tensor_tensor(t_, p_, W_THRES, f1, ALU.max, ALU.mult))
                counted(dve.tensor_reduce(red[:, 7, :], t_, AX_X, ALU.add))
                assert count[0] == ROUTE
                dve.reciprocal(red[:, 0, :], red[:, 7, :]).then_inc(total_ready, 1)
                dve.wait_ge(total_ready, Tn + 1)
                dve.scalar_tensor_tensor(comb[sn][:, :, :], t_, 1.0 / TOP_K, per_expert(red[:, 0, :]), ALU.mult, ALU.mult)\
                   .then_inc(comb_ready, 1)

            def group(T, s):
                def adds(blocks):
                    if exists(T):
                        for m in range(blocks[0] * BLOCK_ADDS, blocks[1] * BLOCK_ADDS):
                            add(T, s, m)

                if exists(T + 1):
                    ln_apply(T + 1, (s + 1) % GPB)
                adds((0, 2))
                if exists(T + 1):
                    h_low(T + 1, (s + 1) % 2)
                adds((2, ROUTE_BLOCK))
                if exists(T + 2):
                    ln_stats(T + 2, (s + 2) % GPB)
                beside = min(ROUTE, (BLOCKS - ROUTE_BLOCK - 1) * BLOCK_ADDS)

                def between(k):
                    if exists(T) and k <= beside:
                        add(T, s, ROUTE_BLOCK * BLOCK_ADDS + k - 1)

                if exists(T + 1):
                    route(T + 1, (s + 1) % 2, between)
                    adds((BLOCKS - 1, BLOCKS))
                else:
                    adds((ROUTE_BLOCK, BLOCKS))
                if isinstance(T, int) and T == -1:
                    for q in range(EXPERTS // EB):
                        dve.wait_ge(hi_split, q + 1)
                        dve.tensor_tensor(piece(ew_lo, q), piece(ew_raw, q), piece(ew_hi, q).bitcast(F32), ALU.subtract)\
                           .then_inc(lo_split, 1)

            expert_groups(dve, group)


_INS = ["L0_attn_x", "L0_attn_Wq", "L0_attn_Wk", "L0_attn_Wv", "L0_attn_Wo", "L0_attn_Wa", "L0_attn_ba",
        "L0_ffn_gate_W", "L0_ffn_gate_b", "L0_ffn_expert_W", "L0_ffn_expert_b", "L0_c", "L0_wmod"]
_OUTS = [((BATCH, SEQ, D), "float32")]


def kernel(**inputs):
    import numpy as _np
    import concourse.bacc as _bacc
    from concourse import mybir as _mybir
    from concourse.bass_utils import run_bass_kernel_spmd as _run

    nc = _bacc.Bacc("TRN2", target_bir_lowering=False, num_devices=1)
    arrays, args = {}, []
    for name in _INS:
        a = _np.ascontiguousarray(inputs[name])
        arrays[f"in_{name}_dram"] = a
        args.append(nc.dram_tensor(f"in_{name}_dram", a.shape, _mybir.dt.from_np(a.dtype), kind="ExternalInput").ap())
    for i, (shape, dtype) in enumerate(_OUTS):
        dt = _mybir.dt.from_np(_np.dtype(dtype))
        args.append(nc.dram_tensor(f"out_{i}_dram", shape, dt, kind="ExternalOutput").ap())
    adaln_block(nc, *args)
    r = _run(nc, [arrays], core_ids=[0])
    got = tuple(r.results[0][f"out_{i}_dram"] for i in range(len(_OUTS)))
    return got[0]
```

```python
import concourse.bass as bass
from concourse import mybir
from contextlib import ExitStack

F32 = mybir.dt.float32
F32R = mybir.dt.float32r
ALU = mybir.AluOpType
ACT = mybir.ActivationFunctionType
AX_X = mybir.AxisListType.X

BATCH, SEQ, D = 8, 2048, 256
HEADS, DH = 16, 64
P_DIM = HEADS * DH
EXPERTS = 8
LN_EPS = 1e-5
DEN_EPS = 1e-6
DECAY_BIAS_SHIFT = 2.0
SCORE_EPS, W_THRES = 1e-4, 0.1
TOP_K = 2
GATE_FLOOR = 0.25
BIG = 3.0e38

CH = 128
HALF = CH // 2
SLICE = CH // 4
NCH = 4
GT = CH * NCH
NG = BATCH * SEQ // GT
GPB = SEQ // GT
KT = D // 128
PAIRS = HEADS // 2
PT = P_DIM // 128
VW = DH + 1
LO = 32
ROWS = LO + HEADS
ROWS_A = 64


def after(eng, sem, count):
    if isinstance(count, int) and count <= 0:
        return
    eng.wait_ge(sem, count)


def exists(T):
    return not isinstance(T, int) or 0 <= T < NG


def leads(T):
    return isinstance(T, int) and T == -1


def unit(T, u, ahead):
    Tn, p = (T, u + ahead) if u + ahead < PAIRS else (T + 1, u + ahead - PAIRS)
    return Tn, p, Tn * PAIRS + p


DENSE_JOBS = {(0, 0): ("wo", -1, 0), (0, 1): ("wo", -1, 1), (1, 0): ("v", 0, 4), (1, 1): ("v", 0, 5),
              (2, 0): ("v", 0, 6), (2, 1): ("h", 1, 0), (3, 0): ("v", 0, 7), (3, 1): ("h", 1, 1), (4, 0): ("z", 1, 0),
              (4, 1): ("v", 1, 0), (5, 0): ("a", 1, 0), (5, 1): ("v", 1, 1), (6, 0): ("v", 1, 2), (7, 0): ("v", 1, 3)}


def dense_at(T, s, u, part):
    job, ahead, k = DENSE_JOBS.get((u, part), (None, 0, 0))
    return (job, T + ahead, s if ahead == 0 else 1 - s, k) if exists(T + ahead) else (None, T, s, k)


def batch_row(T):
    b = T // GPB if isinstance(T, int) else T >> (GPB.bit_length() - 1)
    return b if isinstance(b, int) else b.with_bounds(min_val=0, max_val=BATCH - 1)


def attention_steps(eng, step):
    for T in (-1, 0, 1):
        for u in range(PAIRS):
            step(T, T % 2, u)
    with eng.Fori(1, NG // 2 - 1) as i:
        for s in range(2):
            for u in range(PAIRS):
                step(i * 2 + s, s, u)
    for T in (NG - 2, NG - 1):
        for u in range(PAIRS):
            step(T, T % 2, u)
    step(NG, 0, 0)


def expert_groups(eng, group):
    group(-2, GPB - 2)
    group(-1, GPB - 1)
    for T in range(GPB):
        group(T, T)
    with eng.Fori(1, BATCH - 1) as b:
        for s in range(GPB):
            group(b * GPB + s, s)
    for T in range(NG - GPB, NG):
        group(T, T % GPB)


def adaln_block(nc, x, Wq, Wk, Wv, Wo, Wa, ba, gate_W, gate_b, expert_W, expert_b, c, wmod, out):
    tokens = x.rearrange("b (g c p) d -> (b g) p c d", p=CH, c=NCH)
    out_tokens = out.rearrange("b (g c p) d -> (b g) p c d", p=CH, c=NCH)
    x1_dram = nc.dram_tensor("x1_dram", [NG, CH, NCH, D], F32, kind="Internal").ap()
    gates_dram = nc.dram_tensor("gates_dram", [2, BATCH, D], F32, kind="Internal").ap()

    with ExitStack() as keep:
        mod = keep.enter_context(nc.sbuf_tensor("mod", [128, 4, KT, BATCH], F32))
        ident = keep.enter_context(nc.sbuf_tensor("ident", [128, 128], F32))
        bank = [keep.enter_context(nc.psum_tensor(f"bank{i}", [128, 512], F32)) for i in range(8)]
        attention_phase(nc, tokens, Wq, Wk, Wv, Wo, Wa, ba, c, wmod, x1_dram, gates_dram, mod, ident, bank)
        expert_phase(nc, x1_dram, gates_dram, gate_W, gate_b, expert_W, expert_b, out_tokens, mod, ident, bank)


def attention_phase(nc, tokens, Wq, Wk, Wv, Wo, Wa, ba, c, wmod, x1_dram, gates_dram, mod, ident, bank):
    with ExitStack() as ctx:
        def sb(name, shape, dt=F32):
            return ctx.enter_context(nc.sbuf_tensor(name, shape, dt))

        def sem(name):
            return ctx.enter_context(nc.semaphore(name))

        w_names = ["wq", "wk", "wv"]
        w_hi = {n: sb(n + "_hi", [128, KT, P_DIM], F32R) for n in w_names}
        w_lo = {n: sb(n + "_lo", [128, KT, P_DIM], F32R) for n in w_names}
        wo_hi, wo_lo = (sb("wo_" + h, [128, PT, D], F32R) for h in ("hi", "lo"))
        wa = sb("wa", [128, KT, HEADS])
        ba2 = sb("ba2", [128, HEADS])
        ga = sb("ga", [128, BATCH, D])
        eye4 = sb("eye4", [128, NCH, CH])
        head_sel = sb("head_sel", [ROWS, HEADS, DH], F32R)
        head_sel32 = sb("head_sel32", [ROWS, HEADS])
        zero_row = sb("zero_row", [HEADS, CH])
        bound = sb("bound", [128, NG // 2])
        neg_bound = sb("neg_bound", [128, NG // 2])
        half_neg = sb("half_neg", [128, NCH])
        silu_t = sb("silu_t", [128, KT, BATCH])
        x_in = sb("x_in", [128, NCH, D])
        x_res = sb("x_res", [128, NCH, D])
        xn = sb("xn", [128, NCH, D])
        stats = sb("stats", [128, NCH, 6])
        mean_var = sb("mean_var", [128, NCH, 2])
        var_eps = sb("var_eps", [128, NCH])
        rstd = sb("rstd", [128, NCH])
        h32 = sb("h32", [128, KT, GT])
        h_hi = [sb(f"h_hi{i}", [128, KT, GT], F32R) for i in range(2)]
        h_lo = [sb(f"h_lo{i}", [128, KT, GT], F32R) for i in range(2)]
        v_sb = sb("v_sb", [128, NCH, HEADS, VW])
        a_tok = sb("a_tok", [128, NCH, HEADS])
        a_cols = sb("a_cols", [128, NCH, ROWS_A + HEADS], F32R)
        lam_row = sb("lam_row", [HEADS, GT])
        az = [sb(f"az{i}", [ROWS, NCH, CH], F32R) for i in range(2)]
        lam = sb("lam", [ROWS, NCH, CH], F32R)
        oT_hi = sb("oT_hi", [128, PT, GT], F32R)
        oT_lo = sb("oT_lo", [128, PT, GT], F32R)
        q_sb = sb("q_sb", [128, GT])
        k_sb = sb("k_sb", [128, GT])
        positive = sb("positive", [128, GT])
        qs_sb = sb("qs_sb", [128, 2, GT])
        lam_end = sb("lam_end", [128, 2, NCH])
        decay = sb("decay", [128, 2, GT])
        p_sb = sb("p_sb", [128, 2, 2, GT])
        kd_sb = sb("kd_sb", [128, NCH, 128])
        s_mid = sb("s_mid", [128, 2, NCH - 1, 2 * VW])
        carry = sb("carry", [128, 2, PAIRS, 2 * VW])
        den = sb("den", [128, 2, NCH])
        rden = sb("rden", [128, 2, NCH])
        o_sb = sb("o_sb", [128, NCH, 128])
        c_sb, c_e = h32[0:BATCH, 0, 0:D], h32[0:BATCH, 0, D:2 * D]
        gates = kd_sb[0:BATCH, :, :].rearrange("b c n -> b (c n)").rearrange("b (s d) -> b s d", s=2)
        gates_sign = o_sb[0:BATCH, :, :].rearrange("b c n -> b (c n)").rearrange("b (s d) -> b s d", s=2)

        Q, K, SA, SB, KTR, NUM0, NUM1, DENSE = bank
        S = [SA, SB]
        U = [KTR[:, ch * 2 * VW:(ch + 1) * 2 * VW] for ch in range(NCH - 1)] + [NUM0[:, 0:2 * VW]]
        NUM = [NUM0, NUM1]

        wmod_loaded = sem("wmod_loaded"); small_loaded = sem("small_loaded")
        w_loaded = [sem(f"w_loaded{i}") for i in range(5)]
        hi_split = sem("hi_split"); lo_split = sem("lo_split")
        consts_ready = sem("consts_ready"); carry_ready = sem("carry_ready"); ones_ready = sem("ones_ready")
        fills = sem("fills")
        silu_e = sem("silu_e"); silu_step = sem("silu_step"); silu_ps = sem("silu_ps"); siluT_ready = sem("siluT_ready")
        mod_ps = sem("mod_ps"); mod_ready = sem("mod_ready"); gates_step = sem("gates_step")
        gates_stored = sem("gates_stored"); ga_loaded = sem("ga_loaded"); ba_ready = sem("ba_ready")
        x_loaded = sem("x_loaded"); res_loaded = sem("res_loaded"); x1_stored = sem("x1_stored")
        ln_step = sem("ln_step"); var_ready = sem("var_ready"); rstd_ready = sem("rstd_ready"); xn_ready = sem("xn_ready")
        hT_ps = sem("hT_ps"); h32_ready = sem("h32_ready"); h_hi_ready = sem("h_hi_ready"); h_lo_ready = sem("h_lo_ready")
        z_ps = sem("z_ps"); zb_ready = sem("zb_ready"); z_exp = sem("z_exp"); a_step = sem("a_step")
        a_split = sem("a_split"); a_ready = sem("a_ready")
        arow_ps = sem("arow_ps"); az_ready = sem("az_ready")
        lam_step = sem("lam_step"); lam_hi_ready = sem("lam_hi_ready"); lam_ready = sem("lam_ready")
        v_ps = sem("v_ps"); v_ready = sem("v_ready")
        wo_ps = sem("wo_ps"); wo_scaled = sem("wo_scaled"); x1_ready = sem("x1_ready")
        stats_seen = sem("stats_seen")
        q_ps = sem("q_ps"); q_exp = sem("q_exp"); q_neg = sem("q_neg"); q_pos = sem("q_pos"); q_ready = sem("q_ready")
        k_ps = sem("k_ps"); k_exp = sem("k_exp"); k_neg = sem("k_neg"); k_pos = sem("k_pos"); k_ready = sem("k_ready")
        abc_ps = sem("abc_ps"); decay_ready = sem("decay_ready")
        lam_ps = sem("lam_ps"); qs_ready = sem("qs_ready"); lam_end_ready = sem("lam_end_ready")
        s_ps = sem("s_ps"); p_ready = sem("p_ready")
        ktr_ps = sem("ktr_ps"); kd_ready = sem("kd_ready")
        u_ps = sem("u_ps"); state_step = sem("state_step"); entry_clamped = sem("entry_clamped")
        num_ps = sem("num_ps"); den_step = sem("den_step"); o_ready = sem("o_ready")
        oT_ps = sem("oT_ps"); oT_hi_ready = sem("oT_hi_ready"); oT_lo_ready = sem("oT_lo_ready")

        def wide(t, dims):
            return t.rearrange(f"p {dims} -> p ({dims})")

        p_flat, v_flat = wide(p_sb[:, :, :, :], "a h n"), wide(v_sb[:, :, :, :], "c h v")
        carry_flat = wide(carry[:, :, :, :], "a h v")
        wmod_half = [t[:, 0:KT * 3 * D].rearrange("p (k n) -> p k n", k=KT) for t in (p_flat, carry_flat)]
        W, WO = KT * P_DIM, PT // 2 * D
        WQ, WV, WK, WO0, WO1 = range(5)
        big_w = [(Wq, w_hi["wq"], w_lo["wq"], v_flat[:, 0:W]), (Wv, w_hi["wv"], w_lo["wv"], v_flat[:, W:2 * W]),
                 (Wk, w_hi["wk"], w_lo["wk"], p_flat[:, 0:W]),
                 (Wo[0:P_DIM // 2], wo_hi[:, 0:PT // 2, :], wo_lo[:, 0:PT // 2, :], wide(x_res[:, :, :], "c d")),
                 (Wo[P_DIM // 2:], wo_hi[:, PT // 2:, :], wo_lo[:, PT // 2:, :], wide(qs_sb[:, :, :], "a n"))]
        SPLIT_AT = {0: (WQ,), 1: (WV,), 3: (WK,), 4: (WO0, WO1)}
        SMALL = 3
        MOD_A = 4
        SECTION = [0, 1, 3, 4]

        block = ctx.enter_context(nc.Block())

        @block.sync
        def _(sp):
            wm = wmod.rearrange("(k p) n -> p k n", p=128)
            sp.dma_start(c_sb, c).then_inc(small_loaded, 16)
            sp.dma_start(ba2[:, :], ba.partition_broadcast(128)).then_inc(small_loaded, 16)
            sp.dma_start(wa[:, :, :], Wa.rearrange("(k p) n -> p k n", p=128)).then_inc(small_loaded, 16)
            sp.dma_start(x_in[:, :, :], tokens[0]).then_inc(x_loaded, 16)
            for half in range(2):
                sp.dma_start(wmod_half[half], wm[:, :, half * 3 * D:(half + 1) * 3 * D]).then_inc(wmod_loaded, 16)
            for n, (src, _, _, raw) in enumerate(big_w):
                if n == WK:
                    sp.wait_ge(mod_ps, 1)
                rows = src.rearrange("(k p) n -> p k n", p=128)
                sp.dma_start(raw.rearrange("p (k n) -> p k n", n=src.shape[1]), rows).then_inc(w_loaded[n], 16)
            sp.wait_ge(gates_step, 4)
            sp.dma_start(gates_dram.rearrange("s b d -> b s d"), gates).then_inc(gates_stored, 16)
            sp.wait_ge(gates_stored, 16)
            sp.dma_start(ga[:, :, :], gates_dram[0].partition_broadcast(128)).then_inc(ga_loaded, 16)
            def step(T, s, u):
                if u == 0 and exists(T - 1):
                    after(sp, x1_ready, T * 2)
                    sp.dma_start(x1_dram[bass.ds(T - 1, 1)].rearrange("g p c d -> (g p) c d"), x_res[:, :, :])\
                      .then_inc(x1_stored, 16)
                if u == 0 and exists(T):
                    if isinstance(T, int) and T == 0:
                        sp.wait_ge(lo_split, WO0 + 1)
                    after(sp, x1_stored, T * 16)
                    sp.dma_start(x_res[:, :, :], tokens[bass.ds(T, 1)].rearrange("g p c d -> (g p) c d"))\
                      .then_inc(res_loaded, 16)
                if u == 4 and exists(T + 2):
                    sp.wait_ge(xn_ready, T + 2)
                    sp.dma_start(x_in[:, :, :], tokens[bass.ds(T + 2, 1)].rearrange("g p c d -> (g p) c d"))\
                      .then_inc(x_loaded, 16)

            attention_steps(sp, step)
            sp.wait_ge(x1_stored, 16 * NG)

        @block.gpsimd
        def _(pool):
            def reciprocal_deviation(T):
                pool.wait_ge(var_ready, T + 1)
                pool.tensor_tensor(rstd[:, :], var_eps[:, :], half_neg[:, :], ALU.pow).then_inc(rstd_ready, 1)

            pool.memset(ident[:, :], 0.0).then_inc(fills, 1)
            pool.memset(eye4[:, :, :], 0.0).then_inc(fills, 1)
            pool.memset(head_sel32[:, :], 0.0).then_inc(fills, 1)
            pool.memset(bound[:, :], 0.0).then_inc(fills, 1)
            pool.memset(neg_bound[:, :], 0.0).then_inc(fills, 1)
            pool.memset(half_neg[:, :], -0.5).then_inc(consts_ready, 1)
            pool.memset(zero_row[:, :], 0.0).then_inc(consts_ready, 1)
            pool.memset(s_mid[:, :, :, :], 0.0).then_inc(consts_ready, 1)
            pool.wait_ge(fills, 5)
            pool.memset(bound[:, :].rearrange("p (r e) -> p r e", e=2)[:, :, 1:2], BIG).then_inc(consts_ready, 1)
            pool.memset(neg_bound[:, :].rearrange("p (r e) -> p r e", e=2)[:, :, 1:2], -BIG).then_inc(consts_ready, 1)
            pool.affine_select(out=ident[:, :], in_=ident[:, :], compare_op=ALU.not_equal, fill=1.0, base=0,
                               pattern=[[-1, 128]], channel_multiplier=1).then_inc(consts_ready, 1)
            pool.affine_select(out=eye4[:, :, :], in_=eye4[:, :, :], compare_op=ALU.not_equal, fill=1.0, base=0,
                               pattern=[[0, NCH], [-1, CH]], channel_multiplier=1).then_inc(consts_ready, 1)
            pool.affine_select(out=head_sel32[:, :], in_=head_sel32[:, :], compare_op=ALU.not_equal, fill=1.0,
                               base=0, pattern=[[-1, HEADS]], channel_multiplier=1).then_inc(fills, 1)
            pool.wait_ge(fills, 6)
            pool.affine_select(out=head_sel32[:, :], in_=head_sel32[:, :], compare_op=ALU.not_equal, fill=1.0,
                               base=-LO, pattern=[[-1, HEADS]], channel_multiplier=1).then_inc(consts_ready, 1)
            reciprocal_deviation(0)
            pool.wait_ge(mod_ps, 1)
            pool.memset(carry[:, :, :, :], 0.0).then_inc(carry_ready, 1)

            def h_low(T, s, kt):
                pool.wait_ge(h_hi_ready, T * 2 + kt + 1)
                pool.tensor_tensor(h_lo[s][:, kt, :], h32[:, kt, :], h_hi[s][:, kt, :].bitcast(F32), ALU.subtract)\
                    .then_inc(h_lo_ready, 1)

            def lam_low(T):
                pool.wait_ge(lam_hi_ready, T + 1)
                hi, lo = (lam[at:at + HEADS, :, :].rearrange("r c i -> r (c i)") for at in (0, LO))
                pool.tensor_tensor(lo, lam_row[:, :], hi.bitcast(F32), ALU.subtract).then_inc(lam_ready, 1)

            def add_residual(T, j):
                if j == 0:
                    pool.wait_ge(res_loaded, (T + 1) * 16)
                pool.wait_ge(wo_scaled, T * 2 + j + 1)
                rows = x_res[:, 2 * j:2 * j + 2, :]
                pool.tensor_tensor(rows, rows, xn[:, 2 * j:2 * j + 2, :], ALU.add).then_inc(x1_ready, 1)

            def step(T, s, u):
                Ta, _, a = unit(T, u, 2)
                if exists(Ta):
                    pool.wait_ge(q_exp, a + 1)
                    pool.tensor_tensor(q_sb[:, :], positive[:, :], q_sb[:, :], ALU.add).then_inc(q_ready, 1)
                if u == 0 and exists(T + 1) and not leads(T):
                    reciprocal_deviation(T + 1)
                if u == 0 and exists(T - 1):
                    add_residual(T - 1, 0)
                if exists(Ta):
                    pool.wait_ge(k_exp, a + 1)
                    pool.tensor_tensor(k_sb[:, :], positive[:, :], k_sb[:, :], ALU.add).then_inc(k_ready, 1)
                if u == 0 and exists(T - 1):
                    add_residual(T - 1, 1)
                if u in (2, 3) and exists(T + 1):
                    h_low(T + 1, 1 - s, u - 2)
                if leads(T) and u == 4:
                    pool.wait_ge(lo_split, WV + 1)
                    pool.memset(v_sb[:, :, :, DH:VW], 1.0).then_inc(ones_ready, 1)
                    pool.wait_ge(ones_ready, 1)
                if u == 5 and exists(T + 1):
                    if exists(Ta):
                        pool.wait_ge(k_ready, a + 1)
                    lam_low(T + 1)
                    pool.wait_ge(lam_ready, T + 2)

            attention_steps(pool, step)

        @block.scalar
        def _(act):
            act.wait_ge(small_loaded, 16 * SMALL)
            act.activation(c_e, c_sb, ACT.Exp, scale=-1.0).then_inc(silu_e, 1)

            def split_weight(n):
                _, hi, _, raw = big_w[n]
                act.wait_ge(w_loaded[n], 16)
                act.activation(wide(hi[:, :, :], "k n"), raw, ACT.Copy).then_inc(hi_split, 1)

            def v_out(T, half, ch):
                act.wait_ge(v_ps, T * 8 + half * NCH + ch + 1)
                hs = half * (HEADS // 2)
                act.activation(v_sb[:, ch, hs:hs + HEADS // 2, 0:DH],
                               DENSE[:, :].rearrange("p (h d) -> p h d", d=DH), ACT.Copy).then_inc(v_ready, 1)

            def h_out(T, s, kt):
                act.wait_ge(hT_ps, T * 2 + kt + 1)
                if kt == 0:
                    act.wait_ge(mod_ready, 2)
                b = batch_row(T)
                act.activation(h32[:, kt, :], DENSE[:, :], ACT.Identity, bias=mod[:, 0, kt, bass.ds(b, 1)],
                               scale=mod[:, 1, kt, bass.ds(b, 1)]).then_inc(h32_ready, 1)
                act.wait_ge(h32_ready, T * 2 + kt + 1)
                act.activation(h_hi[s][:, kt, :], h32[:, kt, :], ACT.Copy).then_inc(h_hi_ready, 1)

            def dense_out(T, s, u, part):
                job, of, so, k = dense_at(T, s, u, part)
                if job == "v":
                    v_out(of, k // NCH, k % NCH)
                if job == "h":
                    h_out(of, so, k)
                if job == "a":
                    act.wait_ge(arow_ps, of + 1)
                    after(act, abc_ps, ((of - 1) * PAIRS + PAIRS - 1) * 2)
                    act.activation(az[so][:, :, :].rearrange("r c i -> r (c i)"), DENSE[0:ROWS, :], ACT.Copy)\
                       .then_inc(az_ready, 1)

            def step(T, s, u):
                Tb, _, b = unit(T, u, 1)
                Ta, _, a = unit(T, u, 2)
                if exists(Tb):
                    if isinstance(Tb, int) and b == 0:
                        act.wait_ge(gates_stored, 16)
                    act.wait_ge(decay_ready, 2 * b + 2)
                    act.wait_ge(ktr_ps, b + 1)
                    for ch in range(NCH):
                        for hd in range(2):
                            ins = act.activation(kd_sb[:, ch, hd * DH:(hd + 1) * DH],
                                                 KTR[:, ch * CH + hd * DH:ch * CH + (hd + 1) * DH], ACT.Copy,
                                                 scale=decay[:, hd, (ch + 1) * CH - 1:(ch + 1) * CH])
                    ins.then_inc(kd_ready, 1)
                if exists(Ta):
                    act.wait_ge(q_ps, a + 1)
                    after(act, qs_ready, a)
                    act.activation(q_sb[:, :], Q[:, :], ACT.Relu, scale=-1.0).then_inc(q_neg, 1)
                    after(act, k_ready, a)
                    act.activation(positive[:, :], Q[:, :], ACT.Relu).then_inc(q_pos, 1)
                    act.wait_ge(q_neg, a + 1)
                    act.activation(q_sb[:, :], q_sb[:, :], ACT.Exp, scale=-1.0).then_inc(q_exp, 1)
                dense_out(T, s, u, 0)
                if exists(Ta):
                    act.wait_ge(k_ps, a + 1)
                    act.activation(k_sb[:, :], K[:, :], ACT.Relu, scale=-1.0).then_inc(k_neg, 1)
                    act.wait_ge(q_ready, a + 1)
                    act.activation(positive[:, :], K[:, :], ACT.Relu).then_inc(k_pos, 1)
                    act.wait_ge(k_neg, a + 1)
                    act.activation(k_sb[:, :], k_sb[:, :], ACT.Exp, scale=-1.0).then_inc(k_exp, 1)
                if u == 4 and exists(T + 1):
                    act.wait_ge(zb_ready, T + 2)
                    act.activation(a_tok[:, :, :], a_tok[:, :, :], ACT.Exp, scale=-1.0).then_inc(z_exp, 1)
                dense_out(T, s, u, 1)
                if leads(T):
                    for n in SPLIT_AT.get(u, ()):
                        split_weight(n)
                if exists(T):
                    n = T * PAIRS + u
                    act.wait_ge(oT_ps, n + 1)
                    act.activation(oT_hi[:, u, :], K[:, :], ACT.Copy).then_inc(oT_hi_ready, 1)
                if u == 5 and exists(T + 1):
                    act.wait_ge(lam_step, (T + 2) * NCH)
                    after(act, lam_ps, (T + 1) * PAIRS)
                    act.activation(lam[0:HEADS, :, :].rearrange("r c i -> r (c i)"), lam_row[:, :], ACT.Copy)\
                       .then_inc(lam_hi_ready, 1)

            attention_steps(act, step)

        @block.tensor
        def _(pe):
            pe.wait_ge(consts_ready, 8)
            pe.wait_ge(silu_step, 3)
            for kt in range(KT):
                mm = pe.transpose(DENSE[:, kt * BATCH:(kt + 1) * BATCH], c_e[:, kt * 128:(kt + 1) * 128],
                                  ident[0:BATCH, 0:BATCH])
            mm.then_inc(silu_ps, 1)
            pe.wait_ge(siluT_ready, 1)
            pe.wait_ge(wmod_loaded, 32)
            for m, sec in enumerate(SECTION):
                for kt in range(KT):
                    col = (m * KT + kt) * BATCH
                    w = wmod_half[sec // 3][:, :, (sec % 3) * D + kt * 128:(sec % 3) * D + (kt + 1) * 128]
                    for k2 in range(KT):
                        pe.matmul(SA[:, col:col + BATCH], w[:, k2, :], silu_t[:, k2, :],
                                  start=(k2 == 0), stop=(k2 == KT - 1))
            for g in range(2):
                for k2 in range(KT):
                    mm = pe.matmul(SB[0:BATCH, g * D:(g + 1) * D], silu_t[:, k2, :],
                                   wmod_half[g][:, k2, 2 * D:3 * D], start=(k2 == 0), stop=(k2 == KT - 1))
            mm.then_inc(mod_ps, 1)
            pe.wait_ge(mod_ready, 3)
            pe.wait_ge(gates_step, 3)

            def three_pass(dst, pairs):
                last = len(pairs) - 1
                for n, (s_hi, s_lo, m_hi, m_lo) in enumerate(pairs):
                    pe.matmul(dst, s_hi, m_hi, start=(n == 0), stop=False)
                    pe.matmul(dst, s_hi, m_lo, start=False, stop=False)
                    mm = pe.matmul(dst, s_lo, m_hi, start=False, stop=(n == last))
                return mm

            def project(Tn, sn, p, w, dst, done):
                h, l = h_hi[sn], h_lo[sn]
                cols = slice(p * 128, (p + 1) * 128)
                three_pass(dst[:, :], [(w_hi[w][:, kt, cols], w_lo[w][:, kt, cols], h[:, kt, :], l[:, kt, :])
                                       for kt in range(KT)]).then_inc(done, 1)

            def h_job(T, kt):
                after(pe, v_ready, (T - 1) * 8 + 7 + kt)
                if kt == 0:
                    pe.wait_ge(xn_ready, T + 1)
                else:
                    pe.wait_ge(h32_ready, T * 2 + 1)
                for ch in range(NCH):
                    mm = pe.transpose(DENSE[:, ch * CH:(ch + 1) * CH], xn[:, ch, kt * 128:(kt + 1) * 128], ident[:, :])
                mm.then_inc(hT_ps, 1)

            def z_job(T):
                pe.wait_ge(h32_ready, T * 2 + 2)
                for ch in range(NCH):
                    for kt in range(KT):
                        for at in range(0, CH, SLICE):
                            mm = pe.matmul(DENSE[at:at + SLICE, ch * HEADS:(ch + 1) * HEADS],
                                           h32[:, kt, ch * CH + at:ch * CH + at + SLICE], wa[:, kt, :],
                                           start=(kt == 0), stop=(kt == KT - 1))
                mm.then_inc(z_ps, 1)

            def arow_job(T):
                pe.wait_ge(a_ready, T + 1)
                pe.wait_ge(v_ready, T * 8 + 1)
                for ch in range(NCH):
                    mm = pe.transpose(DENSE[0:ROWS_A + HEADS, ch * CH:(ch + 1) * CH], a_cols[:, ch, :].bitcast(F32),
                                      ident[:, :])
                mm.then_inc(arow_ps, 1)

            def v_job(T, s, half, ch):
                n = T * 8 + half * NCH + ch
                if half == 0 and ch == 0:
                    pe.wait_ge(zb_ready, T + 1)
                    after(pe, num_ps, ((T - 1) * PAIRS + PAIRS // 2) * 2)
                elif half == 1 and ch == 0:
                    after(pe, wo_scaled, T * 2)
                    after(pe, v_ready, n)
                elif half == 0 and ch == 1:
                    pe.wait_ge(az_ready, T + 1)
                    pe.wait_ge(lam_step, (T + 1) * NCH)
                elif half == 1 and ch == NCH - 1 and exists(T + 1):
                    pe.wait_ge(h32_ready, (T + 1) * 2 + 1)
                else:
                    pe.wait_ge(v_ready, n)
                if isinstance(T, int) and T == 0 and n == 0:
                    pe.wait_ge(lo_split, WV + 1)
                pe.wait_ge(h_lo_ready, T * 2 + 2)
                tok = slice(ch * CH, (ch + 1) * CH)
                cols = slice(half * 512, (half + 1) * 512)
                three_pass(DENSE[:, :], [(h_hi[s][:, kt, tok], h_lo[s][:, kt, tok], w_hi["wv"][:, kt, cols],
                                          w_lo["wv"][:, kt, cols]) for kt in range(KT)]).then_inc(v_ps, 1)

            def wo_job(T, j):
                if j == 0:
                    after(pe, v_ready, T * 8 + (12 if exists(T + 1) else 8))
                    pe.wait_ge(oT_lo_ready, T * PAIRS + PAIRS)
                    if isinstance(T, int) and T == 0:
                        pe.wait_ge(lo_split, WO1 + 1)
                else:
                    pe.wait_ge(wo_scaled, T * 2 + 1)
                for i in range(2):
                    tok = slice((2 * j + i) * CH, (2 * j + i + 1) * CH)
                    mm = three_pass(DENSE[:, i * D:(i + 1) * D],
                                    [(oT_hi[:, pt, tok], oT_lo[:, pt, tok], wo_hi[:, pt, :], wo_lo[:, pt, :])
                                     for pt in range(PT)])
                mm.then_inc(wo_ps, 1)

            def dense_job(T, s, u, part):
                job, of, so, k = dense_at(T, s, u, part)
                if job == "wo":
                    wo_job(of, k)
                if job == "v":
                    v_job(of, so, k // NCH, k % NCH)
                if job == "h":
                    h_job(of, k)
                if job == "z":
                    z_job(of)
                if job == "a":
                    arow_job(of)

            def step(T, s, u):
                n = T * PAIRS + u
                Tb, pb, b = unit(T, u, 1)
                Ta, pa, a = unit(T, u, 2)
                sa = s if u + 2 < PAIRS else 1 - s
                if exists(Tb):
                    pe.wait_ge(q_ready, b + 1)
                    pe.wait_ge(k_ready, b + 1)
                    pe.wait_ge(decay_ready, 2 * b + 2)
                    for ch in range(NCH):
                        tok = slice(ch * CH, (ch + 1) * CH)
                        for hd in range(2):
                            rows = slice(hd * DH, (hd + 1) * DH)
                            mm = pe.matmul(S[hd][:, tok], k_sb[rows, tok], q_sb[rows, tok], start=True, stop=True)
                            if ch == NCH - 1:
                                mm.then_inc(s_ps, 1)
                    after(pe, state_step, b * 8 - 2)
                    for ch in range(NCH):
                        mm = pe.transpose(KTR[:, ch * CH:(ch + 1) * CH], k_sb[:, ch * CH:(ch + 1) * CH], ident[:, :])
                    mm.then_inc(ktr_ps, 1)
                if exists(Ta):
                    pe.wait_ge(h_lo_ready, Ta * 2 + 2)
                    if isinstance(Ta, int) and a == 0:
                        pe.wait_ge(lo_split, WK + 1)
                    after(pe, qs_ready, a)
                    project(Ta, sa, pa, "wq", Q, q_ps)
                dense_job(T, s, u, 0)
                if exists(Ta):
                    pe.wait_ge(az_ready, Ta + 1)
                    after(pe, p_ready, 2 * a)
                    for hd in range(2):
                        hcol = head_sel[:, 2 * pa + hd, 0:1]
                        pe.matmul(S[hd][:, :], hcol.to_broadcast([ROWS, 128]),
                                  az[sa][:, :, :].rearrange("r c i -> r (c i)"),
                                  start=True, stop=True).then_inc(abc_ps, 1)
                    after(pe, oT_lo_ready, a - 2)
                    project(Ta, sa, pa, "wk", K, k_ps)

                if exists(T):
                    pe.wait_ge(qs_ready, n + 1)
                    pe.wait_ge(p_ready, 2 * n + 2)
                    pe.wait_ge(state_step, n * 8 + 8)
                    after(pe, o_ready, 2 * n)
                    for ch in range(NCH):
                        tok = slice(ch * CH, (ch + 1) * CH)
                        state = carry[:, s, u, :] if ch == 0 else s_mid[:, u % 2, ch - 1, :]
                        at = (ch % 2) * 2 * VW
                        pe.matmul(NUM[ch // 2][:, at:at + 2 * VW], qs_sb[:, u % 2, tok], state,
                                  start=(ch % 2 == 0), stop=False)
                    for ch in range(NCH):
                        for hd in range(2):
                            at = ((ch % 2) * 2 + hd) * VW
                            for half in range(2):
                                rows = slice(half * HALF, (half + 1) * HALF)
                                keys = slice(0, (half + 1) * HALF)
                                mm = pe.matmul(NUM[ch // 2][rows, at:at + VW],
                                               p_sb[keys, u % 2, hd, ch * CH + half * HALF:ch * CH + (half + 1) * HALF],
                                               v_sb[keys, ch, 2 * u + hd, :], start=False,
                                               stop=(ch % 2 == 1 and hd == 1))
                        if ch % 2:
                            mm.then_inc(num_ps, 1)
                if exists(Ta):
                    pe.wait_ge(lam_ready, Ta + 1)
                    pe.wait_ge(q_pos, a + 1)
                    pe.matmul(Q[:, :], head_sel[:, 2 * pa:2 * pa + 2, :].rearrange("r h d -> r (h d)"),
                              lam[:, :, :].rearrange("r c i -> r (c i)"), start=True, stop=True).then_inc(lam_ps, 1)

                def states(chunks):
                    for ch in chunks:
                        for hd in range(2):
                            rows = slice(hd * DH, (hd + 1) * DH)
                            mm = pe.matmul(U[ch][rows, hd * VW:(hd + 1) * VW], kd_sb[:, ch, rows],
                                           v_sb[:, ch, 2 * pb + hd, :], start=True, stop=True)
                    mm.then_inc(u_ps, 1)

                if exists(Tb):
                    pe.wait_ge(kd_ready, b + 1)
                    if isinstance(Tb, int) and b == 0:
                        pe.wait_ge(ones_ready, 1)
                    pe.wait_ge(v_ready, Tb * 8 + (NCH if pb < PAIRS // 2 else 2 * NCH))
                    states(range(NCH - 1))
                dense_job(T, s, u, 1)

                def transpose_o(half):
                    pe.wait_ge(o_ready, 2 * n + half + 1)
                    for ch in (2 * half, 2 * half + 1):
                        mm = pe.transpose(K[:, ch * CH:(ch + 1) * CH], o_sb[:, ch, :], ident[:, :])
                    return mm

                if exists(T):
                    if exists(Ta):
                        pe.wait_ge(k_pos, a + 1)
                    transpose_o(0)
                if exists(Tb):
                    after(pe, o_ready, 2 * b - 1)
                    states(range(NCH - 1, NCH))
                if exists(T):
                    transpose_o(1).then_inc(oT_ps, 1)

            attention_steps(pe, step)

        @block.vector
        def _(dve):
            dve.wait_ge(silu_e, 1)
            dve.tensor_scalar(c_e, c_e, 1.0, None, ALU.add).then_inc(silu_step, 1)
            dve.wait_ge(silu_step, 1)
            dve.reciprocal(c_e, c_e).then_inc(silu_step, 1)
            dve.wait_ge(silu_step, 2)
            dve.tensor_tensor(c_e, c_e, c_sb, ALU.mult).then_inc(silu_step, 1)
            dve.tensor_scalar(ba2[:, :], ba2[:, :], DECAY_BIAS_SHIFT, None, ALU.add).then_inc(ba_ready, 1)
            dve.wait_ge(silu_ps, 1)
            dve.tensor_copy(silu_t[:, :, :], DENSE[:, 0:KT * BATCH].rearrange("p (k b) -> p k b", b=BATCH))\
               .then_inc(siluT_ready, 1)
            dve.wait_ge(consts_ready, 8)
            dve.tensor_copy(head_sel[:, :, :], head_sel32[:, :].unsqueeze(2).to_broadcast([ROWS, HEADS, DH]))
            for t in (lam, a_cols):
                dve.memset(t[:, :, :].bitcast(F32), 0.0)
            def split_weight(n):
                _, hi, lo, raw = big_w[n]
                dve.wait_ge(hi_split, n + 1)
                dve.tensor_tensor(wide(lo[:, :, :], "k n"), raw, wide(hi[:, :, :], "k n").bitcast(F32), ALU.subtract)\
                   .then_inc(lo_split, 1)

            def wo_out(T, s, j):
                b = batch_row(T)
                if j == 0 and isinstance(T, int) and T == 0:
                    dve.wait_ge(ga_loaded, 16)
                dve.wait_ge(wo_ps, T * 2 + j + 1)
                after(dve, x1_ready, T * 2)
                gb = ga[:, bass.ds(b, 1), :].to_broadcast([128, 2, D])
                dve.tensor_tensor(xn[:, 2 * j:2 * j + 2, :], DENSE[:, :].rearrange("p (c d) -> p c d", d=D), gb,
                                  ALU.mult).then_inc(wo_scaled, 1)

            def ln_stats(T):
                dve.wait_ge(x_loaded, T * 16 + 16)
                for ch in range(NCH):
                    dve.bn_stats(stats[:, ch, :], x_in[:, ch, :]).then_inc(ln_step, 1)
                dve.wait_ge(ln_step, T * 8 + NCH)
                dve.sem_inc(stats_seen)
                for ch in range(NCH):
                    dve.bn_aggr(mean_var[:, ch, :], stats[:, ch, :]).then_inc(ln_step, 1)
                dve.wait_ge(ln_step, T * 8 + 8)
                dve.tensor_scalar(var_eps[:, :].unsqueeze(2), mean_var[:, :, 1:2], LN_EPS, None, ALU.add)\
                   .then_inc(var_ready, 1)

            def ln_apply(T):
                dve.wait_ge(rstd_ready, T + 1)
                after(dve, x1_ready, T * 2 - 2)
                for ch in range(NCH):
                    ins = dve.tensor_scalar(xn[:, ch, :], x_in[:, ch, :], mean_var[:, ch, 0:1], rstd[:, ch:ch + 1],
                                            ALU.subtract, ALU.mult)
                ins.then_inc(xn_ready, 1)

            def z_out(T):
                dve.wait_ge(z_ps, T + 1)
                dve.wait_ge(ba_ready, 1)
                dve.tensor_tensor(a_tok[:, :, :], DENSE[:, 0:NCH * HEADS].rearrange("p (c h) -> p c h", h=HEADS),
                                  ba2[:, :].unsqueeze(1).to_broadcast([128, NCH, HEADS]), ALU.add).then_inc(zb_ready, 1)

            def sigmoid_step(T, k):
                a, hi, lo = (a_cols[:, :, at:at + HEADS] for at in (ROWS_A, 0, LO))
                if k == 0:
                    dve.wait_ge(z_exp, T + 1)
                    dve.tensor_scalar(a_tok[:, :, :], a_tok[:, :, :], 1.0, None, ALU.add).then_inc(a_step, 1)
                if k == 1:
                    after(dve, arow_ps, T)
                    dve.wait_ge(a_step, T * 3 + 1)
                    dve.reciprocal(a.bitcast(F32), a_tok[:, :, :]).then_inc(a_step, 1)
                if k == 2:
                    dve.wait_ge(a_step, T * 3 + 2)
                    dve.tensor_copy(hi, a.bitcast(F32)).then_inc(a_step, 1)
                if k == 3:
                    dve.wait_ge(a_step, T * 3 + 3)
                    dve.tensor_tensor(lo, a.bitcast(F32), hi.bitcast(F32), ALU.subtract).then_inc(a_split, 1)
                if k == 4:
                    dve.wait_ge(a_split, T + 1)
                    dve.memset(a_cols[0:1, :, 0:ROWS].bitcast(F32), 0.0).then_inc(a_ready, 1)

            def decay_products(T):
                dve.wait_ge(arow_ps, T + 1)
                after(dve, lam_ready, T)
                for ch in range(NCH):
                    tok = slice(ch * CH, (ch + 1) * CH)
                    dve.tensor_tensor_scan(lam_row[:, tok], DENSE[ROWS_A:ROWS_A + HEADS, tok], zero_row[:, :], 1.0,
                                           ALU.mult, ALU.add).then_inc(lam_step, 1)

            def dense_out(T, s, u, part):
                job, of, so, k = dense_at(T, s, u, part)
                if job == "wo":
                    wo_out(of, so, k)
                if job == "z":
                    z_out(of)
                if job == "a":
                    decay_products(of)

            def chain(Tb, sb_, pb, b, ch, hd):
                entry = carry[:, sb_, pb, :]
                nb = pb % 2
                if ch == 0 and hd == 0:
                    if sb_ == 0 and not (isinstance(Tb, int) and Tb == 0):
                        i = Tb >> 1
                        dve.wait_ge(state_step, (b - PAIRS + 1) * 8)
                        dve.tensor_scalar(entry, entry, bound[:, bass.ds(i, 1)], neg_bound[:, bass.ds(i, 1)],
                                          ALU.min, ALU.max).then_inc(entry_clamped, 1)
                        dve.wait_ge(entry_clamped, Tb * (PAIRS // 2) - PAIRS + pb + 1)
                    if isinstance(Tb, int) and b == 0:
                        dve.wait_ge(carry_ready, 1)
                    dve.wait_ge(lam_end_ready, b + 1)
                    dve.wait_ge(u_ps, 2 * b + 1)
                if ch == NCH - 1 and hd == 0:
                    dve.wait_ge(u_ps, 2 * b + 2)
                src = entry if ch == 0 else s_mid[:, nb, ch - 1, :]
                dst = s_mid[:, nb, ch, :] if ch < NCH - 1 else carry[:, 1 - sb_, pb, :]
                rows = slice(hd * DH, (hd + 1) * DH)
                cols = slice(hd * VW, (hd + 1) * VW)
                if ch:
                    dve.wait_ge(state_step, b * 8 + ch * 2 + hd - 1)
                dve.scalar_tensor_tensor(dst[rows, cols], src[rows, cols], lam_end[rows, nb, ch:ch + 1], U[ch][rows, cols],
                                         ALU.mult, ALU.add).then_inc(state_step, 1)

            def step(T, s, u):
                n = T * PAIRS + u
                Tb, pb, b = unit(T, u, 1)
                Ta, pa, a = unit(T, u, 2)
                nb = (u + 1) % 2
                na = u % 2
                sb_ = s if u + 1 < PAIRS else 1 - s
                if exists(Tb):
                    for hd in range(2):
                        dve.wait_ge(s_ps, 2 * b + hd + 1)
                        dve.wait_ge(decay_ready, 2 * b + hd + 1)
                        dve.tensor_tensor(p_sb[:, nb, hd, :], S[hd][:, :], decay[:, hd, :], ALU.mult)\
                           .then_inc(p_ready, 1)
                if u == 2 and exists(T + 1) and not leads(T):
                    ln_apply(T + 1)
                if u == 0 and exists(T + 1) and not leads(T):
                    ln_stats(T + 1)
                dense_out(T, s, u, 0)
                if exists(Ta):
                    after(dve, kd_ready, a)
                    for hd in range(2):
                        dve.wait_ge(abc_ps, 2 * a + hd + 1)
                        dve.tensor_tensor_scan(decay[:, hd, :], S[hd][:, :], eye4[:, :, :].rearrange("p c i -> p (c i)"),
                                               0.0, ALU.mult, ALU.add).then_inc(decay_ready, 1)
                if exists(T):
                    for half in range(2):
                        dve.wait_ge(num_ps, 2 * n + half + 1)
                        num = NUM[half][:, 0:4 * VW].rearrange("p (e v) -> p e v", v=VW)
                        dve.tensor_scalar(den[:, half, :].unsqueeze(2), num[:, :, DH:VW], DEN_EPS, None, ALU.add)\
                           .then_inc(den_step, 1)
                        dve.wait_ge(den_step, 4 * n + 2 * half + 1)
                        dve.reciprocal(rden[:, half, :], den[:, half, :]).then_inc(den_step, 1)
                        dve.wait_ge(den_step, 4 * n + 2 * half + 2)
                        dve.tensor_tensor(o_sb[:, 2 * half:2 * half + 2, :].rearrange("p c (h d) -> p (c h) d", d=DH),
                                          num[:, :, 0:DH], rden[:, half, :].unsqueeze(2).to_broadcast([128, 4, DH]),
                                          ALU.mult).then_inc(o_ready, 1)
                for k in range((NCH - 1) * 2):
                    if exists(Tb):
                        chain(Tb, sb_, pb, b, k // 2, k % 2)
                    if u == 4 and exists(T + 1):
                        sigmoid_step(T + 1, k)
                if exists(Ta):
                    dve.wait_ge(lam_ps, a + 1)
                    dve.tensor_copy(lam_end[:, na, :].unsqueeze(2),
                                    Q[:, :].rearrange("p (c i) -> p c i", i=CH)[:, :, CH - 1:CH]).then_inc(lam_end_ready, 1)
                    dve.wait_ge(q_ready, a + 1)
                    if isinstance(Ta, int) and a == 0:
                        dve.wait_ge(lo_split, WO1 + 1)
                    dve.tensor_tensor(qs_sb[:, na, :], Q[:, :], q_sb[:, :], ALU.mult).then_inc(qs_ready, 1)
                dense_out(T, s, u, 1)
                if exists(Tb):
                    for hd in range(2):
                        chain(Tb, sb_, pb, b, NCH - 1, hd)
                if leads(T):
                    for k in SPLIT_AT.get(u, ()):
                        split_weight(k)
                if exists(T):
                    dve.wait_ge(oT_hi_ready, n + 1)
                    dve.tensor_tensor(oT_lo[:, u, :], K[:, :], oT_hi[:, u, :].bitcast(F32), ALU.subtract)\
                       .then_inc(oT_lo_ready, 1)

            ln_stats(0)
            ln_apply(0)
            dve.wait_ge(mod_ps, 1)
            mods = SA[:, 0:MOD_A * KT * BATCH].rearrange("p (m k b) -> p m k b", k=KT, b=BATCH)
            for m in range(MOD_A):
                dve.tensor_scalar(mod[:, m, :, :], mods[:, m, :, :], float(m % 2), None, ALU.add)\
                   .then_inc(mod_ready, 1)
            g_ps = SB[0:BATCH, :].rearrange("b (s d) -> b s d", s=2)
            dve.tensor_scalar(gates_sign, g_ps, 0.0, 2.0, ALU.is_ge, ALU.mult).then_inc(gates_step, 1)
            dve.tensor_scalar(gates, g_ps, -1.0, None, ALU.mult).then_inc(gates_step, 1)
            dve.wait_ge(gates_step, 2)
            dve.scalar_tensor_tensor(gates, g_ps, GATE_FLOOR, gates, ALU.max, ALU.max).then_inc(gates_step, 1)
            dve.wait_ge(gates_step, 3)
            dve.scalar_tensor_tensor(gates, gates_sign, -1.0, gates, ALU.add, ALU.mult).then_inc(gates_step, 1)

            attention_steps(dve, step)


def expert_phase(nc, x1_dram, gates_dram, gate_W, gate_b, expert_W, expert_b, out_tokens, mod, ident, bank):
    EW = EXPERTS * D
    EB = 512 // D
    BLOCKS = 2 * EXPERTS // EB
    EB_ROWS = 2 * LO + EXPERTS
    BLOCK_ADDS = 2 * EB
    with ExitStack() as ctx:
        def sb(name, shape, dt=F32):
            return ctx.enter_context(nc.sbuf_tensor(name, shape, dt))

        def sem(name):
            return ctx.enter_context(nc.semaphore(name))

        ew_hi, ew_lo = (sb("ew_" + h, [128, KT, EXPERTS, D], F32R) for h in ("hi", "lo"))
        ew_raw = sb("ew_raw", [128, KT, EXPERTS, D])
        eb_raw = sb("eb_raw", [EB_ROWS, D])
        eb = sb("eb", [EB_ROWS, D], F32R)
        gw = sb("gw", [128, KT, EXPERTS])
        gbias = sb("gbias", [128, EXPERTS])
        gb = sb("gb", [128, BATCH, D])
        rank = sb("rank", [128, EXPERTS])
        half_neg2 = sb("half_neg2", [128, NCH])

        x1 = [sb(f"x1_{i}", [128, NCH, D]) for i in range(GPB)]
        xn = sb("xn2", [128, NCH, D])
        stats = sb("stats2", [128, NCH, 6])
        mean_var = sb("mean_var2", [128, NCH, 2])
        var_eps = sb("var_eps2", [128, NCH])
        rstd = sb("rstd2", [128, NCH])
        h32 = sb("h32_2", [128, KT, GT])
        h_hi = [sb(f"h2_hi{i}", [128, KT, GT], F32R) for i in range(2)]
        h_lo = [sb(f"h2_lo{i}", [128, KT, GT], F32R) for i in range(2)]
        sc, p, first, second, tmp = (sb(n, [128, NCH, EXPERTS]) for n in ("sc", "prob", "first", "second", "tmp"))
        red = sb("red", [128, 8, NCH])
        comb = [sb(f"comb{i}", [128, NCH, EXPERTS]) for i in range(2)]
        comb_cols = sb("comb_cols", [128, NCH, EB_ROWS], F32R)
        combT = sb("combT", [EB_ROWS, GT], F32R)
        acc = [sb(f"acc{i}", [128, NCH, D]) for i in range(2)]

        Y = bank[0:4]
        HT, GATE, BIAS = bank[4], bank[5], bank[6:8]

        loaded = sem("e_loaded"); eb_loaded = sem("eb_loaded")
        ew_loaded = [sem(f"ew_loaded{i}") for i in range(EXPERTS // EB)]; gb_loaded = sem("gb_loaded")
        hi_split = sem("e_hi_split"); lo_split = sem("e_lo_split")
        fills = sem("e_fills")
        x1_loaded = [sem(f"x1_loaded{i}") for i in range(GPB)]
        out_stored = [sem(f"out_stored{i}") for i in range(GPB)]
        ln_step = sem("ln2_step"); var_ready = sem("var2_ready"); rstd_ready = sem("rstd2_ready")
        xn_ready = sem("xn2_ready")
        hT_ps = sem("h2T_ps"); h32_ready = sem("h2_32_ready"); h_hi_ready = sem("h2_hi_ready")
        h_lo_ready = sem("h2_lo_ready")
        stats_seen = sem("stats2_seen"); sums_seen = sem("sums_seen")
        gate_ps = sem("gate_ps"); route_step = sem("route_step"); route_exp_in = sem("route_exp_in")
        route_exp = sem("route_exp"); total_ready = sem("total_ready")
        comb_ready = sem("comb_ready"); combT_ps = sem("combT_ps"); combT_ready = sem("combT_ready")
        comb_hi = sem("comb_hi"); comb_zero = sem("comb_zero"); comb_split = sem("comb_split")
        bias_ps = sem("bias_ps"); acc_ready = sem("acc_ready"); eb_hi = sem("eb_hi"); eb_ready = sem("eb_ready")
        y_ps = sem("y_ps"); y_added = sem("y_added"); scaled = sem("scaled"); result_ready = sem("result_ready")

        ROUTE = 20
        ROUTE_BLOCK = 3
        ADDS = BLOCKS * BLOCK_ADDS

        def piece(t, q):
            return t[:, :, EB * q:EB * (q + 1), :].rearrange("p k e d -> p k (e d)")

        block = ctx.enter_context(nc.Block())

        @block.sync
        def _(sp):
            def load(T, s):
                after(sp, out_stored[s], (T - s) * (16 // GPB))
                sp.dma_start(x1[s][:, :, :], x1_dram[bass.ds(T, 1)].rearrange("g p c d -> (g p) c d"))\
                  .then_inc(x1_loaded[s], 16)

            load(0, 0)
            sp.dma_start(gw[:, :, :], gate_W.rearrange("(k p) e -> p k e", p=128)).then_inc(loaded, 16)
            sp.dma_start(gbias[:, :], gate_b.partition_broadcast(128)).then_inc(loaded, 16)
            for e in range(EXPERTS):
                sp.dma_start(ew_raw[:, :, e, :], expert_W[e].rearrange("(k p) f -> p k f", p=128))\
                  .then_inc(ew_loaded[e // EB], 16)
            sp.wait_ge(fills, 2 + EXPERTS)
            for at in (0, LO, 2 * LO):
                sp.dma_start(eb_raw[at:at + EXPERTS, :], expert_b).then_inc(eb_loaded, 16)
            load(1, 1)
            sp.dma_start(gb[:, :, :], gates_dram[1].partition_broadcast(128)).then_inc(gb_loaded, 16)

            def store(T, s):
                sp.wait_ge(result_ready, T * 2 + 2)
                sp.dma_start(out_tokens[bass.ds(T, 1)].rearrange("g p c d -> (g p) c d"), x1[s][:, :, :])\
                  .then_inc(out_stored[s], 16)

            def group(T, s):
                if exists(T - 1):
                    store(T - 1, (s - 1) % GPB)
                if exists(T + 3) and not (isinstance(T, int) and T + 3 < 2):
                    load(T + 3, (s + 3) % GPB)

            expert_groups(sp, group)
            store(NG - 1, (NG - 1) % GPB)
            for s in range(GPB):
                sp.wait_ge(out_stored[s], 16 * NG // GPB)

        @block.gpsimd
        def _(pool):
            pool.memset(eb_raw[:, :], 0.0).then_inc(fills, 1)
            pool.memset(half_neg2[:, :], -0.5).then_inc(fills, 1)
            for e in range(EXPERTS):
                pool.memset(rank[:, e:e + 1], float(EXPERTS - e)).then_inc(fills, 1)
            pool.wait_ge(fills, 2 + EXPERTS)

            def result(T, s, pair):
                b = batch_row(T)
                if isinstance(T, int) and T == 0:
                    pool.wait_ge(gb_loaded, 16)
                pool.wait_ge(y_added, T * ADDS + (pair + 1) * (ADDS // 2))
                pool.sem_inc(sums_seen)
                a = acc[s % 2][:, 2 * pair:2 * pair + 2, :]
                rows = x1[s][:, 2 * pair:2 * pair + 2, :]
                pool.tensor_tensor(a, a, gb[:, bass.ds(b, 1), :].to_broadcast([128, 2, D]), ALU.mult).then_inc(scaled, 1)
                pool.wait_ge(scaled, T * 2 + pair + 1)
                pool.tensor_tensor(rows, rows, a, ALU.add).then_inc(result_ready, 1)

            def group(T, s):
                if exists(T):
                    result(T, s, 0)
                if exists(T + 2):
                    pool.wait_ge(var_ready, T + 3)
                    pool.tensor_tensor(rstd[:, :], var_eps[:, :], half_neg2[:, :], ALU.pow).then_inc(rstd_ready, 1)
                if exists(T):
                    result(T, s, 1)

            expert_groups(pool, group)

        @block.scalar
        def _(act):
            def group(T, s):
                if exists(T):
                    for j in range(2):
                        act.wait_ge(bias_ps, T * 2 + j + 1)
                        after(act, result_ready, (T - 2) * 2 + j + 1)
                        act.activation(acc[s % 2][:, 2 * j:2 * j + 2, :], BIAS[j][:, :].rearrange("p (c d) -> p c d", d=D),
                                       ACT.Copy).then_inc(acc_ready, 1)
                if not exists(T + 1):
                    return
                Tn, sn = T + 1, (s + 1) % 2
                b = batch_row(Tn)
                after(act, h_lo_ready, Tn * 2)
                after(act, gate_ps, Tn)
                for kt in range(KT):
                    act.wait_ge(hT_ps, Tn * 2 + kt + 1)
                    act.activation(h32[:, kt, :], HT[:, :], ACT.Identity, bias=mod[:, 2, kt, bass.ds(b, 1)],
                                   scale=mod[:, 3, kt, bass.ds(b, 1)]).then_inc(h32_ready, 1)
                    act.wait_ge(h32_ready, Tn * 2 + kt + 1)
                    act.activation(h_hi[sn][:, kt, :], h32[:, kt, :], ACT.Copy).then_inc(h_hi_ready, 1)
                if leads(T):
                    for q in range(EXPERTS // EB):
                        act.wait_ge(ew_loaded[q], 16 * EB)
                        act.activation(piece(ew_hi, q), piece(ew_raw, q), ACT.Copy).then_inc(hi_split, 1)
                act.wait_ge(route_exp_in, Tn + 1)
                act.activation(p[:, :, :], sc[:, :, :], ACT.Exp).then_inc(route_exp, 1)
                if leads(T):
                    act.wait_ge(eb_loaded, 16 * 3)
                    act.activation(eb[:, :], eb_raw[:, :], ACT.Copy).then_inc(eb_hi, 1)
                act.wait_ge(combT_ps, Tn + 1)
                after(act, bias_ps, Tn * 2)
                act.activation(combT[:, :], GATE[0:EB_ROWS, :], ACT.Copy).then_inc(combT_ready, 1)

            expert_groups(act, group)

        @block.tensor
        def _(pe):

            def y_block(T, s, j):
                pair, q = j // (BLOCKS // 2), j % (BLOCKS // 2)
                h, l = h_hi[s % 2], h_lo[s % 2]
                ex = slice(EB * q, EB * (q + 1))
                if isinstance(T, int) and T == 0 and pair == 0:
                    pe.wait_ge(lo_split, q + 1)
                for i in range(2):
                    y = Y[2 * (j % 2) + i]
                    tok = slice((2 * pair + i) * CH, (2 * pair + i + 1) * CH)
                    after(pe, y_added, T * ADDS + (j - 1) * BLOCK_ADDS - 1 + i)
                    for kt in range(KT):
                        pe.matmul(y[:, :], h[:, kt, tok], ew_hi[:, kt, ex, :], start=(kt == 0), stop=False)
                        pe.matmul(y[:, :], h[:, kt, tok], ew_lo[:, kt, ex, :], start=False, stop=False)
                        mm = pe.matmul(y[:, :], l[:, kt, tok], ew_hi[:, kt, ex, :], start=False, stop=(kt == KT - 1))
                    mm.then_inc(y_ps, 1)

            def transpose_h(Tn, kt):
                pe.wait_ge(xn_ready, Tn + 1)
                after(pe, h32_ready, Tn * 2 + kt)
                for ch in range(NCH):
                    mm = pe.transpose(HT[:, ch * CH:(ch + 1) * CH], xn[:, ch, kt * 128:(kt + 1) * 128], ident[:, :])
                mm.then_inc(hT_ps, 1)

            def gate(Tn):
                pe.wait_ge(h32_ready, Tn * 2 + 2)
                if isinstance(Tn, int) and Tn == 0:
                    pe.wait_ge(loaded, 16 * 2)
                after(pe, combT_ready, Tn)
                for ch in range(NCH):
                    for kt in range(KT):
                        for at in range(0, CH, SLICE):
                            mm = pe.matmul(GATE[at:at + SLICE, ch * EXPERTS:(ch + 1) * EXPERTS],
                                           h32[:, kt, ch * CH + at:ch * CH + at + SLICE], gw[:, kt, :],
                                           start=(kt == 0), stop=(kt == KT - 1))
                mm.then_inc(gate_ps, 1)

            def transpose_comb(Tn):
                pe.wait_ge(comb_split, Tn * 2 + 2)
                for ch in range(NCH):
                    mm = pe.transpose(GATE[0:EB_ROWS, ch * CH:(ch + 1) * CH], comb_cols[:, ch, :].bitcast(F32), ident[:, :])
                mm.then_inc(combT_ps, 1)

            def biases(T):
                pe.wait_ge(combT_ready, T + 1)
                if isinstance(T, int) and T == 0:
                    pe.wait_ge(eb_ready, 1)
                after(pe, acc_ready, T * 2)
                for j in range(2):
                    for i in range(2):
                        ch = 2 * j + i
                        mm = pe.matmul(BIAS[j][:, i * D:(i + 1) * D], combT[:, ch * CH:(ch + 1) * CH], eb[:, :],
                                       start=True, stop=True)
                    mm.then_inc(bias_ps, 1)

            def group(T, s):
                for j in range(BLOCKS):
                    if exists(T):
                        if j == 0:
                            pe.wait_ge(h_lo_ready, T * 2 + 2)
                        y_block(T, s, j)
                    if j == 0 and exists(T):
                        if isinstance(T, int) and T == 0:
                            transpose_comb(T)
                        biases(T)
                    if j < KT and exists(T + 1):
                        transpose_h(T + 1, j)
                    if j == KT and exists(T + 1):
                        gate(T + 1)
                if exists(T + 1) and not leads(T):
                    transpose_comb(T + 1)

            expert_groups(pe, group)

        @block.vector
        def _(dve):
            dve.wait_ge(fills, 2 + EXPERTS)
            dve.wait_ge(loaded, 16 * 2)

            dve.memset(comb_cols[:, :, :].bitcast(F32), 0.0).then_inc(comb_zero, 1)

            def split_low(q):
                dve.wait_ge(hi_split, q + 1)
                dve.tensor_tensor(piece(ew_lo, q), piece(ew_raw, q), piece(ew_hi, q).bitcast(F32), ALU.subtract)\
                   .then_inc(lo_split, 1)

            def add(T, s, m):
                j, k = m // BLOCK_ADDS, m % BLOCK_ADDS
                pair, q = j // (BLOCKS // 2), j % (BLOCKS // 2)
                i, e = k % 2, EB * q + k // 2
                if k < 2:
                    dve.wait_ge(y_ps, T * BLOCKS * 2 + 2 * j + i + 1)
                a = acc[s % 2][:, 2 * pair + i, :]
                if e == 0:
                    dve.wait_ge(acc_ready, T * 2 + pair + 1)
                else:
                    dve.wait_ge(y_added, T * ADDS + m - 1)
                y = Y[2 * (j % 2) + i]
                dve.scalar_tensor_tensor(a, y[:, (k // 2) * D:(k // 2 + 1) * D], comb[s % 2][:, 2 * pair + i, e:e + 1], a,
                                         ALU.mult, ALU.add).then_inc(y_added, 1)

            def ln_stats(Tn, xs, ch):
                if ch == 0:
                    dve.wait_ge(x1_loaded[xs], (Tn - xs) * (16 // GPB) + 16)
                dve.bn_stats(stats[:, ch, :], x1[xs][:, ch, :]).then_inc(ln_step, 1)

            def ln_variance(Tn):
                after(dve, xn_ready, Tn)
                dve.wait_ge(ln_step, Tn * 8 + NCH)
                dve.sem_inc(stats_seen)
                for ch in range(NCH):
                    dve.bn_aggr(mean_var[:, ch, :], stats[:, ch, :]).then_inc(ln_step, 1)
                dve.wait_ge(ln_step, Tn * 8 + 8)
                dve.tensor_scalar(var_eps[:, :].unsqueeze(2), mean_var[:, :, 1:2], LN_EPS, None, ALU.add)\
                   .then_inc(var_ready, 1)

            def ln_apply(Tn, xs):
                dve.wait_ge(rstd_ready, Tn + 1)
                after(dve, hT_ps, Tn * 2)
                for ch in range(NCH):
                    ins = dve.tensor_scalar(xn[:, ch, :], x1[xs][:, ch, :], mean_var[:, ch, 0:1], rstd[:, ch:ch + 1],
                                            ALU.subtract, ALU.mult)
                ins.then_inc(xn_ready, 1)

            def h_low(Tn, sn):
                for kt in range(KT):
                    dve.wait_ge(h_hi_ready, Tn * 2 + kt + 1)
                    dve.tensor_tensor(h_lo[sn][:, kt, :], h32[:, kt, :], h_hi[sn][:, kt, :].bitcast(F32), ALU.subtract)\
                       .then_inc(h_lo_ready, 1)

            def route(Tn, sn, between):
                count = [0]

                def counted(ins):
                    count[0] += 1
                    ins.then_inc(route_step, 1)
                    between(count[0])
                    dve.wait_ge(route_step, Tn * ROUTE + count[0])

                def per_expert(t):
                    return t.unsqueeze(2).to_broadcast([128, NCH, EXPERTS])

                rank_all = rank[:, :].unsqueeze(1).to_broadcast([128, NCH, EXPERTS])
                s_, p_, f1, f2, t_ = (t[:, :, :] for t in (sc, p, first, second, tmp))
                dve.wait_ge(gate_ps, Tn + 1)
                counted(dve.tensor_tensor(s_, GATE[:, 0:NCH * EXPERTS].rearrange("p (c e) -> p c e", e=EXPERTS),
                                          gbias[:, :].unsqueeze(1).to_broadcast([128, NCH, EXPERTS]), ALU.add))
                counted(dve.tensor_scalar(s_, s_, SCORE_EPS, None, ALU.max))
                counted(dve.tensor_reduce(red[:, 0, :], s_, AX_X, ALU.max))
                dve.tensor_tensor(s_, s_, per_expert(red[:, 0, :]), ALU.subtract).then_inc(route_exp_in, 1)
                dve.wait_ge(route_exp, Tn + 1)
                counted(dve.tensor_reduce(red[:, 1, :], p_, AX_X, ALU.add))
                counted(dve.reciprocal(red[:, 2, :], red[:, 1, :]))
                counted(dve.tensor_tensor(p_, p_, per_expert(red[:, 2, :]), ALU.mult))
                counted(dve.tensor_reduce(red[:, 3, :], p_, AX_X, ALU.max))
                counted(dve.tensor_tensor(f1, p_, per_expert(red[:, 3, :]), ALU.is_equal))
                counted(dve.tensor_tensor(f1, f1, rank_all, ALU.mult))
                counted(dve.tensor_reduce(red[:, 4, :], f1, AX_X, ALU.max))
                counted(dve.tensor_tensor(f1, f1, per_expert(red[:, 4, :]), ALU.is_equal))
                counted(dve.scalar_tensor_tensor(t_, f1, -2.0, p_, ALU.mult, ALU.add))
                counted(dve.tensor_reduce(red[:, 5, :], t_, AX_X, ALU.max))
                counted(dve.tensor_tensor(f2, t_, per_expert(red[:, 5, :]), ALU.is_equal))
                counted(dve.tensor_tensor(f2, f2, rank_all, ALU.mult))
                counted(dve.tensor_reduce(red[:, 6, :], f2, AX_X, ALU.max))
                counted(dve.tensor_tensor(f2, f2, per_expert(red[:, 6, :]), ALU.is_equal))
                counted(dve.tensor_tensor(f1, f1, f2, ALU.add))
                counted(dve.scalar_tensor_tensor(t_, p_, W_THRES, f1, ALU.max, ALU.mult))
                counted(dve.tensor_reduce(red[:, 7, :], t_, AX_X, ALU.add))
                assert count[0] == ROUTE
                dve.reciprocal(red[:, 0, :], red[:, 7, :]).then_inc(total_ready, 1)
                dve.wait_ge(total_ready, Tn + 1)
                dve.scalar_tensor_tensor(comb[sn][:, :, :], t_, 1.0 / TOP_K, per_expert(red[:, 0, :]), ALU.mult, ALU.mult)\
                   .then_inc(comb_ready, 1)
                cols = [comb_cols[:, :, at:at + EXPERTS] for at in (0, LO, 2 * LO)]
                dve.wait_ge(comb_zero, 1)
                after(dve, combT_ps, Tn)
                dve.wait_ge(comb_ready, Tn + 1)
                dve.tensor_copy(cols[0], comb[sn][:, :, :]).then_inc(comb_hi, 1)
                dve.tensor_copy(cols[2], comb[sn][:, :, :]).then_inc(comb_split, 1)
                dve.wait_ge(comb_hi, Tn + 1)
                dve.tensor_tensor(cols[1], comb[sn][:, :, :], cols[0].bitcast(F32), ALU.subtract).then_inc(comb_split, 1)

            def group(T, s):
                def adds(m0, m1):
                    if exists(T):
                        for m in range(m0, m1):
                            add(T, s, m)

                if exists(T + 1):
                    ln_apply(T + 1, (s + 1) % GPB)
                adds(0, 2 * BLOCK_ADDS)
                if exists(T + 1):
                    h_low(T + 1, (s + 1) % 2)
                adds(2 * BLOCK_ADDS, ROUTE_BLOCK * BLOCK_ADDS)
                first = ROUTE_BLOCK * BLOCK_ADDS

                def between(k):
                    if k <= 2 * NCH and k % 2:
                        if exists(T + 2):
                            ln_stats(T + 2, (s + 2) % GPB, k // 2)
                    elif leads(T):
                        if k <= 2 * (EXPERTS // EB):
                            split_low(k // 2 - 1)
                    elif exists(T):
                        add(T, s, first + (k // 2 - 1 if k <= 2 * NCH else k - NCH - 1))

                if exists(T + 1):
                    route(T + 1, (s + 1) % 2, between)
                    adds(first + ROUTE - NCH, ADDS - BLOCK_ADDS)
                else:
                    adds(first, ADDS - BLOCK_ADDS)
                    if exists(T + 2):
                        for ch in range(NCH):
                            ln_stats(T + 2, (s + 2) % GPB, ch)
                if exists(T + 2):
                    ln_variance(T + 2)
                adds(ADDS - BLOCK_ADDS, ADDS)
                if leads(T):
                    lo_rows = slice(2 * LO, EB_ROWS)
                    dve.wait_ge(eb_hi, 1)
                    dve.tensor_tensor(eb[lo_rows, :], eb_raw[lo_rows, :], eb[lo_rows, :].bitcast(F32), ALU.subtract)\
                       .then_inc(eb_ready, 1)

            expert_groups(dve, group)


_INS = ["L0_attn_x", "L0_attn_Wq", "L0_attn_Wk", "L0_attn_Wv", "L0_attn_Wo", "L0_attn_Wa", "L0_attn_ba",
        "L0_ffn_gate_W", "L0_ffn_gate_b", "L0_ffn_expert_W", "L0_ffn_expert_b", "L0_c", "L0_wmod"]
_OUTS = [((BATCH, SEQ, D), "float32")]


def kernel(**inputs):
    import numpy as _np
    import concourse.bacc as _bacc
    from concourse import mybir as _mybir
    from concourse.bass_utils import run_bass_kernel_spmd as _run

    nc = _bacc.Bacc("TRN2", target_bir_lowering=False, num_devices=1)
    arrays, args = {}, []
    for name in _INS:
        a = _np.ascontiguousarray(inputs[name])
        arrays[f"in_{name}_dram"] = a
        args.append(nc.dram_tensor(f"in_{name}_dram", a.shape, _mybir.dt.from_np(a.dtype), kind="ExternalInput").ap())
    for i, (shape, dtype) in enumerate(_OUTS):
        dt = _mybir.dt.from_np(_np.dtype(dtype))
        args.append(nc.dram_tensor(f"out_{i}_dram", shape, dt, kind="ExternalOutput").ap())
    adaln_block(nc, *args)
    r = _run(nc, [arrays], core_ids=[0])
    got = tuple(r.results[0][f"out_{i}_dram"] for i in range(len(_OUTS)))
    return got[0]
```
